# Optimizing a Trainium2 kernel written in Bass

```python
import numpy as np
import jax
import jax.numpy as jnp

def _softmax(x, axis=-1):
    return jax.nn.softmax(x, axis=axis)

def _gelu(x):
    return jax.nn.gelu(x, approximate=True)

def _silu(x):
    return jax.nn.silu(x)

def _sigmoid(x):
    return jax.nn.sigmoid(x)

def _layernorm(x, axis=-1, eps=1e-05):
    m = jnp.mean(x, axis=axis, keepdims=True)
    v = jnp.var(x, axis=axis, keepdims=True)
    return (x - m) / jnp.sqrt(v + eps)

def _scatter_add(tgt, idx, src, axis=0):
    return tgt.at[idx].add(src)

def _segment_sum(src, seg, n):
    return jax.ops.segment_sum(src, seg, n)
kernel_name = 'mk_decoder_postln_d1_seqx_r4_3fc7e9'

def setup_inputs(seed: int=0):
    np.random.seed(seed)
    _w = jnp.asarray

    def _rec_inputs():
        import jax
        import jax.numpy as jnp
        _rk = jax.random.key(seed)
        x = -0.0002928 + 1 * jax.random.normal(jax.random.fold_in(_rk, 1), (2, 1024, 256), jnp.float32)
        _lenS = 1024 - jax.random.randint(jax.random.fold_in(_rk, 7), (2,), 0, max(1, 1024 // 4) + 1, jnp.int32)
        _lenS2 = 77 - jax.random.randint(jax.random.fold_in(_rk, 8), (2,), 0, max(1, 77 // 4) + 1, jnp.int32)
        _ctx_1024P = jax.random.normal(jax.random.fold_in(_rk, 11), (2, 16, 256), jnp.float32)
        _ctx_1024c = jax.random.dirichlet(jax.random.fold_in(_rk, 511), 0.3 * jnp.ones((16,), jnp.float32), (2, 77))
        _ctx_1024t = jnp.einsum('bsk,bkd->bsd', _ctx_1024c, _ctx_1024P)
        _ctx_1024t = _ctx_1024t * jax.lax.rsqrt(jnp.mean(jnp.square(_ctx_1024t)) + 1e-12) * 0.953939
        ctx_1024 = -1.39393e-06 + 0.999914 * (_ctx_1024t + 0.3 * jax.random.normal(jax.random.fold_in(_rk, 611), (2, 77, 256), jnp.float32))
        _validS = jnp.arange(1024)[None, :] < _lenS[:, None]
        _validS2 = jnp.arange(77)[None, :] < _lenS2[:, None]
        _causal = jnp.tril(jnp.ones((1024, 1024), dtype=bool))
        mask_BxS2_bf1 = jnp.ones((2, 77), dtype=bool)
        return (x, ctx_1024, mask_BxS2_bf1)
    x, ctx_1024, mask_BxS2_bf1 = _rec_inputs()

    def _L0_attn_setup():
        import jax, jax.numpy as jnp
        import numpy as np
        import math
        TALA_CYCLES = [5, 6, 7, 8]
        N_HEADS = 16
        key = jax.random.key(seed)
        k1, k2, k3, k4 = jax.random.split(key, 4)
        B, T, D = (2, 512, 256)
        x = jax.random.normal(k1, (B, T, D), dtype=jnp.float32)
        w_qkv = jax.random.normal(k2, (D, 3 * D), dtype=jnp.float32) * (1.0 / math.sqrt(D))
        w_out = jax.random.normal(k3, (D, D), dtype=jnp.float32) * (1.0 / math.sqrt(D))
        bandha_gate = jax.random.normal(k4, (N_HEADS, max(TALA_CYCLES)), dtype=jnp.float32)
        return {'x': x, 'w_qkv': w_qkv, 'w_out': w_out, 'bandha_gate': bandha_gate}
    _L0_attn_all = _L0_attn_setup()
    _L0_attn_in = {k: v for k, v in _L0_attn_all.items() if k in ('w_qkv', 'w_out', 'bandha_gate')}
    del _L0_attn_all

    def _L0_xattn_setup():
        import jax, jax.numpy as jnp
        import numpy as np
        N_HEADS = 16
        D_MODEL = 256
        HEAD_DIM = D_MODEL // N_HEADS
        MASK_FILL = -100000000.0

        def _split_heads(x):
            B, S, _ = x.shape
            return x.reshape(B, S, N_HEADS, HEAD_DIM).transpose(0, 2, 1, 3)
        key = jax.random.key(seed)
        ks = jax.random.split(key, 12)
        B, L, P = (2, 512, 512)
        s = 1.0 / np.sqrt(D_MODEL).astype(np.float32)
        inp = {'q': jax.random.normal(ks[0], (B, L, D_MODEL), dtype=jnp.float32), 'k': jax.random.normal(ks[1], (B, P, D_MODEL), dtype=jnp.float32), 'v': jax.random.normal(ks[2], (B, P, D_MODEL), dtype=jnp.float32), 'attention_mask': jnp.ones((B, P), dtype=bool), 'Wq': jax.random.normal(ks[3], (D_MODEL, D_MODEL), dtype=jnp.float32) * s, 'bq': jnp.zeros((D_MODEL,), dtype=jnp.float32), 'Wk': jax.random.normal(ks[4], (D_MODEL, D_MODEL), dtype=jnp.float32) * s, 'bk': jnp.zeros((D_MODEL,), dtype=jnp.float32), 'Wv': jax.random.normal(ks[5], (D_MODEL, D_MODEL), dtype=jnp.float32) * s, 'bv': jnp.zeros((D_MODEL,), dtype=jnp.float32), 'Wo': jax.random.normal(ks[6], (D_MODEL, D_MODEL), dtype=jnp.float32) * s, 'bo': jnp.zeros((D_MODEL,), dtype=jnp.float32)}
        return inp
    _L0_xattn_all = _L0_xattn_setup()
    _L0_xattn_in = {k: v for k, v in _L0_xattn_all.items() if k in ('Wq', 'bq', 'Wk', 'bk', 'Wv', 'bv', 'Wo', 'bo')}
    del _L0_xattn_all

    def _L0_ffn_setup():
        import jax, jax.numpy as jnp
        import numpy as np
        B, S, D = (4, 1024, 256)
        H = 1024
        RH = 256
        E = 16
        K = 2
        NS = 1

        def _swiglu(x, w1, w2, w3):
            return jax.nn.silu(x @ w1) * (x @ w2) @ w3
        key = jax.random.key(seed)
        ks = jax.random.split(key, 9)
        s = 0.02
        return {'x': jax.random.normal(ks[0], (B, S, D), dtype=jnp.float32), 'router_w': jax.random.normal(ks[1], (D, E), dtype=jnp.float32) * s, 'expert_bias': jnp.zeros((E,), dtype=jnp.float32), 'shared_w1': jax.random.normal(ks[2], (NS, D, H), dtype=jnp.float32) * s, 'shared_w2': jax.random.normal(ks[3], (NS, D, H), dtype=jnp.float32) * s, 'shared_w3': jax.random.normal(ks[4], (NS, H, D), dtype=jnp.float32) * s, 'routed_w1': jax.random.normal(ks[5], (E, D, RH), dtype=jnp.float32) * s, 'routed_w2': jax.random.normal(ks[6], (E, D, RH), dtype=jnp.float32) * s, 'routed_w3': jax.random.normal(ks[7], (E, RH, D), dtype=jnp.float32) * s}
    _L0_ffn_all = _L0_ffn_setup()
    _L0_ffn_in = {k: v for k, v in _L0_ffn_all.items() if k in ('router_w', 'expert_bias', 'shared_w1', 'shared_w2', 'shared_w3', 'routed_w1', 'routed_w2', 'routed_w3')}
    del _L0_ffn_all
    return {'x': x, 'ctx_1024': ctx_1024, 'mask_BxS2_bf1': mask_BxS2_bf1, 'L0_attn_w_qkv': _L0_attn_in['w_qkv'], 'L0_attn_w_out': _L0_attn_in['w_out'], 'L0_attn_bandha_gate': _L0_attn_in['bandha_gate'], 'L0_xattn_Wq': _L0_xattn_in['Wq'], 'L0_xattn_bq': _L0_xattn_in['bq'], 'L0_xattn_Wk': _L0_xattn_in['Wk'], 'L0_xattn_bk': _L0_xattn_in['bk'], 'L0_xattn_Wv': _L0_xattn_in['Wv'], 'L0_xattn_bv': _L0_xattn_in['bv'], 'L0_xattn_Wo': _L0_xattn_in['Wo'], 'L0_xattn_bo': _L0_xattn_in['bo'], 'L0_ffn_router_w': _L0_ffn_in['router_w'], 'L0_ffn_expert_bias': _L0_ffn_in['expert_bias'], 'L0_ffn_shared_w1': _L0_ffn_in['shared_w1'], 'L0_ffn_shared_w2': _L0_ffn_in['shared_w2'], 'L0_ffn_shared_w3': _L0_ffn_in['shared_w3'], 'L0_ffn_routed_w1': _L0_ffn_in['routed_w1'], 'L0_ffn_routed_w2': _L0_ffn_in['routed_w2'], 'L0_ffn_routed_w3': _L0_ffn_in['routed_w3']}

def reference(x, ctx_1024, mask_BxS2_bf1, L0_attn_w_qkv, L0_attn_w_out, L0_attn_bandha_gate, L0_xattn_Wq, L0_xattn_bq, L0_xattn_Wk, L0_xattn_bk, L0_xattn_Wv, L0_xattn_bv, L0_xattn_Wo, L0_xattn_bo, L0_ffn_router_w, L0_ffn_expert_bias, L0_ffn_shared_w1, L0_ffn_shared_w2, L0_ffn_shared_w3, L0_ffn_routed_w1, L0_ffn_routed_w2, L0_ffn_routed_w3):
    import jax
    import jax.numpy as jnp

    def _L0_attn_ref(x, w_qkv, w_out, bandha_gate):
        import jax, jax.numpy as jnp
        import numpy as np
        import math
        TALA_CYCLES = [5, 6, 7, 8]
        N_HEADS = 16
        B, T, D = x.shape
        H = N_HEADS
        hd = D // H
        scale = math.sqrt(hd)
        qkv = x @ w_qkv
        q, k, v = jnp.split(qkv, 3, axis=-1)
        to_heads = lambda t: t.reshape(B, T, H, hd).transpose(0, 2, 1, 3)
        q, k, v = (to_heads(q), to_heads(k), to_heads(v))
        cycles = np.array([TALA_CYCLES[i % len(TALA_CYCLES)] for i in range(H)])
        phases = np.arange(T)[None, :] % cycles[:, None]
        gate = jax.nn.sigmoid(jnp.take_along_axis(bandha_gate, jnp.asarray(phases), axis=1))
        q = q * gate[None, :, :, None]
        scores = jnp.einsum('bhqd,bhkd->bhqk', q, k) / scale
        causal = np.tril(np.ones((T, T), dtype=bool))
        scores = jnp.where(jnp.asarray(causal), scores, -jnp.inf)
        attn = jax.nn.softmax(scores, axis=-1)
        out = jnp.einsum('bhqk,bhkd->bhqd', attn, v)
        out = out.transpose(0, 2, 1, 3).reshape(B, T, D)
        return out @ w_out

    def _L0_xattn_ref(q, k, v, attention_mask, Wq, bq, Wk, bk, Wv, bv, Wo, bo):
        import jax, jax.numpy as jnp
        import numpy as np
        N_HEADS = 16
        D_MODEL = 256
        HEAD_DIM = D_MODEL // N_HEADS
        MASK_FILL = -100000000.0

        def _split_heads(x):
            B, S, _ = x.shape
            return x.reshape(B, S, N_HEADS, HEAD_DIM).transpose(0, 2, 1, 3)
        qm = _split_heads(q @ Wq.T + bq)
        km = _split_heads(k @ Wk.T + bk)
        vm = _split_heads(v @ Wv.T + bv)
        scores = jnp.einsum('bnlh,bnph->bnlp', qm, km) / np.sqrt(HEAD_DIM).astype(np.float32)
        mask = attention_mask[:, None, None, :]
        scores = jnp.where(mask, scores, MASK_FILL)
        attn = jax.nn.softmax(scores, axis=-1)
        out = jnp.einsum('bnlp,bnph->bnlh', attn, vm)
        B, _, L, _ = out.shape
        out = out.transpose(0, 2, 1, 3).reshape(B, L, D_MODEL)
        return out @ Wo.T + bo

    def _L0_ffn_ref(x, router_w, expert_bias, shared_w1, shared_w2, shared_w3, routed_w1, routed_w2, routed_w3):
        import jax, jax.numpy as jnp
        import numpy as np
        B, S, D = (4, 1024, 256)
        H = 1024
        RH = 256
        E = 16
        K = 2
        NS = 1

        def _swiglu(x, w1, w2, w3):
            return jax.nn.silu(x @ w1) * (x @ w2) @ w3
        shared_out = jnp.sum(jax.vmap(lambda w1, w2, w3: _swiglu(x, w1, w2, w3))(shared_w1, shared_w2, shared_w3), axis=0)
        scores = jax.nn.sigmoid(x @ router_w)
        sel_scores = scores + expert_bias
        _, top_idx = jax.lax.top_k(sel_scores, K)
        top_scores = jnp.take_along_axis(scores, top_idx, axis=-1)
        gates = jnp.sum(jax.nn.one_hot(top_idx, E, dtype=scores.dtype) * top_scores[..., None], axis=-2)
        xf = x.reshape(-1, D)
        gf = gates.reshape(-1, E).T

        def body(acc, ws):
            w1, w2, w3, g = ws
            return (acc + _swiglu(xf, w1, w2, w3) * g[:, None], None)
        routed_out, _ = jax.lax.scan(body, jnp.zeros_like(xf), (routed_w1, routed_w2, routed_w3, gf))
        return shared_out + routed_out.reshape(x.shape)
    x = _layernorm(x + _L0_attn_ref(x, L0_attn_w_qkv, L0_attn_w_out, L0_attn_bandha_gate), axis=-1)
    x = _layernorm(x + _L0_xattn_ref(x, ctx_1024, ctx_1024, mask_BxS2_bf1, L0_xattn_Wq, L0_xattn_bq, L0_xattn_Wk, L0_xattn_bk, L0_xattn_Wv, L0_xattn_bv, L0_xattn_Wo, L0_xattn_bo), axis=-1)
    x = _layernorm(x + _L0_ffn_ref(x, L0_ffn_router_w, L0_ffn_expert_bias, L0_ffn_shared_w1, L0_ffn_shared_w2, L0_ffn_shared_w3, L0_ffn_routed_w1, L0_ffn_routed_w2, L0_ffn_routed_w3), axis=-1)
    return x

_drawn_inputs = setup_inputs


def setup_inputs(seed=0):
    import zlib

    import numpy as np

    out = dict(_drawn_inputs(seed))
    spreads = {'L0_xattn_bq': (0.0, 0.346),
     'L0_xattn_bk': (0.0, 2.0),
     'L0_xattn_bv': (0.0, 0.1),
     'L0_xattn_bo': (0.0, 0.1),
     'L0_ffn_expert_bias': (0.0, 0.524)}
    factors = {'L0_attn_bandha_gate': 2.702,
     'L0_ffn_router_w': 5.334,
     'L0_ffn_routed_w1': 4.286,
     'L0_ffn_routed_w2': 4.314,
     'L0_ffn_routed_w3': 4.238,
     'L0_ffn_shared_w1': 2.784,
     'L0_ffn_shared_w2': 2.758,
     'L0_ffn_shared_w3': 2.779}
    for name, (base, spread) in spreads.items():
        noise = np.random.default_rng([zlib.crc32(name.encode()), seed]).standard_normal(out[name].shape)
        drawn = base * np.exp(spread * noise) if base else spread * noise
        out[name] = jnp.asarray(drawn.astype(out[name].dtype))
    for name, factor in factors.items():
        out[name] = (out[name] * factor).astype(out[name].dtype)
    return out
```

```python
from contextlib import ExitStack

import numpy as np

import concourse.bass as bass
from concourse import mybir

ALU = mybir.AluOpType
ACT = mybir.ActivationFunctionType
AX = mybir.AxisListType
F32 = mybir.dt.float32
BF16 = mybir.dt.bfloat16
I32 = mybir.dt.int32
U32 = mybir.dt.uint32
U16 = mybir.dt.uint16
U8 = mybir.dt.uint8

P = 128
B, S, D = 2, 1024, 256
TOK = B * S
HD = 16
SKV = 77
KD = D // P
CH = 512
NCH = TOK // CH
CPB = S // CH
GH = 4
NG = D // HD // GH
NN = B * NG
QT = S // P
TPC = CH // P
NT = TOK // P
FH = 1024
NE, RH, TOPK = 16, 256, 2
TILES = (TOPK * TOK + NE * (P - 1)) // P
EPS = 1e-5
SCALE = float(HD) ** -0.5
MASK_FILL = 1e8
LOWEST = -3e38
LATER_KEY = -1e30
RING = 3
ITEMS = 3
QUERY_PARTS = (0, 0, 0, 1, 1, 2)
KEY_PARTS = (0, 1, 2, 0, 1, 0)
STACK = len(QUERY_PARTS) * HD
SMALL = 16 * 13
TALA_CYCLES = (5, 6, 7, 8)


def row_groups(parts):
    runs, r = [], 0
    while r < len(parts):
        n = 1
        step = 0 if r + 1 < len(parts) and parts[r + 1] == parts[r] else 1
        while r + n < len(parts) and parts[r + n] == parts[r] + step * n:
            n += 1
        runs.append((r, r + n, parts[r], 1 if step == 0 else n, n if step == 0 else 1))
        r += n
    return runs


def bf16_bits(x):
    bits = int(np.float32(x).view(np.uint32))
    return (bits + 0x7FFF + ((bits >> 16) & 1)) >> 16


def bf16_round(x):
    return float(np.uint32(bf16_bits(x) << 16).view(np.float32))


def bf16_parts(x):
    out = []
    for _ in range(3):
        out.append(bf16_round(x))
        x -= out[-1]
    assert x == 0
    return out


FILL_PARTS = bf16_parts(MASK_FILL / SCALE)


class Attention:

    def __init__(self, causal):
        self.causal = causal
        self.keys = P if causal else SKV
        if causal:
            self.units = []
            for i in range(QT):
                for kc in range(i // TPC + 1):
                    w = min(CH, (i + 1) * P - CH * kc)
                    per = CH // w
                    self.units += [(i, kc, h0, per, w) for h0 in range(0, GH, per)]
            self.steps = [(c, j, max(0, j - TPC * c) * P) for c in range(CPB) for j in range(TPC * (c + 1))]
            self.unit_steps, self.top_step = 9, 10
            self.extra = 0
        else:
            self.units = [(i, 0, 0, GH, SKV) for i in range(QT)]
            self.steps = [(c, 0, 0) for c in range(CPB)]
            self.unit_steps, self.top_step = 2, 1
            self.extra = 3
        self.nu, self.ns = len(self.units), len(self.steps)
        self.last = [max(s for s, e in enumerate(self.steps) if e[0] == c) for c in range(CPB)]
        self.diagonal = [s for s, (c, j, _) in enumerate(self.steps) if causal and j >= TPC * c]
        self.top_row = STACK + self.extra
        self.max_rows, self.exp_rows = STACK + self.extra, STACK + self.extra + 3

    def units_of(self, s):
        if s >= self.unit_steps:
            return range(0)
        return range(self.nu * s // self.unit_steps, self.nu * (s + 1) // self.unit_steps)


SELF, CROSS = Attention(True), Attention(False)


def decoder_layer(nc, x, xT, ctxT, mask, w_qkv, gate_raw, gate_pick, phase, w_out, w_q, b_q, w_k, b_k, w_v, b_v,
                  w_o, b_o, router_w, expert_bias, sw1, sw2, sw3, rw1, rw2, rw3,
                  ident_f, ident_b, causal, before, out):
    q_parts_d = nc.dram_tensor("q_parts_d", [3, NN, GH * HD, S], BF16, kind="Internal").ap()
    k_parts_d = nc.dram_tensor("k_parts_d", [3, NN, GH * HD, S], BF16, kind="Internal").ap()
    xq_parts_d = nc.dram_tensor("xq_parts_d", [3, NN, GH * HD, S], BF16, kind="Internal").ap()
    xk_parts_d = nc.dram_tensor("xk_parts_d", [3, NN, GH * HD, SKV], BF16, kind="Internal").ap()
    o_self_d = nc.dram_tensor("o_self_d", [NN, P, S], F32, kind="Internal").ap()
    o_cross_d = nc.dram_tensor("o_cross_d", [NN, P, S], F32, kind="Internal").ap()
    slots_x_d = nc.dram_tensor("slots_x_d", [(TILES + 1) * P, D], F32, kind="Internal").ap()
    slots_y_d = nc.dram_tensor("slots_y_d", [TILES * P, D], F32, kind="Internal").ap()

    ctx = ExitStack()
    with ctx:
        def sb(name, shape, dt=F32):
            return ctx.enter_context(nc.sbuf_tensor(name, shape, dt))

        def sem(name):
            return ctx.enter_context(nc.semaphore(name))

        def sems(name, n):
            return [sem(f"{name}{i}") for i in range(n)]

        PS = ctx.enter_context(nc.psum_tensor("PS", [P, 8, CH], F32))

        feat_a = sb("feat_a", [P, KD, TOK])
        feat_b = sb("feat_b", [P, KD, TOK])
        rows = sb("rows", [P, NT, D])
        region_r = sb("region_r", [P, 24576])
        region_s = sb("region_s", [P, 6144])
        region_m = sb("region_m", [P, 6144])
        region_w = sb("region_w", [P, 2560])
        used = {}

        def carve(region, key, shape, dt=F32, parts=P):
            words = int(np.prod(shape)) * (2 if dt == BF16 else 4) // 4
            at = used.get(key, 0)
            used[key] = at + words
            assert at + words <= region.shape[1], (key, at + words)
            flat = region[0:parts, at:at + words]
            if dt != F32:
                flat = flat.bitcast(dt)
            names = "abcde"[:len(shape)]
            if len(shape) == 1:
                return flat
            return flat.rearrange(f"p ({' '.join(names)}) -> p {' '.join(names)}",
                                  **{n: s for n, s in zip(names[1:], shape[1:])})

        rows_flat = rows[:].rearrange("p t d -> p (t d)")
        wqkv_s = carve(rows_flat, "rows", [KD, 3 * D])
        gate_rows = carve(rows_flat, "rows", [2, D])
        phase_s = carve(rows_flat, "rows", [S])
        mask_b = carve(rows_flat, "rows", [B * SKV])
        xk_rest = carve(rows_flat, "rows", [KD, B * SKV])
        bv_b = carve(rows_flat, "rows", [D])
        q_st = carve(region_r, "r", [RING, GH, S], BF16)
        k_st = carve(region_r, "r", [RING, GH, S], BF16)
        v_st = carve(region_r, "r", [RING, QT, GH, 32])
        probs = carve(region_r, "r", [4, GH, CH])
        xk_parts = carve(region_r, "r", [3, KD * B * SKV], BF16)
        bo_b = carve(region_r, "r", [D])
        ntop_p = carve(region_r, "r", [3, P], BF16, parts=GH * QT)
        gate = carve(region_s, "s", [KD, S])
        o_blk = carve(region_s, "s", [CPB, CH])
        o_nrm = carve(region_s, "s", [CPB, CH])
        o_rec = carve(region_s, "s", [CPB, CH // 32])
        xk_all = carve(region_s, "s", [NN, GH * SKV], BF16)
        xv_all = carve(region_s, "s", [NN, GH * HD])
        fill_row = carve(region_s, "s", [3, B * SKV], BF16, parts=1)
        v_all = feat_b[:].rearrange("p k t -> p (k t)").rearrange("p (n t r) -> p n t r", n=NN, t=QT)
        whole = carve(region_m, "m", [ITEMS, CH])
        rest = carve(region_m, "m", [ITEMS, CH])
        parts = carve(region_m, "m", [ITEMS, 3, CH], BF16)
        ctxT_s = carve(region_m, "m", [KD, B * SKV])
        xk_whole = carve(region_m, "m", [KD, B * SKV])
        ntop_r = carve(region_m, "m", [P], parts=GH * QT)
        wo_s = carve(region_w, "w", [KD, D])
        wq_s = carve(region_w, "w", [KD, D])
        wk_s = carve(region_w, "w", [KD, D])
        wv_s = carve(region_w, "w", [KD, D])
        wxo_s = carve(region_w, "w", [KD, D])
        w12_s = region_r[:, 0:NE * KD * 2 * RH].rearrange("p (e k n) -> p e k n", e=NE, k=KD)
        w3_s = region_r[:, NE * KD * 2 * RH:].rearrange("p (e k n) -> p e k n", e=NE, k=KD)
        gathered = region_r[:, 0:NT * TOPK * D].rearrange("p (t k d) -> p t k d", t=NT, k=TOPK)
        sw1_s = region_s[:, 0:KD * FH].rearrange("p (k n) -> p k n", k=KD)
        sw2_s = region_s[:, KD * FH:2 * KD * FH].rearrange("p (k n) -> p k n", k=KD)
        sw3_s = region_s[:, 2 * KD * FH:].rearrange("p (k n) -> p k n", n=D)
        shared = feat_a[:].rearrange("p k t -> p (k t)").rearrange("p (t d) -> p t d", d=D)
        hidT = carve(region_w, "w2", [4, CH])
        sil = carve(region_m, "m2", [2, CH])
        scores = carve(region_m, "m2", [NT, NE])
        select = carve(region_m, "m2", [NT, NE])
        best = carve(region_m, "m2", [TOPK, 2, NT])
        onehot = carve(region_m, "m2", [TOPK, NE, NT])
        picked = carve(region_m, "m2", [NE, NT])
        work = carve(region_m, "m2", [NE, NT])
        scan_keep = carve(region_m, "m2", [NE, NT])
        rev_e = carve(region_m, "m2", [NE])
        experts = carve(region_m, "m2", [4, NE])
        slots_f = carve(region_m, "m2", [TOPK, NT])
        tile_work = carve(region_m, "m2", [48], parts=1)
        xs_in = carve(region_m, "m2", [2, D])
        xs_T = carve(region_m, "m2", [2, KD * P])
        xs_sil = carve(region_m, "m2", [2, RH])
        xs_h = carve(region_m, "m2", [2, RH])
        xs_out = carve(region_m, "m2", [4, KD * P])
        xs_hT, xs_y = xs_out[:, 0:2, :], xs_out[:, 2:4, :]

        idf = sb("idf", [P, P])
        idb = sb("idb", [P, P], BF16)
        causal_s = sb("causal_s", [P, GH, P], BF16)
        before_s = sb("before_s", [P, P])
        ones_s = sb("ones_s", [P, P])
        tops = sb("tops", [P, GH, QT, 2])
        ntop = sb("ntop", [P, P])
        stats = sb("stats", [P, TPC, 6])
        mean_var = sb("mean_var", [P, TPC, 2])
        std = sb("std", [P, TPC])
        rstd = sb("rstd", [P, TPC])
        bq_s = sb("bq_s", [P, KD])
        bk_s = sb("bk_s", [P, KD])
        router_s = sb("router_s", [P, KD, NE])
        ebias_b = sb("ebias_b", [P, NE])
        mask_u = sb("mask_u", [P, B * SKV], U8)
        eps_s = sb("eps_s", [P, 1])
        gates = sb("gates", [P, TOPK, NT])
        slots_u = sb("slots_u", [P, TOPK, NT], U32)
        tiles_i = sb("tiles_i", [P, NE], I32)
        expert_of = sb("expert_of", [1, 48], I32)
        iota_e = sb("iota_e", [P, NE])
        iota_t = sb("iota_t", [1, 48])

        gate_in, wqkv_in, small_in, ident_in, cross_w_in, rows_in = map(sem, (
            "gate_in", "wqkv_in", "small_in", "ident_in", "cross_w_in", "rows_in"))
        xT_in, oT_in, oxT_in = sems("xT_in", NCH), sems("oT_in", NCH), sems("oxT_in", NCH)
        xk_stored, xk_in, ones_rows, zeroed = map(sem, ("xk_stored", "xk_in", "ones_rows", "zeroed"))
        shared_w_in, routed_w_in = sem("shared_w_in"), sems("routed_w_in", 4)
        gate_sig, gate_prod, gate_ready, gate_out = map(sem, ("gate_sig", "gate_prod", "gate_ready", "gate_out"))
        ctx_ready, ctx_step, v_ready, v_taken = map(sem, ("ctx_ready", "ctx_step", "v_ready", "v_taken"))
        fill_ready = sem("fill_ready")
        projected, whole_ready, part1_ready, rest_ready, part2_ready, part3_ready = map(sem, (
            "projected", "whole_ready", "part1_ready", "rest_ready", "part2_ready", "part3_ready"))
        parts_stored = sems("parts_stored", ITEMS)
        set_up = sem("set_up")
        iota_ready = sem("iota_ready")

        class Signals:

            def __init__(self, a):
                self.stacks_in = sems(f"{a}_stacks_in", RING)
                self.staged = sem(f"{a}_staged")
                self.unit_ready = sem(f"{a}_unit_ready")
                self.unit_taken = sem(f"{a}_unit_taken")
                self.tops_ready = sem(f"{a}_tops_ready")
                self.top_split = sem(f"{a}_top_split")
                self.top_rows_in = sem(f"{a}_top_rows_in")
                self.scores_ready = sem(f"{a}_scores_ready")
                self.exp_done = sem(f"{a}_exp_done")
                self.masked = sem(f"{a}_masked")
                self.values_done = sem(f"{a}_values_done")
                self.o_taken = sem(f"{a}_o_taken")
                self.rec_ready = sem(f"{a}_rec_ready")
                self.o_scaled = sem(f"{a}_o_scaled")
                self.o_ready = sem(f"{a}_o_ready")
                self.o_stored = sems(f"{a}_o_stored", CPB)

        class BlockSignals:

            def __init__(self, a):
                self.out_ready = sem(f"{a}_out_ready")
                self.added = sem(f"{a}_added")
                self.stat_step = sem(f"{a}_stat_step")
                self.var_ready = sem(f"{a}_var_ready")
                self.std_ready = sem(f"{a}_std_ready")
                self.rstd_ready = sem(f"{a}_rstd_ready")
                self.normed = sem(f"{a}_normed")
                self.turned = sem(f"{a}_turned")
                self.turned_taken = sem(f"{a}_turned_taken")

        ss, cs = Signals("self"), Signals("cross")
        n1, n2, n3 = BlockSignals("norm1"), BlockSignals("norm2"), BlockSignals("norm3")
        bias_added = sem("bias_added")
        pool_turn, sync_turn, vector_turn = sem("pool_turn"), sem("sync_turn"), sem("vector_turn")
        logits_ready, scores_done, route_step, counted, slots_ready, expert_ready = map(sem, (
            "logits_ready", "scores_done", "route_step", "counted", "slots_ready", "expert_ready"))
        counts_ready, counts_taken = sem("counts_ready"), sem("counts_taken")
        scattered, gathered_in = sem("scattered"), sems("gathered_in", NCH)
        hid_ready, sil_done, hid_done, acc_ready, acc_taken, down_done = map(sem, (
            "hid_ready", "sil_done", "hid_done", "acc_ready", "acc_taken", "down_done"))
        slot_in, slot_turned, slot_T, slot_hid, slot_sil, slot_h, slot_hturned, slot_hT, slot_out, slot_y = (
            sems("slot_in", 2), sem("slot_turned"), sem("slot_T"), sem("slot_hid"), sem("slot_sil"), sem("slot_h"),
            sem("slot_hturned"), sem("slot_hT"), sem("slot_out"), sem("slot_y"))
        slot_stored = sems("slot_stored", 2)
        final_step, out_stored = sem("final_step"), sem("out_stored")

        block = ctx.enter_context(nc.Block())
        LOOPS = (NN - 2) // RING
        N_ITEMS = 4 * NCH

        @block.sync
        def _(sync):
            sync.dma_start(gate_rows[:, 0, :], gate_raw).then_inc(gate_in, 16)
            sync.dma_start(gate_rows[:, 1, :], gate_pick).then_inc(gate_in, 16)
            sync.dma_start(phase_s, phase).then_inc(gate_in, 16)
            sync.dma_start(wqkv_s, w_qkv.rearrange("(k p) n -> p k n", p=P)).then_inc(wqkv_in, 16)
            xT_v = xT.rearrange("(k p) t -> p k t", p=P)
            for n in range(NCH):
                sync.dma_start(feat_a[:, :, n * CH:(n + 1) * CH], xT_v[:, :, n * CH:(n + 1) * CH]).then_inc(xT_in[n], 16)
            for dst, src in ((idf[:], ident_f), (idb[:].bitcast(U16), ident_b), (causal_s[:].bitcast(U16), causal), (before_s[:], before)):
                sync.dma_start(dst, src).then_inc(ident_in, 16)

            def store_parts(it, n, m, dst_d, tile):
                sync.wait_ge(part3_ready, it + 1)
                b, c = divmod(n, CPB)
                g0 = NG * b + 2 * tile
                dst = dst_d[:, g0:g0 + 2, :, c * CH:(c + 1) * CH].rearrange("s g r t -> (g r) s t")
                sync.dma_start(dst, parts[:, it % ITEMS, :, :]).then_inc(parts_stored[it % ITEMS], 16)

            for n in range(NCH):
                for m in range(4):
                    store_parts(4 * n + m, n, m, (q_parts_d, k_parts_d)[m // KD], m % KD)

            for r in range(ITEMS):
                sync.wait_ge(parts_stored[r], 16 * len(range(r, N_ITEMS, ITEMS)))

            def load_stacks(A, s, n, p):
                for st, order, src_d in ((q_st, QUERY_PARTS, q_parts_d if A.causal else xq_parts_d),
                                         (k_st, KEY_PARTS, k_parts_d))[0:2 if A.causal else 1]:
                    for r0, r1, s0, count, copies in row_groups(order):
                        src = src_d[s0:s0 + count, bass.ds(n, 1)].rearrange("s o (d h) t -> s (o d) (h t)", d=HD)
                        if copies > 1:
                            src = src.to_broadcast([copies, HD, GH * S])
                        dst = st[r0 * HD:r1 * HD, p, :, :].rearrange("r h t -> r (h t)")
                        sync.dma_start(dst, src).then_inc(s.stacks_in[p], 16)

            def store_output(A, s, dst_d, n, c):
                sync.wait_ge(s.o_ready, CPB * n + c + 1)
                sync.sem_inc(sync_turn, 1)
                dst = dst_d[bass.ds(n, 1), :, c * CH:(c + 1) * CH].rearrange("o r t -> (o r) t")
                sync.dma_start(dst, o_nrm[:, c, :]).then_inc(s.o_stored[c], 16)

            def store_top_rows(A, s, n, p):
                sync.wait_ge(s.top_split, 3 * n + 3)
                for k in range(3):
                    dst = q_st[A.top_row + k:A.top_row + k + 1, p, :, :].rearrange("o h (i t) -> o (h i) t", t=P)
                    sync.dma_start(dst, ntop_p[:, k:k + 1, :]).then_inc(s.top_rows_in, 16)

            def attention(A, s, dst_d):
                def pair(n, p, last):
                    if A.causal:
                        store_output(A, s, dst_d, n, 0)
                    if not last:
                        store_top_rows(A, s, n + 1, (p + 1) % RING)
                    if not A.causal:
                        store_output(A, s, dst_d, n, 0)
                    store_output(A, s, dst_d, n, 1)

                for c in range(CPB):
                    sync.sem_inc(s.o_stored[c], 16)
                load_stacks(A, s, 0, 0)
                load_stacks(A, s, 1, 1)
                store_top_rows(A, s, 0, 0)
                with sync.Fori(0, LOOPS) as i:
                    for p in range(RING):
                        n = RING * i + p
                        sync.wait_ge(s.values_done, 1 + A.ns * n)
                        load_stacks(A, s, n + 2, (p + 2) % RING)
                        pair(n, p, False)
                pair(NN - 2, (NN - 2) % RING, False)
                pair(NN - 1, (NN - 1) % RING, True)
                for c in range(CPB):
                    sync.wait_ge(s.o_stored[c], 16 * (NN + 1))

            def load_output(dst_sems, src_d):
                for n in range(NCH):
                    b, c = divmod(n, CPB)
                    for k in range(KD):
                        g0 = NG * b + 2 * k
                        src = src_d[g0:g0 + 2, :, c * CH:(c + 1) * CH].rearrange("g (h r) t -> (g h) r t", r=32)[:, 0:HD, :]
                        sync.dma_start(feat_a[:, k, n * CH:(n + 1) * CH], src).then_inc(dst_sems[n], 16)

            sync.wait_ge(set_up, 6)
            attention(SELF, ss, o_self_d)
            load_output(oT_in, o_self_d)

            sync.wait_ge(ctx_step, 13)
            for m in range(KD):
                for b in range(B):
                    g0 = NG * b + 2 * m
                    src = xk_parts[:, :, (B * m + b) * SKV:(B * m + b + 1) * SKV]
                    sync.dma_start(xk_parts_d[:, g0:g0 + 2, :, :].rearrange("s g r t -> (g r) s t"), src).then_inc(xk_stored, 16)
            sync.wait_ge(xk_stored, 16 * KD * B)
            sync.wait_ge(ones_rows, 2)
            for r, part in enumerate(KEY_PARTS):
                src = xk_parts_d[part].rearrange("n (d h) t -> d n (h t)", d=HD)
                sync.dma_start(xk_all[r * HD:(r + 1) * HD, :, :], src).then_inc(xk_in, 16)
            for r in range(3):
                for b in range(B):
                    src = fill_row[:, r, b * SKV:(b + 1) * SKV][:, None, :].to_broadcast([1, NG * GH, SKV])
                    dst = xk_all[STACK + r:STACK + r + 1, NG * b:NG * (b + 1), :].rearrange("o g (h t) -> o (g h) t", h=GH)
                    sync.dma_start(dst, src).then_inc(xk_in, 16)

            for n in range(NCH):
                for m in range(KD):
                    store_parts(N_ITEMS + KD * n + m, n, m, xq_parts_d, m)
            total = N_ITEMS + KD * NCH
            for r in range(ITEMS):
                sync.wait_ge(parts_stored[r], 16 * len(range(r, total, ITEMS)))
            sync.wait_ge(ones_rows, 4)
            attention(CROSS, cs, o_cross_d)
            load_output(oxT_in, o_cross_d)

            sync.wait_ge(cs.values_done, 1 + CROSS.ns * NN)
            sync.wait_ge(bias_added, NT // TPC)
            for dst, src in ((sw1_s, sw1), (sw2_s, sw2)):
                sync.dma_start(dst, src.rearrange("(k p) n -> p k n", p=P)).then_inc(shared_w_in, 16)
            sync.dma_start(sw3_s, sw3.rearrange("(k p) n -> p k n", p=P)).then_inc(shared_w_in, 16)
            for q in range(4):
                e0, e1 = NE // 4 * q, NE // 4 * (q + 1)
                for w, src in enumerate((rw1, rw2)):
                    dst = w12_s[:, e0:e1, :, w * RH:(w + 1) * RH].rearrange("p e k n -> p (e k) n")
                    sync.dma_start(dst, src[e0:e1].rearrange("e (k p) n -> p (e k) n", p=P)).then_inc(routed_w_in[q], 16)
                dst = w3_s[:, e0:e1, :, :].rearrange("p e k n -> p (e k) n")
                sync.dma_start(dst, rw3[e0:e1].rearrange("e (k p) n -> p (e k) n", p=P)).then_inc(routed_w_in[q], 16)

            def load_slot(j, p):
                src = slots_x_d[bass.ds(j * P, P), :]
                sync.dma_start(xs_in[:, p, :], src).then_inc(slot_in[p], 16)

            def store_slot(j, p):
                sync.wait_ge(slot_y, j + 1)
                sync.sem_inc(sync_turn, 1)
                sync.dma_start(slots_y_d[bass.ds(j * P, P), :], xs_y[:, p, :]).then_inc(slot_stored[p], 16)

            sync.wait_ge(scattered, 16 * TOPK * NT)
            sync.wait_ge(zeroed, 32)
            load_slot(0, 0)
            load_slot(1, 1)
            for j in range(2):
                sync.wait_ge(slot_turned, j + 1)
                load_slot(j + 2, j % 2)
            with sync.Fori(1, (TILES - 1) // 2) as i:
                for p in range(2):
                    j = 2 * i + p
                    sync.wait_ge(slot_turned, j + 1)
                    sync.sem_inc(sync_turn, 1)
                    load_slot(j + 2, p)
                    store_slot(j - 2, p)
            for j in range(TILES - 3, TILES):
                store_slot(j, j % 2)

            out_v = out.rearrange("b (t p) d -> p (b t) d", p=P)
            for n in range(NCH):
                sync.wait_ge(n3.normed, TPC * (n + 1))
                sync.dma_start(out_v[:, TPC * n:TPC * (n + 1), :], rows[:, TPC * n:TPC * (n + 1), :]).then_inc(out_stored, 16)
            sync.wait_ge(out_stored, 16 * NCH)
            for r in range(2):
                sync.wait_ge(slot_stored[r], 16 * len(range(r, TILES, 2)))

        @block.gpsimd
        def _(pool):
            pool.iota(iota_e[:], [[1, NE]], base=0, channel_multiplier=0,
                      allow_small_or_imprecise_dtypes=True).then_inc(iota_ready, 1)
            pool.wait_ge(iota_ready, 1)
            pool.iota(iota_t[:], [[1, 48]], base=0, channel_multiplier=0,
                      allow_small_or_imprecise_dtypes=True).then_inc(iota_ready, 1)
            pool.wait_ge(iota_ready, 2)
            zero = pool.to_reg(0.0)

            def part3(it):
                r = it % ITEMS
                pool.wait_ge(part2_ready, it + 1)
                pool.tensor_tensor(parts[:, r, 2, :], rest[:, r, :], parts[:, r, 1, :], ALU.subtract).then_inc(part3_ready, 1)

            for it in range(N_ITEMS):
                part3(it)

            def stage(A, s, n, p):
                if A.causal:
                    src = v_all[:, bass.ds(n, 1), :, :].rearrange("p o t (h d) -> p (o t) h d", d=HD)
                    pool.tensor_copy(v_st[:, p, :, :, 0:HD], src).then_inc(s.staged, 1)
                else:
                    src = xv_all[:, bass.ds(n, 1), :].rearrange("p o (h d) -> p (o h) d", d=HD)
                    pool.tensor_copy(v_st[:, p, 0, :, 0:HD], src).then_inc(s.staged, 1)
                    keys = k_st[:, p, :, :].rearrange("p h t -> p (h t)")[:, 0:GH * SKV]
                    pool.tensor_copy(keys, xk_all[:, bass.ds(n, 1), :].rearrange("p o t -> p (o t)")).then_inc(s.staged, 1)

            def scale_output(s, n, c):
                pool.wait_ge(s.rec_ready, CPB * n + c + 1)
                blocks = o_blk[:, c, :].rearrange("p (q r) -> p q r", r=32)[:, :, 0:HD]
                rec = o_rec[:, c, :, None].to_broadcast([P, CH // 32, HD])
                pool.tensor_tensor(blocks, blocks, rec, ALU.mult).then_inc(s.o_scaled, 1)

            def attention(A, s):
                def pair(n):
                    for d, st in enumerate(A.diagonal):
                        pool.wait_ge(s.exp_done, 2 * (A.ns * n + st + 1))
                        pool.sem_inc(pool_turn, 1)
                        q0 = A.steps[st][2]
                        blk = probs[:, st % 4, :, q0:q0 + P]
                        pool.affine_select(out=blk, in_=blk, pattern=[[0, GH], [1, P]], compare_op=ALU.is_ge,
                                           fill=zero, base=0, channel_multiplier=-1).then_inc(s.masked, 1)
                        if st == A.last[0]:
                            scale_output(s, n, 0)
                    if not A.causal:
                        scale_output(s, n, 0)
                    scale_output(s, n, 1)

                stage(A, s, 0, 0)
                stage(A, s, 1, 1)
                with pool.Fori(0, LOOPS) as i:
                    for p in range(RING):
                        n = RING * i + p
                        pool.wait_ge(s.values_done, 1 + A.ns * n)
                        stage(A, s, n + 2, (p + 2) % RING)
                        pair(n)
                pair(NN - 2)
                pair(NN - 1)

            pool.wait_ge(v_taken, 2 * NCH)
            pool.wait_ge(set_up, 6)
            attention(SELF, ss)
            for it in range(N_ITEMS, N_ITEMS + KD * NCH):
                part3(it)
            for n in range(NCH):
                pool.wait_ge(n1.turned_taken, KD * (n + 1))
                pool.wait_ge(small_in, SMALL)
                tiles = rows[:, TPC * n:TPC * (n + 1), :]
                pool.tensor_tensor(tiles, tiles, bo_b[:, None, :].to_broadcast([P, TPC, D]), ALU.add).then_inc(bias_added, 1)
            pool.wait_ge(xk_in, 16 * (len(KEY_PARTS) + 3 * B))
            attention(CROSS, cs)

            pool.wait_ge(slots_ready, 1)
            pool.wait_ge(zeroed, 32)
            for t in range(NT):
                for k in range(TOPK):
                    pool.indirect_dma_start(out=slots_x_d, out_offset=bass.IndirectOffsetOnAxis(ap=slots_u[:, k, t:t + 1], axis=0),
                                            in_=rows[:, t, :], in_offset=None).then_inc(scattered, 16)
            for r in range(2):
                pool.wait_ge(slot_stored[r], 16 * len(range(r, TILES, 2)))
            pool.wait_ge(slot_out, TILES)
            for t in range(NT):
                for k in range(TOPK):
                    pool.indirect_dma_start(out=gathered[:, t, k, :], out_offset=None, in_=slots_y_d,
                                            in_offset=bass.IndirectOffsetOnAxis(ap=slots_u[:, k, t:t + 1], axis=0)
                                            ).then_inc(gathered_in[t // TPC], 16)

        @block.scalar
        def _(act):
            small = [(router_s[:], router_w.rearrange("(k p) n -> p k n", p=P)),
                     (ctxT_s, ctxT.rearrange("(k p) t -> p k t", p=P)),
                     (wk_s, w_k.rearrange("(k p) n -> p k n", p=P)), (wv_s, w_v.rearrange("(k p) n -> p k n", p=P)),
                     (bq_s[:], b_q), (bk_s[:], b_k),
                     (mask_u[:], mask.rearrange("b t -> (b t)").rearrange("(o t) -> o t", o=1).to_broadcast([P, B * SKV])),
                     (bv_b[0:SKV], b_v.rearrange("(o t) -> o t", o=1).to_broadcast([SKV, D])),
                     (bo_b, b_o.rearrange("(o t) -> o t", o=1).to_broadcast([P, D])),
                     (ebias_b[:], expert_bias.rearrange("(o t) -> o t", o=1).to_broadcast([P, NE])),
                     (wo_s, w_out.rearrange("(k p) n -> p k n", p=P)), (wq_s, w_q.rearrange("(k p) n -> p k n", p=P)),
                     (wxo_s, w_o.rearrange("(k p) n -> p k n", p=P))]
            for dst, src in small:
                act.dma_start(dst, src).then_inc(small_in, 16)
            assert 16 * len(small) == SMALL
            act.wait_ge(set_up, 1)
            halves = slots_x_d.rearrange("(j p) (c d) -> c p j d", p=P, c=2)
            for c in range(2):
                act.dma_start(halves[c], ntop[:, None, :].to_broadcast([P, TILES + 1, P])).then_inc(zeroed, 16)
            act.wait_ge(gate_in, 48)
            act.activation(gate_rows[:, 0, :], gate_rows[:, 0, :], ACT.Sigmoid).then_inc(gate_sig, 1)
            for k in range(4):
                act.wait_ge(gate_ready, k + 1)
                act.activation(gate[:, k // 2, (k % 2) * CH:(k % 2 + 1) * CH], PS[:, k, :], ACT.Copy).then_inc(gate_out, 1)

            def part1(it):
                act.wait_ge(whole_ready, it + 1)
                if it >= ITEMS:
                    act.wait_ge(parts_stored[it % ITEMS], 16 * (it // ITEMS))
                act.activation(parts[:, it % ITEMS, 0, :], whole[:, it % ITEMS, :], ACT.Copy).then_inc(part1_ready, 1)

            def part2(it):
                act.wait_ge(rest_ready, it + 1)
                act.activation(parts[:, it % ITEMS, 1, :], rest[:, it % ITEMS, :], ACT.Copy).then_inc(part2_ready, 1)

            for n in range(NCH):
                b, c = divmod(n, CPB)
                part1(4 * n)
                for it in range(4 * n + 1, 4 * n + 4):
                    part1(it)
                    part2(it - 1)
                part2(4 * n + 3)
                for v in range(2):
                    act.wait_ge(v_ready, 2 * n + v + 1)
                    for u in range(2):
                        ins = act.activation(v_all[:, NG * b:NG * (b + 1), TPC * c + 2 * v + u, :],
                                             PS[:, 4 + v, u * D:(u + 1) * D].rearrange("p (g r) -> p g r", g=NG), ACT.Copy)
                    ins.then_inc(v_taken, 1)
            act.wait_ge(v_ready, 2 * NCH)
            act.wait_ge(ctx_step, 13)
            act.dma_start(rows[:], x.rearrange("b (t p) d -> p (b t) d", p=P)).then_inc(rows_in, 16)

            def attention(A, s):
                def exponentials(n):
                    for st, (c, j, q0) in enumerate(A.steps):
                        act.wait_ge(s.values_done, 1 + A.ns * n + max(0, st - 3))
                        for hp in range(2):
                            act.wait_ge(s.scores_ready, 2 * (A.ns * n + st) + hp + 1)
                            act.activation(probs[0:A.keys, st % 4, 2 * hp:2 * hp + 2, q0:CH],
                                           PS[0:A.keys, 2 + 2 * hp:4 + 2 * hp, q0:CH], ACT.Exp, scale=SCALE).then_inc(s.exp_done, 1)

                with act.Fori(0, LOOPS) as i:
                    for p in range(RING):
                        exponentials(RING * i + p)
                exponentials(NN - 2)
                exponentials(NN - 1)

            def norm(g, n):
                act.wait_ge(g.var_ready, n + 1)
                act.wait_ge(g.rstd_ready, n)
                act.activation(std[:], mean_var[:, :, 1], ACT.Sqrt, bias=eps_s[:]).then_inc(g.std_ready, 1)

            def take_turned(g, n):
                for k in range(KD):
                    act.wait_ge(g.turned, KD * n + k + 1)
                    act.activation(feat_b[:, k, n * CH:(n + 1) * CH], PS[:, 4 + k, :], ACT.Copy).then_inc(g.turned_taken, 1)

            attention(SELF, ss)
            for n in range(NCH + 1):
                if n < NCH:
                    norm(n1, n)
                if n:
                    take_turned(n1, n - 1)
                    it = N_ITEMS + KD * (n - 1)
                    part1(it)
                    part1(it + 1)
                    part2(it)
                    part2(it + 1)
            attention(CROSS, cs)
            for n in range(NCH + 1):
                if n < NCH:
                    norm(n2, n)
                if n:
                    take_turned(n2, n - 1)

            act.wait_ge(logits_ready, 1)
            act.activation(scores, PS[:, 7, 0:NT * NE].rearrange("p (t e) -> p t e", e=NE), ACT.Sigmoid).then_inc(scores_done, 1)

            def shared_chunk(n):
                for h in range(FH // P):
                    act.wait_ge(hid_ready, 2 * (FH // P) * n + 2 * h + 1)
                    act.wait_ge(hid_done, (FH // P) * n + max(0, h - 1))
                    act.activation(sil[:, h % 2, :], PS[:, 2 * (h % 2), :], ACT.Silu).then_inc(sil_done, 1)

            for n in range(NCH // 2):
                shared_chunk(n)

            def slot_turn(j, p):
                act.wait_ge(slot_turned, j + 1)
                act.activation(xs_T[:, p, :], PS[:, p, 0:KD * P], ACT.Copy).then_inc(slot_T, 1)

            def slot_silu(j, p):
                act.wait_ge(slot_hid, j + 1)
                if not (isinstance(j, int) and j < 2):
                    act.wait_ge(slot_h, j - 1)
                act.activation(xs_sil[:, p, :], PS[:, 2 + p, 0:RH], ACT.Silu).then_inc(slot_sil, 1)

            act.wait_ge(acc_taken, 4 * NCH // 2)
            slot_turn(0, 0)
            for j in range(2):
                slot_turn(j + 1, (j + 1) % 2)
                slot_silu(j, j)
            with act.Fori(1, (TILES - 1) // 2) as i:
                for p in range(2):
                    slot_turn(2 * i + p + 1, 1 - p)
                    slot_silu(2 * i + p, p)
            slot_silu(TILES - 1, 0)
            with act.Fori(NCH // 2, NCH) as n:
                shared_chunk(n)
            for n in range(NCH):
                norm(n3, n)

        @block.tensor
        def _(pe):
            pe.wait_ge(gate_prod, 1)
            for k in range(4):
                pe.matmul(PS[:, k, :], gate_rows[:, 0, (k // 2) * P:(k // 2 + 1) * P],
                          phase_s[:, (k % 2) * CH:(k % 2 + 1) * CH], start=True, stop=True).then_inc(gate_ready, 1)
            pe.wait_ge(small_in, SMALL)
            for m in range(KD):
                for k in range(KD):
                    mm = pe.matmul(PS[:, 6, m * B * SKV:(m + 1) * B * SKV], wk_s[:, k, m * P:(m + 1) * P], ctxT_s[:, k, :],
                                   start=(k == 0), stop=(k == KD - 1))
            mm.then_inc(ctx_ready, 1)
            for b in range(B):
                for k in range(KD):
                    mm = pe.matmul(PS[0:SKV, 7, b * D:(b + 1) * D], ctxT_s[:, k, b * SKV:(b + 1) * SKV], wv_s[:, k, :],
                                   start=(k == 0), stop=(k == KD - 1))
            mm.then_inc(ctx_ready, 1)

            pe.wait_ge(wqkv_in, 16)
            pe.wait_ge(gate_out, 4)
            for n in range(NCH):
                pe.wait_ge(xT_in[n], 16)
                for m in range(4):
                    if n:
                        pe.wait_ge(whole_ready, 4 * (n - 1) + m + 1)
                    for k in range(KD):
                        mm = pe.matmul(PS[:, m, :], wqkv_s[:, k, m * P:(m + 1) * P], feat_a[:, k, n * CH:(n + 1) * CH],
                                       start=(k == 0), stop=(k == KD - 1))
                    mm.then_inc(projected, 1)
                if n:
                    pe.wait_ge(v_taken, 2 * n)
                for v in range(2):
                    for u in range(2):
                        t0 = n * CH + (2 * v + u) * P
                        for k in range(KD):
                            mm = pe.matmul(PS[:, 4 + v, u * D:(u + 1) * D], feat_a[:, k, t0:t0 + P], wqkv_s[:, k, 2 * D:3 * D],
                                           start=(k == 0), stop=(k == KD - 1))
                    mm.then_inc(v_ready, 1)

            def attention(A, s):
                ring_units = A.nu + 1
                loads = sum(len(row_groups(o)) for o in ((QUERY_PARTS, KEY_PARTS) if A.causal else (QUERY_PARTS,)))
                staged = 1 if A.causal else 2

                def stack_slot(i, p):
                    pe.wait_ge(s.stacks_in[p], 16 * loads * (i + 1))
                    if not A.causal:
                        pe.wait_ge(s.staged, staged * (RING * i + p + 1))

                def max_unit(n, p, k):
                    i, kc, h0, nh, w = A.units[k]
                    pe.wait_ge(s.unit_taken, ring_units * n + max(0, k - 1))
                    bank = PS[:, k % 2, :]
                    for a in range(nh):
                        keys = (k_st[0:A.max_rows, p, h0 + a, kc * CH:kc * CH + w] if A.causal else
                                k_st[0:A.max_rows, p, :, :].rearrange("p h t -> p (h t)")[:, (h0 + a) * w:(h0 + a + 1) * w])
                        mm = pe.matmul(bank[:, a * w:(a + 1) * w], q_st[0:A.max_rows, p, h0 + a, i * P:(i + 1) * P], keys,
                                       start=(a == 0), stop=False, skip_group_check=True)
                    if A.causal and kc == i // TPC:
                        out_ = bank[:, 0:nh * w].rearrange("p (a w) -> p a w", a=nh)[:, :, w - P:w]
                        mm = pe.matmul(out_, idb[:], causal_s[:, 0:nh, :], start=False, stop=True, skip_group_check=True)
                    mm.then_inc(s.unit_ready, 1)

                def turn_tops(n):
                    pe.wait_ge(s.tops_ready, n + 1)
                    pe.transpose(PS[:, A.nu % 2, 0:P], ntop[:], idf[:]).then_inc(s.unit_ready, 1)

                def values(n, p, st):
                    c, j, q0 = A.steps[st]
                    pe.wait_ge(s.exp_done, 2 * (A.ns * n + st + 1))
                    if st in A.diagonal:
                        pe.wait_ge(s.masked, len(A.diagonal) * n + A.diagonal.index(st) + 1)
                    if j == 0:
                        pe.wait_ge(s.o_taken, 1 + CPB * n)
                    for h in range(GH):
                        mm = pe.matmul(PS[32 * h:32 * h + 32, 6 + c, q0:CH], v_st[0:A.keys, p, j, h, :],
                                       probs[0:A.keys, st % 4, h, q0:CH], start=(j == 0), stop=(st == A.last[c]),
                                       skip_group_check=True)
                    mm.then_inc(s.values_done, 1)

                def pair(i, p, last):
                    n, p1 = RING * i + p, (p + 1) % RING
                    stack_slot(i, p)
                    pe.wait_ge(s.staged, staged * (n + 1))
                    pe.wait_ge(s.top_rows_in, 48 * (n + 1))
                    if not last:
                        stack_slot(i + (p + 1) // RING, p1)
                    for st, (c, j, q0) in enumerate(A.steps):
                        for hp in range(2):
                            if st:
                                pe.wait_ge(s.exp_done, 2 * (A.ns * n + st) + hp - 1)
                            for h in (2 * hp, 2 * hp + 1):
                                keys = (k_st[0:A.exp_rows, p, h, j * P:(j + 1) * P] if A.causal else
                                        k_st[0:A.exp_rows, p, :, :].rearrange("p h t -> p (h t)")[:, h * SKV:(h + 1) * SKV])
                                mm = pe.matmul(PS[0:A.keys, 2 + h, q0:CH], keys,
                                               q_st[0:A.exp_rows, p, h, c * CH + q0:(c + 1) * CH], start=True, stop=True)
                            mm.then_inc(s.scores_ready, 1)
                        if not last:
                            for k in A.units_of(st):
                                max_unit(n + 1, p1, k)
                        if st:
                            values(n, p, st - 1)
                        if st == A.top_step and not last:
                            turn_tops(n + 1)
                    values(n, p, A.ns - 1)

                pe.sem_inc(s.values_done, 1)
                stack_slot(0, 0)
                for k in range(A.nu):
                    max_unit(0, 0, k)
                turn_tops(0)
                with pe.Fori(0, LOOPS) as i:
                    for p in range(RING):
                        pair(i, p, False)
                pair(LOOPS, 0, False)
                pair(LOOPS, 1, True)

            def out_projection(g, n, w, in_sems):
                pe.wait_ge(in_sems[n], 16 * KD)
                for t in range(TPC * n, TPC * (n + 1)):
                    if t >= TPC:
                        pe.wait_ge(g.added, t - TPC + 1)
                    for k in range(KD):
                        mm = pe.matmul(PS[:, t % TPC, 0:D], feat_a[:, k, t * P:(t + 1) * P], w[:, k, :],
                                       start=(k == 0), stop=(k == KD - 1))
                    mm.then_inc(g.out_ready, 1)

            def turn(g, n):
                for k in range(KD):
                    if n:
                        pe.wait_ge(g.turned_taken, KD * (n - 1) + k + 1)
                    for u in range(TPC):
                        t = TPC * n + u
                        pe.wait_ge(g.normed, t + 1)
                        mm = pe.transpose(PS[:, 4 + k, u * P:(u + 1) * P], rows[:, t, k * P:(k + 1) * P], idf[:])
                    mm.then_inc(g.turned, 1)

            pe.wait_ge(whole_ready, N_ITEMS)
            pe.wait_ge(v_taken, 2 * NCH)
            pe.wait_ge(ctx_step, 10)
            pe.wait_ge(ident_in, 64)
            pe.wait_ge(set_up, 6)
            attention(SELF, ss)

            pe.wait_ge(ss.o_taken, 1 + CPB * NN)
            for n in range(NCH + 1):
                if n < NCH:
                    out_projection(n1, n, wo_s, oT_in)
                if n:
                    turn(n1, n - 1)
                    pe.wait_ge(n1.turned_taken, KD * n)
                    for m in range(KD):
                        if n > 1:
                            pe.wait_ge(whole_ready, N_ITEMS + KD * (n - 2) + m + 1)
                        for k in range(KD):
                            mm = pe.matmul(PS[:, 6 + m, :], wq_s[:, k, m * P:(m + 1) * P], feat_b[:, k, (n - 1) * CH:n * CH],
                                           start=(k == 0), stop=(k == KD - 1))
                        mm.then_inc(projected, 1)

            pe.wait_ge(n1.added, NT)
            pe.wait_ge(whole_ready, N_ITEMS + KD * NCH)
            pe.wait_ge(xk_in, 16 * (len(KEY_PARTS) + 3 * B))
            pe.wait_ge(ones_rows, 4)
            attention(CROSS, cs)

            pe.wait_ge(cs.o_taken, 1 + CPB * NN)
            for n in range(NCH + 1):
                if n < NCH:
                    out_projection(n2, n, wxo_s, oxT_in)
                if n:
                    turn(n2, n - 1)
                    pe.wait_ge(n2.turned_taken, KD * n)
                    for t in range(TPC * (n - 1), TPC * n):
                        for k in range(KD):
                            mm = pe.matmul(PS[:, 7, t * NE:(t + 1) * NE], feat_b[:, k, t * P:(t + 1) * P], router_s[:, k, :],
                                           start=(k == 0), stop=(k == KD - 1))
            mm.then_inc(logits_ready, 1)
            pe.wait_ge(n2.added, NT)

            def count_tokens():
                pe.wait_ge(scores_done, 1)
                pe.wait_ge(counted, 1)
                flat = picked.rearrange("p e t -> p (e t)")
                pe.matmul(PS[:, 7, 0:NE * NT], before_s[:], flat, start=True, stop=True)
                pe.matmul(PS[:, 7, NE * NT:2 * NE * NT], ones_s[:], flat, start=True, stop=True).then_inc(counts_ready, 1)

            count_tokens()

            def shared_chunk(n):
                hs = FH // P
                for h in range(hs + 1):
                    if h < hs:
                        pe.wait_ge(hid_done, hs * n + max(0, h - 1))
                        for w, ws in enumerate((sw1_s, sw2_s)):
                            for k in range(KD):
                                mm = pe.matmul(PS[:, 2 * (h % 2) + w, :], ws[:, k, h * P:(h + 1) * P],
                                               feat_b[:, k, bass.ds(n * CH, CH)], start=(k == 0), stop=(k == KD - 1))
                            mm.then_inc(hid_ready, 1)
                    if h:
                        pe.wait_ge(hid_done, hs * n + h)
                        if h == 1:
                            pe.wait_ge(acc_taken, TPC * n)
                        for u in range(TPC):
                            mm = pe.matmul(PS[:, 4 + u, 0:D], hidT[:, (h - 1) % 4, u * P:(u + 1) * P], sw3_s[:, h - 1, :],
                                           start=(h == 1), stop=(h == hs))
                        mm.then_inc(down_done, 1)

            pe.wait_ge(shared_w_in, 48)
            pe.wait_ge(counts_taken, 1)
            for n in range(NCH // 2):
                shared_chunk(n)

            pe.wait_ge(acc_taken, TPC * NCH // 2)
            pe.wait_ge(expert_ready, 1)
            for q in range(4):
                pe.wait_ge(routed_w_in[q], 48)

            def turn_slot(i, p):
                j = 2 * i + p
                pe.wait_ge(slot_in[p], 16 * (i + 1))
                if not (isinstance(j, int) and j < 2):
                    pe.wait_ge(slot_T, j - 1)
                for k in range(KD):
                    mm = pe.transpose(PS[:, p, k * P:(k + 1) * P], xs_in[:, p, k * P:(k + 1) * P], idf[:])
                mm.then_inc(slot_turned, 1)

            def hidden_slot(i, p, e):
                j = 2 * i + p
                pe.wait_ge(slot_T, j + 1)
                if not (isinstance(j, int) and j < 2):
                    pe.wait_ge(slot_h, j - 1)
                for k in range(KD):
                    w = w12_s[:, bass.ds(e, 1), k, :].rearrange("p o n -> p (o n)")
                    mm = pe.matmul(PS[:, 2 + p, :], xs_T[:, p, k * P:(k + 1) * P], w, start=(k == 0), stop=(k == KD - 1))
                mm.then_inc(slot_hid, 1)

            def turn_hidden(i, p):
                j = 2 * i + p
                pe.wait_ge(slot_h, j + 1)
                if not (isinstance(j, int) and j < 2):
                    pe.wait_ge(slot_hT, j - 1)
                for k in range(KD):
                    mm = pe.transpose(PS[:, 4 + p, k * P:(k + 1) * P], xs_h[:, p, k * P:(k + 1) * P], idf[:])
                mm.then_inc(slot_hturned, 1)

            def out_slot(i, p, e):
                j = 2 * i + p
                pe.wait_ge(slot_hT, j + 1)
                if not (isinstance(j, int) and j < 2):
                    pe.wait_ge(slot_y, j - 1)
                for k in range(KD):
                    w = w3_s[:, bass.ds(e, 1), k, :].rearrange("p o n -> p (o n)")
                    mm = pe.matmul(PS[:, 6 + p, 0:D], xs_hT[:, p, k * P:(k + 1) * P], w, start=(k == 0), stop=(k == KD - 1))
                mm.then_inc(slot_out, 1)

            def expert(j):
                return pe.value_load(expert_of[0:1, bass.ds(j, 1)], min_val=0, max_val=NE - 1)

            turn_slot(0, 0)
            turn_slot(0, 1)
            hidden_slot(0, 0, expert(0))
            turn_slot(1, 0)
            hidden_slot(0, 1, expert(1))
            turn_hidden(0, 0)

            def step(i, p):
                j = 2 * i + p
                turn_slot(i + p, 1 - p)
                hidden_slot(i, p, expert(j))
                out_slot(i - 1, p, expert(j - 2))
                turn_hidden(i - 1 + p, 1 - p)

            step(1, 0)
            step(1, 1)
            with pe.Fori(2, (TILES - 1) // 2) as i:
                for p in range(2):
                    step(i, p)
            i = (TILES - 1) // 2
            hidden_slot(i, 0, expert(2 * i))
            out_slot(i - 1, 0, expert(2 * i - 2))
            turn_hidden(i - 1, 1)
            out_slot(i - 1, 1, expert(2 * i - 1))
            turn_hidden(i, 0)
            out_slot(i, 0, expert(2 * i))
            pe.wait_ge(slot_y, TILES)

            with pe.Fori(NCH // 2, NCH) as n:
                shared_chunk(n)


        @block.vector
        def _(v):
            v.memset(ntop[:], 0.0).then_inc(set_up, 1)
            v.memset(tops[:], LOWEST).then_inc(set_up, 1)
            v.memset(eps_s[:], EPS).then_inc(set_up, 1)
            v.memset(k_st[STACK:STACK + 3], 1.0).then_inc(set_up, 1)
            v.memset(v_st[:], 0.0).then_inc(set_up, 1)
            v.wait_ge(set_up, 5)
            v.memset(v_st[:, :, :, :, HD:HD + 1], 1.0).then_inc(set_up, 1)
            v.memset(ones_s[:], 1.0).then_inc(ones_rows, 1)
            v.memset(xk_all[STACK:P], 1.0).then_inc(ones_rows, 1)
            v.memset(xv_all[:], 0.0).then_inc(ones_rows, 1)

            v.wait_ge(gate_sig, 1)
            v.tensor_tensor(gate_rows[:, 0, :], gate_rows[:, 0, :], gate_rows[:, 1, :], ALU.mult).then_inc(gate_prod, 1)

            v.wait_ge(small_in, SMALL)
            v.tensor_copy(mask_b, mask_u[:]).then_inc(ctx_step, 1)
            v.wait_ge(ctx_ready, 1)
            for m in range(KD):
                v.tensor_scalar(xk_whole[:, m, :], PS[:, 6, m * B * SKV:(m + 1) * B * SKV], bk_s[:, m:m + 1], None,
                                ALU.add).then_inc(ctx_step, 1)
            v.wait_ge(ctx_step, 3)
            v.tensor_tensor(xk_whole, xk_whole, mask_b[:, None, :].to_broadcast([P, KD, B * SKV]), ALU.mult).then_inc(ctx_step, 1)
            xk_part = [xk_parts[:, r, :].rearrange("p (m t) -> p m t", m=KD) for r in range(3)]
            v.wait_ge(ctx_step, 4)
            v.tensor_copy(xk_part[0], xk_whole).then_inc(ctx_step, 1)
            v.wait_ge(ctx_step, 5)
            v.tensor_tensor(xk_rest, xk_whole, xk_part[0], ALU.subtract).then_inc(ctx_step, 1)
            v.wait_ge(ctx_step, 6)
            v.tensor_copy(xk_part[1], xk_rest).then_inc(ctx_step, 1)
            v.wait_ge(ctx_step, 7)
            v.tensor_tensor(xk_part[2], xk_rest, xk_part[1], ALU.subtract).then_inc(ctx_step, 1)
            v.wait_ge(ctx_ready, 2)
            v.wait_ge(ones_rows, 3)
            for b in range(B):
                v.tensor_tensor(xv_all[0:SKV, NG * b:NG * (b + 1), :], PS[0:SKV, 7, b * D:(b + 1) * D].rearrange("p (g r) -> p g r", g=NG),
                                bv_b[0:SKV].rearrange("p (g r) -> p g r", g=NG), ALU.add).then_inc(ctx_step, 1)
            for r in range(3):
                v.tensor_scalar(fill_row[:, r, :], mask_b[0:1], -1.0, FILL_PARTS[r], ALU.add, ALU.mult).then_inc(ctx_step, 1)

            def take_whole(it, make):
                r = it % ITEMS
                v.wait_ge(projected, it + 1)
                if it >= ITEMS:
                    v.wait_ge(part1_ready, it - ITEMS + 1)
                    v.wait_ge(rest_ready, it - ITEMS + 1)
                make(whole[:, r, :]).then_inc(whole_ready, 1)

            def take_rest(it):
                r = it % ITEMS
                v.wait_ge(part1_ready, it + 1)
                if it >= ITEMS:
                    v.wait_ge(part3_ready, it - ITEMS + 1)
                v.tensor_tensor(rest[:, r, :], whole[:, r, :], parts[:, r, 0, :], ALU.subtract).then_inc(rest_ready, 1)

            def gated(m, c):
                return lambda dst: v.tensor_tensor(dst, PS[:, m, :], gate[:, m, c * CH:(c + 1) * CH], ALU.mult)

            def copied(m):
                return lambda dst: v.tensor_copy(dst, PS[:, m, :])

            def biased(m):
                return lambda dst: v.tensor_scalar(dst, PS[:, 6 + m, :], bq_s[:, m:m + 1], None, ALU.add)

            def split(first, makes):
                take_whole(first, makes[0])
                for k, make in enumerate(makes[1:]):
                    take_whole(first + k + 1, make)
                    take_rest(first + k)
                take_rest(first + len(makes) - 1)

            v.wait_ge(gate_out, 4)
            for n in range(NCH):
                split(4 * n, [gated(0, n % CPB), gated(1, n % CPB), copied(2), copied(3)])

            def attention(A, s):
                ring_units = A.nu + 1

                def take_unit(n, k):
                    i, kc, h0, nh, w = A.units[k]
                    v.wait_ge(s.unit_ready, ring_units * n + k + 1)
                    v.tensor_reduce(tops[:, h0:h0 + nh, i, kc], PS[:, k % 2, 0:nh * w].rearrange("p (a w) -> p a w", a=nh),
                                    AX.X, ALU.max).then_inc(s.unit_taken, 1)

                def fold_tops(n):
                    v.wait_ge(s.unit_taken, ring_units * n + A.nu)
                    v.wait_ge(s.unit_ready, ring_units * n)
                    v.tensor_reduce(ntop[:, 0:GH * QT], tops[:].rearrange("p h i c -> p (h i) c"), AX.X, ALU.max,
                                    negate=True).then_inc(s.tops_ready, 1)

                def split_tops(n):
                    v.wait_ge(s.unit_ready, ring_units * (n + 1))
                    v.wait_ge(s.top_rows_in, 48 * n)
                    src = PS[0:GH * QT, A.nu % 2, 0:P]
                    v.tensor_copy(ntop_p[:, 0, :], src).then_inc(s.top_split, 1)
                    v.wait_ge(s.top_split, 3 * n + 1)
                    v.tensor_tensor(ntop_r, src, ntop_p[:, 0, :], ALU.subtract).then_inc(s.unit_taken, 1)
                    v.wait_ge(s.unit_taken, ring_units * (n + 1))
                    v.tensor_copy(ntop_p[:, 1, :], ntop_r).then_inc(s.top_split, 1)
                    v.wait_ge(s.top_split, 3 * n + 2)
                    v.tensor_tensor(ntop_p[:, 2, :], ntop_r, ntop_p[:, 1, :], ALU.subtract).then_inc(s.top_split, 1)

                def take_output(n, c):
                    v.wait_ge(s.values_done, 1 + A.ns * n + A.last[c] + 1)
                    v.transpose(o_blk[:, c, :], PS[:, 6 + c, :]).then_inc(s.o_taken, 1)
                    v.wait_ge(s.o_taken, 1 + CPB * n + c + 1)
                    v.reciprocal(o_rec[:, c, :], o_blk[:, c, HD:CH:32]).then_inc(s.rec_ready, 1)

                def give_output(n, c):
                    v.wait_ge(s.o_scaled, CPB * n + c + 1)
                    v.wait_ge(s.o_stored[c], 16 * (n + 1))
                    v.transpose(o_nrm[:, c, :], o_blk[:, c, :]).then_inc(s.o_ready, 1)

                def pair(n, last):
                    for st in range(A.ns):
                        if not last:
                            for k in A.units_of(st):
                                take_unit(n + 1, k)
                            if st == A.unit_steps - 1:
                                fold_tops(n + 1)
                        if st - 1 == A.last[0]:
                            take_output(n, 0)
                        if st - 2 == A.last[0]:
                            give_output(n, 0)
                        if st == A.top_step and not last:
                            split_tops(n + 1)
                    if A.ns - 1 < A.last[0] + 2:
                        give_output(n, 0)
                    take_output(n, 1)
                    give_output(n, 1)

                v.sem_inc(s.o_taken, 1)
                for k in range(A.nu):
                    take_unit(0, k)
                fold_tops(0)
                split_tops(0)
                with v.Fori(0, LOOPS) as i:
                    for p in range(RING):
                        pair(RING * i + p, False)
                pair(NN - 2, False)
                pair(NN - 1, True)

            def moments(g, n):
                for u in range(TPC):
                    v.wait_ge(g.added, TPC * n + u + 1)
                    v.bn_stats(stats[:, u, :], rows[:, TPC * n + u, :]).then_inc(g.stat_step, 1)
                for u in range(TPC):
                    v.wait_ge(g.stat_step, 2 * TPC * n + u + 1)
                    v.bn_aggr(mean_var[:, u, :], stats[:, u, :]).then_inc(g.stat_step, 1)
                v.wait_ge(g.stat_step, 2 * TPC * (n + 1))
                v.sem_inc(g.var_ready, 1)

            def add_block(g, n):
                for u in range(TPC):
                    t = TPC * n + u
                    v.wait_ge(g.out_ready, t + 1)
                    v.tensor_tensor(rows[:, t, :], PS[:, u, 0:D], rows[:, t, :], ALU.add).then_inc(g.added, 1)
                moments(g, n)

            def normalise(g, n):
                v.wait_ge(g.std_ready, n + 1)
                v.reciprocal(rstd[:], std[:]).then_inc(g.rstd_ready, 1)
                v.wait_ge(g.rstd_ready, n + 1)
                for u in range(TPC):
                    t = TPC * n + u
                    v.tensor_scalar(rows[:, t, :], rows[:, t, :], mean_var[:, u, 0:1], rstd[:, u:u + 1],
                                    ALU.subtract, ALU.mult).then_inc(g.normed, 1)

            v.wait_ge(set_up, 6)
            v.wait_ge(zeroed, 32)
            attention(SELF, ss)
            v.wait_ge(ss.scores_ready, 2 * SELF.ns * NN)
            v.memset(q_st[STACK:STACK + 3], 1.0).then_inc(ones_rows, 1)
            v.wait_ge(ss.tops_ready, NN)
            v.memset(tops[:], LOWEST).then_inc(ones_rows, 1)

            v.wait_ge(rows_in, 16)
            for n in range(NCH + 1):
                if n < NCH:
                    add_block(n1, n)
                if n:
                    split(N_ITEMS + KD * (n - 1), [biased(m) for m in range(KD)])
                if n < NCH:
                    normalise(n1, n)

            v.wait_ge(ones_rows, 5)
            attention(CROSS, cs)

            for n in range(NCH):
                v.wait_ge(bias_added, n + 1)
                add_block(n2, n)
                normalise(n2, n)

            steps = 0

            def routed():
                v.wait_ge(route_step, steps)

            def by_token(a):
                return a.rearrange("p e t -> p t e")

            v.memset(experts[:, 3, :], 1.0).then_inc(route_step, 1)
            v.memset(scan_keep, 1.0).then_inc(route_step, 1)
            v.wait_ge(route_step, 2)
            v.memset(scan_keep[:, :, 0:1], 0.0).then_inc(route_step, 1)
            v.wait_ge(iota_ready, 2)
            v.tensor_scalar(rev_e, iota_e[:], -1.0, float(NE), ALU.mult, ALU.add).then_inc(route_step, 1)
            v.wait_ge(scores_done, 1)
            v.tensor_tensor(select, scores, ebias_b[:, None, :].to_broadcast([P, NT, NE]), ALU.add).then_inc(route_step, 1)
            steps += 5
            for k in range(TOPK):
                routed()
                v.tensor_reduce(best[:, k, 0, :], select, AX.X, ALU.max).then_inc(route_step, 1)
                steps += 1
                routed()
                v.tensor_tensor(by_token(work), select, best[:, k, 0, :, None].to_broadcast([P, NT, NE]),
                                ALU.is_equal).then_inc(route_step, 1)
                steps += 1
                routed()
                v.tensor_tensor(by_token(work), by_token(work), rev_e[:, None, :].to_broadcast([P, NT, NE]),
                                ALU.mult).then_inc(route_step, 1)
                steps += 1
                routed()
                v.tensor_reduce(best[:, k, 1, :], by_token(work), AX.X, ALU.max).then_inc(route_step, 1)
                steps += 1
                routed()
                v.tensor_tensor(by_token(onehot[:, k]), rev_e[:, None, :].to_broadcast([P, NT, NE]),
                                best[:, k, 1, :, None].to_broadcast([P, NT, NE]), ALU.is_equal).then_inc(route_step, 1)
                steps += 1
                if k == 0:
                    routed()
                    v.scalar_tensor_tensor(select, by_token(onehot[:, k]), LOWEST, select, ALU.mult, ALU.add).then_inc(route_step, 1)
                    steps += 1
            routed()
            v.tensor_tensor(picked, onehot[:, 0], onehot[:, 1], ALU.add).then_inc(counted, 1)
            for k in range(TOPK):
                v.tensor_tensor(by_token(work), by_token(onehot[:, k]), scores, ALU.mult).then_inc(route_step, 1)
                steps += 1
                routed()
                v.tensor_reduce(gates[:, k, :], by_token(work), AX.X, ALU.add).then_inc(route_step, 1)
                steps += 1
                routed()

            v.wait_ge(counts_ready, 1)
            before_n = PS[:, 7, 0:NE * NT].rearrange("p (e t) -> p e t", e=NE)
            in_tile = PS[:, 7, NE * NT:2 * NE * NT].rearrange("p (e t) -> p e t", e=NE)
            v.tensor_tensor_scan(work.rearrange("p e t -> p (e t)"), scan_keep.rearrange("p e t -> p (e t)"),
                                 PS[:, 7, NE * NT:2 * NE * NT], 0.0, ALU.mult, ALU.add).then_inc(route_step, 1)
            steps += 1
            routed()
            v.tensor_scalar(tiles_i[:], work[:, :, NT - 1], float(P - 1), None, ALU.add).then_inc(route_step, 1)
            steps += 1
            routed()
            v.tensor_single_scalar(tiles_i[:], tiles_i[:], P.bit_length() - 1, ALU.arith_shift_right).then_inc(route_step, 1)
            steps += 1
            routed()
            v.tensor_copy(experts[:, 0, :], tiles_i[:]).then_inc(route_step, 1)
            steps += 1
            routed()
            v.tensor_tensor_scan(experts[:, 1, :], experts[:, 3, :], experts[:, 0, :], 0.0, ALU.mult, ALU.add).then_inc(route_step, 1)
            steps += 1
            routed()
            v.tensor_tensor(experts[:, 2, :], experts[:, 1, :], experts[:, 0, :], ALU.subtract).then_inc(route_step, 1)
            v.tensor_tensor(work, work, in_tile, ALU.subtract).then_inc(route_step, 1)
            steps += 2
            routed()
            v.tensor_tensor(work, work, before_n, ALU.add).then_inc(route_step, 1)
            steps += 1
            routed()
            v.sem_inc(counts_taken, 1)
            v.scalar_tensor_tensor(work, experts[:, 2, :, None].to_broadcast([P, NE, NT]), float(P), work,
                                   ALU.mult, ALU.add).then_inc(route_step, 1)
            steps += 1
            for k in range(TOPK):
                routed()
                v.tensor_tensor(picked, onehot[:, k], work, ALU.mult).then_inc(route_step, 1)
                steps += 1
                routed()
                v.tensor_reduce(slots_f[:, k, :], by_token(picked), AX.X, ALU.add).then_inc(route_step, 1)
                steps += 1
            routed()
            v.tensor_copy(slots_u[:], slots_f).then_inc(slots_ready, 1)
            ended = xs_out[0:1].rearrange("p r n -> p (r n)")[:, 0:48 * NE].rearrange("p (j e) -> p j e", e=NE)
            v.tensor_tensor(ended, iota_t[:, :, None].to_broadcast([1, 48, NE]),
                            experts[0:1, 1, None, :].to_broadcast([1, 48, NE]), ALU.is_ge).then_inc(route_step, 1)
            steps += 1
            routed()
            v.tensor_reduce(tile_work, ended, AX.X, ALU.add).then_inc(route_step, 1)
            steps += 1
            routed()
            v.tensor_scalar(expert_of[:], tile_work, float(NE - 1), None, ALU.min).then_inc(expert_ready, 1)

            def shared_chunk(n):
                hs = FH // P
                for h in range(hs):
                    v.wait_ge(hid_ready, 2 * hs * n + 2 * h + 2)
                    v.wait_ge(sil_done, hs * n + h + 1)
                    v.wait_ge(down_done, hs * n + max(0, h - 3))
                    v.tensor_tensor(hidT[:, h % 4, :], sil[:, h % 2, :], PS[:, 2 * (h % 2) + 1, :], ALU.mult).then_inc(hid_done, 1)
                v.wait_ge(down_done, hs * (n + 1))
                v.sem_inc(vector_turn, 1)
                for u in range(TPC):
                    dst = shared[:, bass.ds(TPC * n + u, 1), :].rearrange("p o d -> p (o d)")
                    v.tensor_copy(dst, PS[:, 4 + u, 0:D]).then_inc(acc_taken, 1)

            for n in range(NCH // 2):
                shared_chunk(n)

            def multiply(i, p):
                j = 2 * i + p
                v.wait_ge(slot_sil, j + 1)
                if not (isinstance(j, int) and j < 2):
                    v.wait_ge(slot_hturned, j - 1)
                v.tensor_tensor(xs_h[:, p, :], xs_sil[:, p, :], PS[:, 2 + p, RH:2 * RH], ALU.mult).then_inc(slot_h, 1)

            def take_hidden(i, p):
                v.wait_ge(slot_hturned, 2 * i + p + 1)
                v.tensor_copy(xs_hT[:, p, :], PS[:, 4 + p, 0:KD * P]).then_inc(slot_hT, 1)

            def take_slot(i, p):
                v.wait_ge(slot_out, 2 * i + p + 1)
                v.wait_ge(slot_stored[p], 16 * i)
                v.tensor_copy(xs_y[:, p, :], PS[:, 6 + p, 0:D]).then_inc(slot_y, 1)

            multiply(0, 0)
            multiply(0, 1)
            take_hidden(0, 0)

            def step(i, p):
                multiply(i, p)
                take_slot(i - 1, p)
                take_hidden(i - 1 + p, 1 - p)

            step(1, 0)
            step(1, 1)
            with v.Fori(2, (TILES - 1) // 2) as i:
                for p in range(2):
                    step(i, p)
            i = (TILES - 1) // 2
            multiply(i, 0)
            take_slot(i - 1, 0)
            take_hidden(i - 1, 1)
            take_slot(i - 1, 1)
            take_hidden(i, 0)
            take_slot(i, 0)

            with v.Fori(NCH // 2, NCH) as n:
                shared_chunk(n)

            final = 0
            for n in range(NCH):
                tiles = rows[:, TPC * n:TPC * (n + 1), :]
                v.wait_ge(acc_taken, TPC * (n + 1))
                v.tensor_tensor(tiles, tiles, shared[:, TPC * n:TPC * (n + 1), :], ALU.add).then_inc(final_step, 1)
                final += 1
                v.wait_ge(gathered_in[n], 16 * TOPK * TPC)
                for k in range(TOPK):
                    v.wait_ge(final_step, final)
                    for t in range(TPC * n, TPC * (n + 1)):
                        v.scalar_tensor_tensor(rows[:, t, :], gathered[:, t, k, :], gates[:, k, t:t + 1], rows[:, t, :],
                                               ALU.mult, ALU.add).then_inc(final_step if k == 0 else n3.added, 1)
                    final += TPC if k == 0 else 0
                moments(n3, n)
                normalise(n3, n)


_HEADS = D // HD


def _columns():
    return np.array([GH * HD * g + HD * h + d for g in range(NG) for d in range(HD) for h in range(GH)])


def _gate_rows(values):
    raw = np.zeros((P, D), values.dtype)
    pick = np.zeros((P, D), np.float32)
    row = 0
    for c, cycle in enumerate(TALA_CYCLES):
        for r in range(cycle):
            for h in range(c, _HEADS, len(TALA_CYCLES)):
                raw[row, HD * h:HD * (h + 1)] = values[h, r]
                pick[row, HD * h:HD * (h + 1)] = 1
            row += 1
    cols = _columns()
    return raw[:, cols], pick[:, cols]


def _phase_rows():
    rows = np.zeros((P, S), np.float32)
    row = 0
    for cycle in TALA_CYCLES:
        for r in range(cycle):
            rows[row, r::cycle] = 1
            row += 1
    return rows


def _operands(inputs):
    g = {k: np.asarray(v) for k, v in inputs.items()}
    cols = _columns()
    w_qkv = g["L0_attn_w_qkv"]
    raw, pick = _gate_rows(g["L0_attn_bandha_gate"])
    key, query = np.arange(P)[None, :], np.arange(P)[:, None]
    causal = np.where(key <= query, 0, bf16_bits(LATER_KEY)).astype(np.uint16)
    ops = {
        "x": g["x"], "xT": g["x"].reshape(TOK, D).T, "ctxT": g["ctx_1024"].reshape(B * SKV, D).T,
        "mask": g["mask_BxS2_bf1"].view(np.uint8),
        "w_qkv": np.concatenate([w_qkv[:, 0:D][:, cols], w_qkv[:, D:2 * D][:, cols], w_qkv[:, 2 * D:]], axis=1),
        "gate_raw": raw, "gate_pick": pick, "phase": _phase_rows(), "w_out": g["L0_attn_w_out"],
        "w_q": g["L0_xattn_Wq"].T[:, cols], "b_q": g["L0_xattn_bq"][cols].reshape(KD, P).T,
        "w_k": g["L0_xattn_Wk"].T[:, cols], "b_k": g["L0_xattn_bk"][cols].reshape(KD, P).T,
        "w_v": g["L0_xattn_Wv"].T, "b_v": g["L0_xattn_bv"], "w_o": g["L0_xattn_Wo"].T, "b_o": g["L0_xattn_bo"],
        "router_w": g["L0_ffn_router_w"], "expert_bias": g["L0_ffn_expert_bias"],
        "sw1": g["L0_ffn_shared_w1"][0], "sw2": g["L0_ffn_shared_w2"][0], "sw3": g["L0_ffn_shared_w3"][0],
        "rw1": g["L0_ffn_routed_w1"], "rw2": g["L0_ffn_routed_w2"], "rw3": g["L0_ffn_routed_w3"],
        "ident_f": np.eye(P, dtype=np.float32), "ident_b": np.eye(P, dtype=np.uint16) * np.uint16(bf16_bits(1.0)),
        "causal": np.broadcast_to(causal[:, None, :], (P, GH, P)),
        "before": (np.arange(P)[:, None] < np.arange(P)[None, :]).astype(np.float32),
    }
    return {k: np.ascontiguousarray(v) for k, v in ops.items()}


def kernel(**inputs):
    import concourse.bacc as bacc
    from concourse import mybir as mb
    from concourse.bass_utils import run_bass_kernel_spmd

    nc = bacc.Bacc("TRN2", target_bir_lowering=False, num_devices=1)
    arrays, args = {}, []
    for name, a in _operands(inputs).items():
        arrays[f"in_{name}_dram"] = a
        args.append(nc.dram_tensor(f"in_{name}_dram", a.shape, mb.dt.from_np(a.dtype), kind="ExternalInput").ap())
    args.append(nc.dram_tensor("out_dram", (B, S, D), mb.dt.float32, kind="ExternalOutput").ap())
    decoder_layer(nc, *args)
    result = run_bass_kernel_spmd(nc, [arrays], core_ids=[0])
    return result.results[0]["out_dram"]
```

```python
from contextlib import ExitStack

import numpy as np

import concourse.bass as bass
from concourse import mybir

ALU = mybir.AluOpType
ACT = mybir.ActivationFunctionType
AX = mybir.AxisListType
F32 = mybir.dt.float32
BF16 = mybir.dt.bfloat16
I32 = mybir.dt.int32
U32 = mybir.dt.uint32
U16 = mybir.dt.uint16
U8 = mybir.dt.uint8

P = 128
B, S, D = 2, 1024, 256
TOK = B * S
HD = 16
SKV = 77
KD = D // P
CH = 512
NCH = TOK // CH
CPB = S // CH
GH = 4
NG = D // HD // GH
NN = B * NG
QT = S // P
TPC = CH // P
NT = TOK // P
FH = 1024
NE, RH, TOPK = 16, 256, 2
TILES = (TOPK * TOK + NE * (P - 1)) // P
EPS = 1e-5
SCALE = float(HD) ** -0.5
MASK_FILL = 1e8
LOWEST = -3e38
LATER_KEY = -1e30
RING = 3
ITEMS = 3
QUERY_PARTS = (0, 0, 0, 1, 1, 2)
KEY_PARTS = (0, 1, 2, 0, 1, 0)
STACK = len(QUERY_PARTS) * HD
SMALL = 16 * 13
TALA_CYCLES = (5, 6, 7, 8)


def row_groups(parts):
    runs, r = [], 0
    while r < len(parts):
        n = 1
        step = 0 if r + 1 < len(parts) and parts[r + 1] == parts[r] else 1
        while r + n < len(parts) and parts[r + n] == parts[r] + step * n:
            n += 1
        runs.append((r, r + n, parts[r], 1 if step == 0 else n, n if step == 0 else 1))
        r += n
    return runs


def bf16_bits(x):
    bits = int(np.float32(x).view(np.uint32))
    return (bits + 0x7FFF + ((bits >> 16) & 1)) >> 16


def bf16_round(x):
    return float(np.uint32(bf16_bits(x) << 16).view(np.float32))


def bf16_parts(x):
    out = []
    for _ in range(3):
        out.append(bf16_round(x))
        x -= out[-1]
    assert x == 0
    return out


FILL_PARTS = bf16_parts(MASK_FILL / SCALE)


class Attention:

    def __init__(self, causal):
        self.causal = causal
        self.keys = P if causal else SKV
        if causal:
            self.units = []
            for i in range(QT):
                for kc in range(i // TPC + 1):
                    w = min(CH, (i + 1) * P - CH * kc)
                    per = CH // w
                    self.units += [(i, kc, h0, per, w) for h0 in range(0, GH, per)]
            order = ((0, 3, 1, 2), (0, 7, 1, 6, 5, 4, 2, 3))
            self.steps = [(c, j, max(0, j - TPC * c) * P) for c in range(CPB) for j in order[c]]
            self.unit_steps, self.top_step = 8, 9
            self.extra = 0
            self.slots, self.lag, self.take_lag = 4, 2, 3
        else:
            self.units = []
            self.steps = [(c, 0, 0) for c in range(CPB)]
            self.unit_steps, self.top_step = 0, -1
            self.slots, self.lag, self.take_lag = 2, 1, 1
            self.extra = 3
        self.nu, self.ns = len(self.units), len(self.steps)
        self.last = [max(s for s, e in enumerate(self.steps) if e[0] == c) for c in range(CPB)]
        self.diagonal = [s for s, (c, j, _) in enumerate(self.steps) if causal and j >= TPC * c]
        self.top_row = STACK + self.extra
        self.max_rows, self.exp_rows = STACK + self.extra, STACK + self.extra + 3

    def units_of(self, s, quarter):
        if s >= self.unit_steps:
            return range(0)
        at = 4 * s + quarter
        return range(self.nu * at // (4 * self.unit_steps), self.nu * (at + 1) // (4 * self.unit_steps))

    def output_at(self, s, lag):
        return [(back, c) for back in (1, 0) for c in range(CPB) if self.last[c] + lag == s + self.ns * back]


FINISH = {(NCH - 2, 4 + part): (0, part) for part in range(TOPK + 2)}
FINISH.update({(NCH - 1, 4 * n + part): (1 + n, part) for n in range(2) for part in range(TOPK + 2)})

SELF, CROSS = Attention(True), Attention(False)


def decoder_layer(nc, x, xT, ctxT, mask, w_qkv, gate_raw, gate_pick, phase, w_out, w_q, b_q, w_k, b_k, w_v, b_v,
                  w_o, b_o, router_w, expert_bias, sw1, sw2, sw3, rw1, rw2, rw3,
                  ident_f, ident_b, causal, before, ones, out):
    q_parts_d = nc.dram_tensor("q_parts_d", [3, NN, GH * HD, S], BF16, kind="Internal").ap()
    k_parts_d = nc.dram_tensor("k_parts_d", [3, NN, GH * HD, S], BF16, kind="Internal").ap()
    xq_parts_d = nc.dram_tensor("xq_parts_d", [3, NN, GH * HD, S], BF16, kind="Internal").ap()
    xk_parts_d = nc.dram_tensor("xk_parts_d", [3, NN, GH * HD, SKV], BF16, kind="Internal").ap()
    o_self_d = nc.dram_tensor("o_self_d", [NN, P, S], F32, kind="Internal").ap()
    o_cross_d = nc.dram_tensor("o_cross_d", [NN, P, S], F32, kind="Internal").ap()
    slots_x_d = nc.dram_tensor("slots_x_d", [(TILES + 1) * P, D], F32, kind="Internal").ap()
    slots_y_d = nc.dram_tensor("slots_y_d", [TILES * P, D], F32, kind="Internal").ap()

    ctx = ExitStack()
    with ctx:
        def sb(name, shape, dt=F32):
            return ctx.enter_context(nc.sbuf_tensor(name, shape, dt))

        def sem(name):
            return ctx.enter_context(nc.semaphore(name))

        def sems(name, n):
            return [sem(f"{name}{i}") for i in range(n)]

        PS = ctx.enter_context(nc.psum_tensor("PS", [P, 8, CH], F32))

        feat_a = sb("feat_a", [P, KD, TOK])
        feat_b = sb("feat_b", [P, KD, TOK])
        rows = sb("rows", [P, NT, D])
        region_r = sb("region_r", [P, 24576])
        region_s = sb("region_s", [P, 6144])
        region_m = sb("region_m", [P, 6144])
        region_w = sb("region_w", [P, 2560])
        used = {}

        def carve(region, key, shape, dt=F32, parts=P):
            words = int(np.prod(shape)) * (2 if dt == BF16 else 4) // 4
            at = used.get(key, 0)
            used[key] = at + words
            assert at + words <= region.shape[1], (key, at + words)
            flat = region[0:parts, at:at + words]
            if dt != F32:
                flat = flat.bitcast(dt)
            names = "abcde"[:len(shape)]
            if len(shape) == 1:
                return flat
            return flat.rearrange(f"p ({' '.join(names)}) -> p {' '.join(names)}",
                                  **{n: s for n, s in zip(names[1:], shape[1:])})

        rows_flat = rows[:].rearrange("p t d -> p (t d)")
        wqkv_s = carve(rows_flat, "rows", [KD, 3 * D])
        gate_rows = carve(rows_flat, "rows", [2, D])
        phase_s = carve(rows_flat, "rows", [S])
        mask_b = carve(rows_flat, "rows", [B * SKV])
        xk_rest = carve(rows_flat, "rows", [KD, B * SKV])
        bv_b = carve(rows_flat, "rows", [D])
        v_st = carve(region_r, "r", [RING, QT, GH, 32])
        xk_parts = carve(region_r, "r", [3, KD * B * SKV], BF16)
        bo_b = carve(region_r, "r", [D])
        ntop_p = carve(region_r, "r", [3, P], BF16)
        used["rx"] = used["r"]
        q_st = carve(region_r, "r", [RING, GH, S], BF16)
        k_st = carve(region_r, "r", [RING, GH, S], BF16)
        probs = carve(region_r, "r", [SELF.slots, GH, CH])
        xq_all = carve(region_r, "rx", [NN, GH * S], BF16)
        xprobs = carve(region_r, "rx", [CROSS.slots, GH, CH])
        gate = carve(region_s, "s", [KD, S])
        o_blk = carve(region_s, "s", [CPB, CH])
        o_nrm = carve(region_s, "s", [CPB, CH])
        o_rec = carve(region_s, "s", [CPB, CH // 32])
        xk_all = carve(region_s, "s", [NN, GH * SKV], BF16)
        xv_all = carve(region_s, "s", [NN, GH * HD])
        fill_row = carve(region_s, "s", [3, B * SKV], BF16, parts=1)
        v_all = feat_b[:].rearrange("p k t -> p (k t)").rearrange("p (n t r) -> p n t r", n=NN, t=QT)
        whole = carve(region_m, "m", [ITEMS, CH])
        rest = carve(region_m, "m", [ITEMS, CH])
        parts = carve(region_m, "m", [ITEMS, 3, CH], BF16)
        ctxT_s = carve(region_m, "m", [KD, B * SKV])
        xk_whole = carve(region_m, "m", [KD, B * SKV])
        ntop_r = carve(region_m, "m", [P])
        wo_s = carve(region_w, "w", [KD, D])
        wq_s = carve(region_w, "w", [KD, D])
        wk_s = carve(region_w, "w", [KD, D])
        wv_s = carve(region_w, "w", [KD, D])
        wxo_s = carve(region_w, "w", [KD, D])
        w12_s = region_r[:, 0:NE * KD * 2 * RH].rearrange("p (e k n) -> p e k n", e=NE, k=KD)
        w3_s = region_r[:, NE * KD * 2 * RH:].rearrange("p (e k n) -> p e k n", e=NE, k=KD)
        gathered = region_r[:, 0:NT * TOPK * D].rearrange("p (t k d) -> p t k d", t=NT, k=TOPK)
        sw1_s = region_s[:, 0:KD * FH].rearrange("p (k n) -> p k n", k=KD)
        sw2_s = region_s[:, KD * FH:2 * KD * FH].rearrange("p (k n) -> p k n", k=KD)
        sw3_s = region_s[:, 2 * KD * FH:].rearrange("p (k n) -> p k n", n=D)
        shared = feat_a[:].rearrange("p k t -> p (k t)").rearrange("p (t d) -> p t d", d=D)
        hidT = carve(region_w, "w2", [4, CH])
        sil = carve(region_m, "m2", [2, CH])
        scores = carve(region_m, "m2", [NT, NE])
        select = carve(region_m, "m2", [NT, NE])
        best = carve(region_m, "m2", [TOPK, 2, NT])
        onehot = carve(region_m, "m2", [TOPK, NE, NT])
        picked = carve(region_m, "m2", [NE, NT])
        work = carve(region_m, "m2", [NE, NT])
        scan_keep = carve(region_m, "m2", [NE, NT])
        rev_e = carve(region_m, "m2", [NE])
        experts = carve(region_m, "m2", [4, NE])
        slots_f = carve(region_m, "m2", [TOPK, NT])
        tile_work = carve(region_m, "m2", [48], parts=1)
        xs_in = carve(region_m, "m2", [2, D])
        xs_T = carve(region_m, "m2", [2, KD * P])
        xs_sil = carve(region_m, "m2", [2, RH])
        xs_h = carve(region_m, "m2", [2, RH])
        xs_out = carve(region_m, "m2", [4, KD * P])
        xs_hT, xs_y = xs_out[:, 0:2, :], xs_out[:, 2:4, :]

        idf = sb("idf", [P, P])
        idb = sb("idb", [P, P], BF16)
        causal_s = sb("causal_s", [P, GH, P], BF16)
        before_s = sb("before_s", [P, P])
        ones_s = sb("ones_s", [P, P])
        tops = sb("tops", [P, GH, QT, 2])
        ntop = sb("ntop", [P, P])
        stats = sb("stats", [P, TPC, 6])
        mean_var = sb("mean_var", [P, TPC, 2])
        std = sb("std", [P, TPC])
        rstd = sb("rstd", [P, TPC])
        bq_s = sb("bq_s", [P, KD])
        bk_s = sb("bk_s", [P, KD])
        router_s = sb("router_s", [P, KD, NE])
        ebias_b = sb("ebias_b", [P, NE])
        mask_u = sb("mask_u", [P, B * SKV], U8)
        eps_s = sb("eps_s", [P, 1])
        gates = sb("gates", [P, TOPK, NT])
        slots_u = sb("slots_u", [P, TOPK, NT], U32)
        tiles_i = sb("tiles_i", [P, NE], I32)
        expert_of = sb("expert_of", [1, 48], I32)
        iota_e = sb("iota_e", [P, NE])
        iota_t = sb("iota_t", [1, 48])

        gate_in, wqkv_in, small_in, ident_in, cross_w_in, rows_in = map(sem, (
            "gate_in", "wqkv_in", "small_in", "ident_in", "cross_w_in", "rows_in"))
        xT_in, oT_in, oxT_in = sems("xT_in", NCH), sems("oT_in", NCH), sems("oxT_in", NCH)
        xk_stored, xk_in, ones_rows, zeroed = map(sem, ("xk_stored", "xk_in", "ones_rows", "zeroed"))
        shared_w_in, routed_w_in = sem("shared_w_in"), sems("routed_w_in", 4)
        gate_sig, gate_prod, gate_ready, gate_out = map(sem, ("gate_sig", "gate_prod", "gate_ready", "gate_out"))
        ctx_ready, ctx_step, v_ready, v_taken = map(sem, ("ctx_ready", "ctx_step", "v_ready", "v_taken"))
        projected, whole_ready, part1_ready, rest_ready, part2_ready, part3_ready = map(sem, (
            "projected", "whole_ready", "part1_ready", "rest_ready", "part2_ready", "part3_ready"))
        parts_stored = sems("parts_stored", ITEMS)
        set_up = sem("set_up")
        iota_ready = sem("iota_ready")

        class Signals:

            def __init__(self, a, causal):
                if causal:
                    self.stacks_in = sems(f"{a}_stacks_in", RING)
                    self.masked = sem(f"{a}_masked")
                self.staged = sem(f"{a}_staged")
                self.unit_ready = sem(f"{a}_unit_ready")
                self.unit_taken = sem(f"{a}_unit_taken")
                self.tops_ready = sem(f"{a}_tops_ready")
                self.top_split = sem(f"{a}_top_split")
                self.top_rows_in = sem(f"{a}_top_rows_in")
                self.scores_ready = sem(f"{a}_scores_ready")
                self.exp_done = sem(f"{a}_exp_done")
                self.values_done = sem(f"{a}_values_done")
                self.o_taken = sem(f"{a}_o_taken")
                self.rec_ready = sem(f"{a}_rec_ready")
                self.o_scaled = sem(f"{a}_o_scaled")
                self.o_ready = sem(f"{a}_o_ready")
                self.o_stored = sems(f"{a}_o_stored", CPB)

        class BlockSignals:

            def __init__(self, a):
                self.out_ready = sem(f"{a}_out_ready")
                self.added = sem(f"{a}_added")
                self.stat_step = sem(f"{a}_stat_step")
                self.var_ready = sem(f"{a}_var_ready")
                self.std_ready = sem(f"{a}_std_ready")
                self.rstd_ready = sem(f"{a}_rstd_ready")
                self.normed = sem(f"{a}_normed")
                self.turned = sem(f"{a}_turned")
                self.turned_taken = sem(f"{a}_turned_taken")

        ss, cs = Signals("self", True), Signals("cross", False)
        n1, n2, n3 = BlockSignals("norm1"), BlockSignals("norm2"), BlockSignals("norm3")
        bias_added = sem("bias_added")
        xq_in = sems("xq_in", B)
        xtops_turned, xtop_rest = sem("xtops_turned"), sem("xtop_rest")
        pool_turn, sync_turn, vector_turn = sem("pool_turn"), sem("sync_turn"), sem("vector_turn")
        logits_ready, scores_done, route_step, counted, slots_ready, expert_ready = map(sem, (
            "logits_ready", "scores_done", "route_step", "counted", "slots_ready", "expert_ready"))
        counts_ready, counts_taken = sem("counts_ready"), sem("counts_taken")
        scattered, gathered_in = sem("scattered"), sems("gathered_in", NCH)
        hid_ready, sil_done, hid_done, acc_taken, down_done = map(sem, (
            "hid_ready", "sil_done", "hid_done", "acc_taken", "down_done"))
        slot_in, slot_turned, slot_T, slot_hid, slot_sil, slot_h, slot_hturned, slot_hT, slot_out, slot_y = (
            sems("slot_in", 2), sem("slot_turned"), sem("slot_T"), sem("slot_hid"), sem("slot_sil"), sem("slot_h"),
            sem("slot_hturned"), sem("slot_hT"), sem("slot_out"), sem("slot_y"))
        slot_stored = sems("slot_stored", 2)
        final_step, out_stored = sem("final_step"), sem("out_stored")

        block = ctx.enter_context(nc.Block())
        LOOPS = (NN - 2) // RING
        N_ITEMS = 4 * NCH
        XBANKS = 4

        @block.sync
        def _(sync):
            sync.dma_start(gate_rows[:, 0, :], gate_raw).then_inc(gate_in, 16)
            sync.dma_start(gate_rows[:, 1, :], gate_pick).then_inc(gate_in, 16)
            sync.dma_start(phase_s, phase).then_inc(gate_in, 16)
            sync.dma_start(wqkv_s, w_qkv.rearrange("(k p) n -> p k n", p=P)).then_inc(wqkv_in, 16)
            xT_v = xT.rearrange("(k p) t -> p k t", p=P)
            for n in range(NCH):
                sync.dma_start(feat_a[:, :, n * CH:(n + 1) * CH], xT_v[:, :, n * CH:(n + 1) * CH]).then_inc(xT_in[n], 16)
            for dst, src in ((idf[:], ident_f), (idb[:].bitcast(U16), ident_b), (causal_s[:].bitcast(U16), causal), (before_s[:], before)):
                sync.dma_start(dst, src).then_inc(ident_in, 16)

            def store_parts(it, n, m, dst_d, tile):
                sync.wait_ge(part3_ready, it + 1)
                b, c = divmod(n, CPB)
                g0 = NG * b + 2 * tile
                dst = dst_d[:, g0:g0 + 2, :, c * CH:(c + 1) * CH].rearrange("s g r t -> (g r) s t")
                sync.dma_start(dst, parts[:, it % ITEMS, :, :]).then_inc(parts_stored[it % ITEMS], 16)

            def wait_stored(items):
                for r in range(ITEMS):
                    sync.wait_ge(parts_stored[r], 16 * len(range(r, items, ITEMS)))

            def load_stacks(s, n, p):
                for st, order, src_d in ((q_st, QUERY_PARTS, q_parts_d), (k_st, KEY_PARTS, k_parts_d)):
                    for r0, r1, s0, count, copies in row_groups(order):
                        src = src_d[s0:s0 + count, bass.ds(n, 1)].rearrange("s o (d h) t -> s (o d) (h t)", d=HD)
                        if copies > 1:
                            src = src.to_broadcast([copies, HD, GH * S])
                        dst = st[r0 * HD:r1 * HD, p, :, :].rearrange("r h t -> r (h t)")
                        sync.dma_start(dst, src).then_inc(s.stacks_in[p], 16)

            def store_output(A, s, dst_d, n, c):
                sync.wait_ge(s.o_ready, CPB * (n + 1) + (c + 1))
                sync.sem_inc(sync_turn, 1)
                dst = dst_d[bass.ds(n, 1), :, c * CH:(c + 1) * CH].rearrange("o r t -> (o r) t")
                sync.dma_start(dst, o_nrm[:, c, :]).then_inc(s.o_stored[c], 16)

            def store_top_rows(A, s, n, p):
                sync.wait_ge(s.top_split, 3 * n + 3)
                for k in range(3):
                    dst = q_st[A.top_row + k:A.top_row + k + 1, p, :, :].rearrange("o h (i t) -> o (h i) t", t=P)
                    sync.dma_start(dst, ntop_p[0:GH * QT, k:k + 1, :]).then_inc(s.top_rows_in, 16)

            def load_output(in_sems, src_d, n):
                b, c = divmod(n, CPB)
                for k in range(KD):
                    g0 = NG * b + 2 * k
                    src = src_d[g0:g0 + 2, :, c * CH:(c + 1) * CH].rearrange("g (h r) t -> (g h) r t", r=32)[:, 0:HD, :]
                    sync.dma_start(feat_a[:, k, n * CH:(n + 1) * CH], src).then_inc(in_sems[n], 16)

            def attention(A, s, dst_d, in_sems):
                def pair(n, p, last):
                    store_output(A, s, dst_d, n, 0)
                    if A.causal and not last:
                        store_top_rows(A, s, n + 1, (p + 1) % RING)
                    store_output(A, s, dst_d, n, 1)

                for c in range(CPB):
                    sync.sem_inc(s.o_stored[c], 16)
                if A.causal:
                    store_top_rows(A, s, 0, 0)
                with sync.Fori(0, LOOPS) as i:
                    for p in range(RING):
                        n = RING * i + p
                        if A.causal:
                            sync.wait_ge(s.values_done, A.slots + A.ns * n)
                            load_stacks(s, n + 2, (p + 2) % RING)
                        pair(n, p, False)
                for c in range(CPB):
                    sync.wait_ge(s.o_stored[c], 16 * (NG + 1))
                    load_output(in_sems, dst_d, c)
                pair(NN - 2, (NN - 2) % RING, False)
                pair(NN - 1, (NN - 1) % RING, True)
                for c in range(CPB):
                    sync.wait_ge(s.o_stored[c], 16 * (NN + 1))
                    load_output(in_sems, dst_d, CPB + c)

            for n in range(NCH):
                for m in range(4):
                    store_parts(4 * n + m, n, m, (q_parts_d, k_parts_d)[m // KD], m % KD)
                if n == CPB - 1:
                    wait_stored(4 * CPB)
                    sync.wait_ge(set_up, 6)
                    load_stacks(ss, 0, 0)
                    load_stacks(ss, 1, 1)
            wait_stored(N_ITEMS)
            sync.wait_ge(v_ready, 2 * NCH)
            attention(SELF, ss, o_self_d, oT_in)

            sync.dma_start(xq_all[STACK:STACK + 3].bitcast(U16), ones.rearrange("(o n t) -> o n t", o=1, n=1)
                           .to_broadcast([3, NN, GH * S])).then_inc(xq_in[0], 16)
            sync.wait_ge(ctx_step, 13)
            for m in range(KD):
                for b in range(B):
                    g0 = NG * b + 2 * m
                    src = xk_parts[:, :, (B * m + b) * SKV:(B * m + b + 1) * SKV]
                    sync.dma_start(xk_parts_d[:, g0:g0 + 2, :, :].rearrange("s g r t -> (g r) s t"), src).then_inc(xk_stored, 16)
            sync.wait_ge(xk_stored, 16 * KD * B)
            sync.wait_ge(ones_rows, 2)
            for r, part in enumerate(KEY_PARTS):
                src = xk_parts_d[part].rearrange("n (d h) t -> d n (h t)", d=HD)
                sync.dma_start(xk_all[r * HD:(r + 1) * HD, :, :], src).then_inc(xk_in, 16)
            for r in range(3):
                for b in range(B):
                    src = fill_row[:, r, b * SKV:(b + 1) * SKV][:, None, :].to_broadcast([1, NG * GH, SKV])
                    dst = xk_all[STACK + r:STACK + r + 1, NG * b:NG * (b + 1), :].rearrange("o g (h t) -> o (g h) t", h=GH)
                    sync.dma_start(dst, src).then_inc(xk_in, 16)

            for n in range(NCH):
                for m in range(KD):
                    store_parts(N_ITEMS + KD * n + m, n, m, xq_parts_d, m)
                if n % CPB == CPB - 1:
                    wait_stored(N_ITEMS + KD * (n + 1))
                    b = n // CPB
                    for r, part in enumerate(QUERY_PARTS):
                        src = xq_parts_d[part, NG * b:NG * (b + 1)].rearrange("g (d h) t -> d g (h t)", d=HD)
                        sync.dma_start(xq_all[r * HD:(r + 1) * HD, NG * b:NG * (b + 1), :], src).then_inc(xq_in[b], 16)
            for b in range(B):
                sync.wait_ge(cs.top_split, 3 * (b + 1))
                for k in range(3):
                    dst = xq_all[CROSS.top_row + k:CROSS.top_row + k + 1, NG * b:NG * (b + 1), :]
                    dst = dst.rearrange("o g (r t) -> o (g r) t", t=P)
                    sync.dma_start(dst, ntop_p[:, k:k + 1, :]).then_inc(cs.top_rows_in, 16)
            sync.wait_ge(n1.out_ready, NT)
            attention(CROSS, cs, o_cross_d, oxT_in)

            sync.wait_ge(cs.values_done, CROSS.slots + CROSS.ns * NN)
            sync.wait_ge(bias_added, NT // TPC)
            for dst, src in ((sw1_s, sw1), (sw2_s, sw2)):
                sync.dma_start(dst, src.rearrange("(k p) n -> p k n", p=P)).then_inc(shared_w_in, 16)
            sync.dma_start(sw3_s, sw3.rearrange("(k p) n -> p k n", p=P)).then_inc(shared_w_in, 16)
            for q in range(4):
                e0, e1 = NE // 4 * q, NE // 4 * (q + 1)
                for w, src in enumerate((rw1, rw2)):
                    dst = w12_s[:, e0:e1, :, w * RH:(w + 1) * RH].rearrange("p e k n -> p (e k) n")
                    sync.dma_start(dst, src[e0:e1].rearrange("e (k p) n -> p (e k) n", p=P)).then_inc(routed_w_in[q], 16)
                dst = w3_s[:, e0:e1, :, :].rearrange("p e k n -> p (e k) n")
                sync.dma_start(dst, rw3[e0:e1].rearrange("e (k p) n -> p (e k) n", p=P)).then_inc(routed_w_in[q], 16)

            def load_slot(j, p):
                src = slots_x_d[bass.ds(j * P, P), :]
                sync.dma_start(xs_in[:, p, :], src).then_inc(slot_in[p], 16)

            def store_slot(j, p):
                sync.wait_ge(slot_y, j + 1)
                sync.sem_inc(sync_turn, 1)
                sync.dma_start(slots_y_d[bass.ds(j * P, P), :], xs_y[:, p, :]).then_inc(slot_stored[p], 16)

            sync.wait_ge(scattered, 16 * TOPK * NT)
            sync.wait_ge(zeroed, 32)
            load_slot(0, 0)
            load_slot(1, 1)
            for j in range(2):
                sync.wait_ge(slot_turned, j + 1)
                load_slot(j + 2, j % 2)
            with sync.Fori(1, (TILES - 1) // 2) as i:
                for p in range(2):
                    j = 2 * i + p
                    sync.wait_ge(slot_turned, j + 1)
                    sync.sem_inc(sync_turn, 1)
                    load_slot(j + 2, p)
                    store_slot(j - 2, p)
            for j in range(TILES - 3, TILES):
                store_slot(j, j % 2)

            out_v = out.rearrange("b (t p) d -> p (b t) d", p=P)
            for n in range(NCH):
                sync.wait_ge(n3.normed, TPC * (n + 1))
                sync.dma_start(out_v[:, TPC * n:TPC * (n + 1), :], rows[:, TPC * n:TPC * (n + 1), :]).then_inc(out_stored, 16)
            sync.wait_ge(out_stored, 16 * NCH)
            for r in range(2):
                sync.wait_ge(slot_stored[r], 16 * len(range(r, TILES, 2)))

        @block.gpsimd
        def _(pool):
            pool.iota(iota_e[:], [[1, NE]], base=0, channel_multiplier=0,
                      allow_small_or_imprecise_dtypes=True).then_inc(iota_ready, 1)
            pool.wait_ge(iota_ready, 1)
            pool.iota(iota_t[:], [[1, 48]], base=0, channel_multiplier=0,
                      allow_small_or_imprecise_dtypes=True).then_inc(iota_ready, 1)
            pool.wait_ge(iota_ready, 2)
            zero = pool.to_reg(0.0)

            def part3(it):
                r = it % ITEMS
                pool.wait_ge(part2_ready, it + 1)
                pool.tensor_tensor(parts[:, r, 2, :], rest[:, r, :], parts[:, r, 1, :], ALU.subtract).then_inc(part3_ready, 1)

            for it in range(N_ITEMS):
                part3(it)

            def stage(A, s, n, p):
                if A.causal:
                    src = v_all[:, bass.ds(n, 1), :, :].rearrange("p o t (h d) -> p (o t) h d", d=HD)
                    pool.tensor_copy(v_st[:, p, :, :, 0:HD], src).then_inc(s.staged, 1)
                else:
                    src = xv_all[:, bass.ds(n, 1), :].rearrange("p o (h d) -> p (o h) d", d=HD)
                    pool.tensor_copy(v_st[:, p, 0, :, 0:HD], src).then_inc(s.staged, 1)

            def scale_output(s, n, c):
                pool.wait_ge(s.rec_ready, CPB * n + c + 1)
                blocks = o_blk[:, c, :].rearrange("p (q r) -> p q r", r=32)[:, :, 0:HD]
                rec = o_rec[:, c, :, None].to_broadcast([P, CH // 32, HD])
                pool.tensor_tensor(blocks, blocks, rec, ALU.mult).then_inc(s.o_scaled, 1)

            def self_attention(A, s):
                def pair(n, p):
                    for st, (_, _, q0) in enumerate(A.steps):
                        if st in A.diagonal:
                            pool.wait_ge(s.exp_done, 2 * (A.ns * n + st + 1))
                            pool.sem_inc(pool_turn, 1)
                            blk = probs[:, st % A.slots, :, q0:q0 + P]
                            pool.affine_select(out=blk, in_=blk, pattern=[[0, GH], [1, P]], compare_op=ALU.is_ge,
                                               fill=zero, base=0, channel_multiplier=-1).then_inc(s.masked, 1)
                        for back, c in A.output_at(st, A.take_lag):
                            if not (isinstance(n, int) and n < back):
                                scale_output(s, n - back, c)
                        if st == A.take_lag and not (isinstance(n, int) and n == NN - 1):
                            stage(A, s, n + 1, (p + 1) % RING)

                stage(A, s, 0, 0)
                pair(0, 0)
                with pool.Fori(0, LOOPS) as i:
                    for q in range(RING):
                        pair(RING * i + (q + 1), (q + 1) % RING)
                pair(NN - 1, (NN - 1) % RING)
                scale_output(s, NN - 1, 1)

            def cross_attention(A, s):
                def pair(n):
                    scale_output(s, n, 0)
                    scale_output(s, n, 1)

                stage(A, s, 0, 0)
                stage(A, s, 1, 1)
                with pool.Fori(0, LOOPS) as i:
                    for p in range(RING):
                        n = RING * i + p
                        pool.wait_ge(s.values_done, A.slots + A.ns * n)
                        stage(A, s, n + 2, (p + 2) % RING)
                        pair(n)
                pair(NN - 2)
                pair(NN - 1)

            pool.wait_ge(v_taken, 2 * NCH)
            pool.wait_ge(set_up, 6)
            self_attention(SELF, ss)
            for it in range(N_ITEMS, N_ITEMS + KD * NCH):
                part3(it)
            for n in range(NCH):
                pool.wait_ge(n1.turned_taken, KD * (n + 1))
                pool.wait_ge(small_in, SMALL)
                tiles = rows[:, TPC * n:TPC * (n + 1), :]
                pool.tensor_tensor(tiles, tiles, bo_b[:, None, :].to_broadcast([P, TPC, D]), ALU.add).then_inc(bias_added, 1)
            pool.wait_ge(xk_in, 16 * (len(KEY_PARTS) + 3 * B))
            cross_attention(CROSS, cs)

            pool.wait_ge(slots_ready, 1)
            pool.wait_ge(zeroed, 32)
            for t in range(NT):
                for k in range(TOPK):
                    pool.indirect_dma_start(out=slots_x_d, out_offset=bass.IndirectOffsetOnAxis(ap=slots_u[:, k, t:t + 1], axis=0),
                                            in_=rows[:, t, :], in_offset=None).then_inc(scattered, 16)
            for r in range(2):
                pool.wait_ge(slot_stored[r], 16 * len(range(r, TILES, 2)))
            pool.wait_ge(slot_out, TILES)
            for t in range(NT):
                for k in range(TOPK):
                    pool.indirect_dma_start(out=gathered[:, t, k, :], out_offset=None, in_=slots_y_d,
                                            in_offset=bass.IndirectOffsetOnAxis(ap=slots_u[:, k, t:t + 1], axis=0)
                                            ).then_inc(gathered_in[t // TPC], 16)

        @block.scalar
        def _(act):
            small = [(router_s[:], router_w.rearrange("(k p) n -> p k n", p=P)),
                     (ctxT_s, ctxT.rearrange("(k p) t -> p k t", p=P)),
                     (wk_s, w_k.rearrange("(k p) n -> p k n", p=P)), (wv_s, w_v.rearrange("(k p) n -> p k n", p=P)),
                     (bq_s[:], b_q), (bk_s[:], b_k),
                     (mask_u[:], mask.rearrange("b t -> (b t)").rearrange("(o t) -> o t", o=1).to_broadcast([P, B * SKV])),
                     (bv_b[0:SKV], b_v.rearrange("(o t) -> o t", o=1).to_broadcast([SKV, D])),
                     (bo_b, b_o.rearrange("(o t) -> o t", o=1).to_broadcast([P, D])),
                     (ebias_b[:], expert_bias.rearrange("(o t) -> o t", o=1).to_broadcast([P, NE])),
                     (wo_s, w_out.rearrange("(k p) n -> p k n", p=P)), (wq_s, w_q.rearrange("(k p) n -> p k n", p=P)),
                     (wxo_s, w_o.rearrange("(k p) n -> p k n", p=P))]
            for dst, src in small:
                act.dma_start(dst, src).then_inc(small_in, 16)
            assert 16 * len(small) == SMALL
            act.wait_ge(set_up, 1)
            halves = slots_x_d.rearrange("(j p) (c d) -> c p j d", p=P, c=2)
            for c in range(2):
                act.dma_start(halves[c], ntop[:, None, :].to_broadcast([P, TILES + 1, P])).then_inc(zeroed, 16)
            act.wait_ge(gate_in, 48)
            act.activation(gate_rows[:, 0, :], gate_rows[:, 0, :], ACT.Sigmoid).then_inc(gate_sig, 1)
            for k in range(4):
                act.wait_ge(gate_ready, k + 1)
                act.activation(gate[:, k // 2, (k % 2) * CH:(k % 2 + 1) * CH], PS[:, k, :], ACT.Copy).then_inc(gate_out, 1)

            def part1(it):
                act.wait_ge(whole_ready, it + 1)
                if it >= ITEMS:
                    act.wait_ge(parts_stored[it % ITEMS], 16 * (it // ITEMS))
                act.activation(parts[:, it % ITEMS, 0, :], whole[:, it % ITEMS, :], ACT.Copy).then_inc(part1_ready, 1)

            def part2(it):
                act.wait_ge(rest_ready, it + 1)
                act.activation(parts[:, it % ITEMS, 1, :], rest[:, it % ITEMS, :], ACT.Copy).then_inc(part2_ready, 1)

            for n in range(NCH):
                b, c = divmod(n, CPB)
                part1(4 * n)
                for it in range(4 * n + 1, 4 * n + 4):
                    part1(it)
                    part2(it - 1)
                part2(4 * n + 3)
                for v in range(2):
                    act.wait_ge(v_ready, 2 * n + v + 1)
                    for u in range(2):
                        ins = act.activation(v_all[:, NG * b:NG * (b + 1), TPC * c + 2 * v + u, :],
                                             PS[:, 4 + v, u * D:(u + 1) * D].rearrange("p (g r) -> p g r", g=NG), ACT.Copy)
                    ins.then_inc(v_taken, 1)
            act.wait_ge(v_ready, 2 * NCH)
            act.wait_ge(ctx_step, 13)
            act.dma_start(rows[:], x.rearrange("b (t p) d -> p (b t) d", p=P)).then_inc(rows_in, 16)

            def attention(A, s, probs):
                def exponentials(n):
                    for st, (c, j, q0) in enumerate(A.steps):
                        act.wait_ge(s.values_done, A.ns * n + (st + 1))
                        for hp in range(2):
                            act.wait_ge(s.scores_ready, 2 * (A.ns * n + st) + hp + 1)
                            act.activation(probs[0:A.keys, st % A.slots, 2 * hp:2 * hp + 2, q0:CH],
                                           PS[0:A.keys, 2 + 2 * hp:4 + 2 * hp, q0:CH], ACT.Exp, scale=SCALE).then_inc(s.exp_done, 1)

                with act.Fori(0, LOOPS) as i:
                    for p in range(RING):
                        exponentials(RING * i + p)
                exponentials(NN - 2)
                exponentials(NN - 1)

            def norm(g, n):
                act.wait_ge(g.var_ready, n + 1)
                act.wait_ge(g.rstd_ready, n)
                act.activation(std[:], mean_var[:, :, 1], ACT.Sqrt, bias=eps_s[:]).then_inc(g.std_ready, 1)

            def take_turned(g, n):
                for k in range(KD):
                    act.wait_ge(g.turned, KD * n + k + 1)
                    act.activation(feat_b[:, k, n * CH:(n + 1) * CH], PS[:, 4 + k, :], ACT.Copy).then_inc(g.turned_taken, 1)

            attention(SELF, ss, probs)
            for n in range(NCH + 1):
                if n < NCH:
                    norm(n1, n)
                if n:
                    take_turned(n1, n - 1)
                    it = N_ITEMS + KD * (n - 1)
                    part1(it)
                    part1(it + 1)
                    part2(it)
                    part2(it + 1)
            attention(CROSS, cs, xprobs)
            for n in range(NCH + 1):
                if n < NCH:
                    norm(n2, n)
                if n:
                    take_turned(n2, n - 1)

            act.wait_ge(logits_ready, 1)
            act.activation(scores, PS[:, 7, 0:NT * NE].rearrange("p (t e) -> p t e", e=NE), ACT.Sigmoid).then_inc(scores_done, 1)

            def shared_chunk(n):
                for h in range(FH // P):
                    act.wait_ge(hid_ready, 2 * (FH // P) * n + 2 * h + 1)
                    act.wait_ge(hid_done, (FH // P) * n + max(0, h - 1))
                    act.activation(sil[:, h % 2, :], PS[:, 2 * (h % 2), :], ACT.Silu).then_inc(sil_done, 1)
                    chunk, part = FINISH.get((n, h), (0, 0))
                    if part == TOPK + 1:
                        norm(n3, chunk)

            for n in range(NCH // 2):
                shared_chunk(n)

            def slot_turn(j, p):
                act.wait_ge(slot_turned, j + 1)
                act.activation(xs_T[:, p, :], PS[:, p, 0:KD * P], ACT.Copy).then_inc(slot_T, 1)

            def slot_silu(j, p):
                act.wait_ge(slot_hid, j + 1)
                if not (isinstance(j, int) and j < 2):
                    act.wait_ge(slot_h, j - 1)
                act.activation(xs_sil[:, p, :], PS[:, 2 + p, 0:RH], ACT.Silu).then_inc(slot_sil, 1)

            act.wait_ge(acc_taken, 4 * NCH // 2)
            slot_turn(0, 0)
            for j in range(2):
                slot_turn(j + 1, (j + 1) % 2)
                slot_silu(j, j)
            with act.Fori(1, (TILES - 1) // 2) as i:
                for p in range(2):
                    slot_turn(2 * i + p + 1, 1 - p)
                    slot_silu(2 * i + p, p)
            slot_silu(TILES - 1, 0)
            for n in range(NCH // 2, NCH):
                shared_chunk(n)
            norm(n3, NCH - 1)

        @block.tensor
        def _(pe):
            pe.wait_ge(gate_prod, 1)
            for k in range(4):
                pe.matmul(PS[:, k, :], gate_rows[:, 0, (k // 2) * P:(k // 2 + 1) * P],
                          phase_s[:, (k % 2) * CH:(k % 2 + 1) * CH], start=True, stop=True).then_inc(gate_ready, 1)
            pe.wait_ge(small_in, SMALL)
            for m in range(KD):
                for k in range(KD):
                    mm = pe.matmul(PS[:, 6, m * B * SKV:(m + 1) * B * SKV], wk_s[:, k, m * P:(m + 1) * P], ctxT_s[:, k, :],
                                   start=(k == 0), stop=(k == KD - 1))
            mm.then_inc(ctx_ready, 1)
            for b in range(B):
                for k in range(KD):
                    mm = pe.matmul(PS[0:SKV, 7, b * D:(b + 1) * D], ctxT_s[:, k, b * SKV:(b + 1) * SKV], wv_s[:, k, :],
                                   start=(k == 0), stop=(k == KD - 1))
            mm.then_inc(ctx_ready, 1)

            pe.wait_ge(wqkv_in, 16)
            pe.wait_ge(gate_out, 4)
            for n in range(NCH):
                pe.wait_ge(xT_in[n], 16)
                for m in range(4):
                    if n:
                        pe.wait_ge(whole_ready, 4 * (n - 1) + m + 1)
                    for k in range(KD):
                        mm = pe.matmul(PS[:, m, :], wqkv_s[:, k, m * P:(m + 1) * P], feat_a[:, k, n * CH:(n + 1) * CH],
                                       start=(k == 0), stop=(k == KD - 1))
                    mm.then_inc(projected, 1)
                if n:
                    pe.wait_ge(v_taken, 2 * n)
                for v in range(2):
                    for u in range(2):
                        t0 = n * CH + (2 * v + u) * P
                        for k in range(KD):
                            mm = pe.matmul(PS[:, 4 + v, u * D:(u + 1) * D], feat_a[:, k, t0:t0 + P], wqkv_s[:, k, 2 * D:3 * D],
                                           start=(k == 0), stop=(k == KD - 1))
                    mm.then_inc(v_ready, 1)

            def attention(A, s, weights):
                ring_units = A.nu + 1
                loads = sum(len(row_groups(o)) for o in (QUERY_PARTS, KEY_PARTS))

                def stack_slot(turn, p):
                    pe.wait_ge(s.stacks_in[p], 16 * loads * (turn + 1))

                def max_unit(n, p, k):
                    i, kc, h0, nh, w = A.units[k]
                    pe.wait_ge(s.unit_taken, ring_units * n + max(0, k - 1))
                    bank = PS[:, k % 2, :]
                    for a in range(nh):
                        mm = pe.matmul(bank[:, a * w:(a + 1) * w], q_st[0:A.max_rows, p, h0 + a, i * P:(i + 1) * P],
                                       k_st[0:A.max_rows, p, h0 + a, kc * CH:kc * CH + w],
                                       start=(a == 0), stop=False, skip_group_check=True)
                    if kc == i // TPC:
                        out_ = bank[:, 0:nh * w].rearrange("p (a w) -> p a w", a=nh)[:, :, w - P:w]
                        mm = pe.matmul(out_, idb[:], causal_s[:, 0:nh, :], start=False, stop=True, skip_group_check=True)
                    mm.then_inc(s.unit_ready, 1)

                def turn_tops(n):
                    pe.wait_ge(s.tops_ready, n + 1)
                    pe.transpose(PS[:, A.nu % 2, 0:P], ntop[:], idf[:]).then_inc(s.unit_ready, 1)

                def scores(n, p, st, hp):
                    c, j, q0 = A.steps[st]
                    if not (isinstance(n, int) and n == 0 and st == 0):
                        pe.wait_ge(s.exp_done, 2 * (A.ns * n + st) + hp - 1)
                    for h in (2 * hp, 2 * hp + 1):
                        if A.causal:
                            keys = k_st[0:A.exp_rows, p, h, j * P:(j + 1) * P]
                            queries = q_st[0:A.exp_rows, p, h, c * CH + q0:(c + 1) * CH]
                        else:
                            keys = xk_all[0:A.exp_rows, bass.ds(n, 1), h * SKV:(h + 1) * SKV].rearrange("p o t -> p (o t)")
                            queries = xq_all[0:A.exp_rows, bass.ds(n, 1), h * S + c * CH:h * S + (c + 1) * CH]
                            queries = queries.rearrange("p o t -> p (o t)")
                        mm = pe.matmul(PS[0:A.keys, 2 + h, q0:CH], keys, queries, start=True, stop=True)
                    mm.then_inc(s.scores_ready, 1)

                def values(n, p, st, hp):
                    c, j, q0 = A.steps[st]
                    if hp == 0:
                        pe.wait_ge(s.exp_done, 2 * (A.ns * n + st + 1))
                        if st in A.diagonal:
                            pe.wait_ge(s.masked, len(A.diagonal) * n + A.diagonal.index(st) + 1)
                        if j == 0:
                            pe.wait_ge(s.staged, n + 1)
                            pe.wait_ge(s.o_taken, CPB * n + (c + 1))
                    for h in (2 * hp, 2 * hp + 1):
                        mm = pe.matmul(PS[32 * h:32 * h + 32, 6 + c, q0:CH], v_st[0:A.keys, p, j, h, :],
                                       weights[0:A.keys, st % A.slots, h, q0:CH], start=(j == 0), stop=(st == A.last[c]),
                                       skip_group_check=True)
                    if hp == 1:
                        mm.then_inc(s.values_done, 1)

                def pair(n, i, q):
                    first, last = (isinstance(n, int) and n == e for e in (0, NN - 1))
                    p, p1 = (q + 1) % RING, (q + 2) % RING
                    if A.causal:
                        pe.wait_ge(s.top_rows_in, 48 * (n + 1))
                        if not last:
                            stack_slot(i + (q + 2) // RING, p1)

                    def units(st, quarter):
                        if not last:
                            for k in A.units_of(st, quarter):
                                max_unit(n + 1, p1, k)

                    for st in range(A.ns):
                        for hp in range(2):
                            scores(n, p, st, hp)
                            units(st, hp)
                        for hp in range(2):
                            if st >= A.lag:
                                values(n, p, st - A.lag, hp)
                            elif not first:
                                values(n - 1, q % RING, A.ns + st - A.lag, hp)
                            units(st, 2 + hp)
                        if st == A.top_step and not last:
                            turn_tops(n + 1)

                pe.sem_inc(s.values_done, A.slots)
                if A.causal:
                    stack_slot(0, 0)
                    for k in range(A.nu):
                        max_unit(0, 0, k)
                    turn_tops(0)
                pair(0, 0, -1)
                with pe.Fori(0, LOOPS) as i:
                    for q in range(RING):
                        pair(RING * i + (q + 1), i, q)
                pair(NN - 1, LOOPS, 0)
                for st in range(A.ns - A.lag, A.ns):
                    for hp in range(2):
                        values(NN - 1, (NN - 1) % RING, st, hp)

            def out_projection(g, n, w, in_sems):
                pe.wait_ge(in_sems[n], 16 * KD)
                for t in range(TPC * n, TPC * (n + 1)):
                    if t >= TPC:
                        pe.wait_ge(g.added, t - TPC + 1)
                    for k in range(KD):
                        mm = pe.matmul(PS[:, t % TPC, 0:D], feat_a[:, k, t * P:(t + 1) * P], w[:, k, :],
                                       start=(k == 0), stop=(k == KD - 1))
                    mm.then_inc(g.out_ready, 1)

            def turn(g, n):
                for k in range(KD):
                    if n:
                        pe.wait_ge(g.turned_taken, KD * (n - 1) + k + 1)
                    for u in range(TPC):
                        t = TPC * n + u
                        pe.wait_ge(g.normed, t + 1)
                        mm = pe.transpose(PS[:, 4 + k, u * P:(u + 1) * P], rows[:, t, k * P:(k + 1) * P], idf[:])
                    mm.then_inc(g.turned, 1)

            pe.wait_ge(whole_ready, N_ITEMS)
            pe.wait_ge(v_taken, 2 * NCH)
            pe.wait_ge(ctx_step, 10)
            pe.wait_ge(ident_in, 64)
            pe.wait_ge(set_up, 6)
            attention(SELF, ss, probs)

            pe.wait_ge(ss.o_taken, CPB * (NN + 1))
            for n in range(NCH + 1):
                if n < NCH:
                    out_projection(n1, n, wo_s, oT_in)
                if n:
                    turn(n1, n - 1)
                    pe.wait_ge(n1.turned_taken, KD * n)
                    for m in range(KD):
                        if n > 1:
                            pe.wait_ge(whole_ready, N_ITEMS + KD * (n - 2) + m + 1)
                        for k in range(KD):
                            mm = pe.matmul(PS[:, 6 + m, :], wq_s[:, k, m * P:(m + 1) * P], feat_b[:, k, (n - 1) * CH:n * CH],
                                           start=(k == 0), stop=(k == KD - 1))
                        mm.then_inc(projected, 1)

            pe.wait_ge(n1.added, NT)
            pe.wait_ge(whole_ready, N_ITEMS + KD * NCH)
            pe.wait_ge(xk_in, 16 * (len(KEY_PARTS) + 3 * B))
            rows_ = CROSS.max_rows
            for b in range(B):
                pe.wait_ge(xq_in[b], 16 * (len(QUERY_PARTS) + (0 if b else 1)))
                with pe.Fori(0, NG) as g:
                    for i in range(QT):
                        pe.wait_ge(cs.unit_taken, QT * g + (QT * NG * b + i + 1))
                        for h in range(GH):
                            queries = xq_all[0:rows_, bass.ds(g + NG * b, 1), h * S + i * P:h * S + (i + 1) * P]
                            keys = xk_all[0:rows_, bass.ds(g + NG * b, 1), h * SKV:(h + 1) * SKV]
                            mm = pe.matmul(PS[:, i % XBANKS, h * SKV:(h + 1) * SKV], queries.rearrange("p o t -> p (o t)"),
                                           keys.rearrange("p o t -> p (o t)"), start=True, stop=True)
                        mm.then_inc(cs.unit_ready, 1)
                pe.wait_ge(cs.tops_ready, b + 1)
                pe.transpose(PS[:, 4 + b, 0:P], ntop[:], idf[:]).then_inc(xtops_turned, 1)
            pe.wait_ge(cs.top_rows_in, 16 * 3 * B)
            attention(CROSS, cs, xprobs)

            pe.wait_ge(cs.o_taken, CPB * (NN + 1))
            for n in range(NCH + 1):
                if n < NCH:
                    out_projection(n2, n, wxo_s, oxT_in)
                if n:
                    turn(n2, n - 1)
                    pe.wait_ge(n2.turned_taken, KD * n)
                    for t in range(TPC * (n - 1), TPC * n):
                        for k in range(KD):
                            mm = pe.matmul(PS[:, 7, t * NE:(t + 1) * NE], feat_b[:, k, t * P:(t + 1) * P], router_s[:, k, :],
                                           start=(k == 0), stop=(k == KD - 1))
            mm.then_inc(logits_ready, 1)
            pe.wait_ge(n2.added, NT)

            def count_tokens():
                pe.wait_ge(scores_done, 1)
                pe.wait_ge(counted, 1)
                flat = picked.rearrange("p e t -> p (e t)")
                pe.matmul(PS[:, 7, 0:NE * NT], before_s[:], flat, start=True, stop=True)
                pe.matmul(PS[:, 7, NE * NT:2 * NE * NT], ones_s[:], flat, start=True, stop=True).then_inc(counts_ready, 1)

            count_tokens()

            def shared_chunk(n):
                hs = FH // P
                for h in range(hs + 1):
                    if h < hs:
                        pe.wait_ge(hid_done, hs * n + max(0, h - 1))
                        for w, ws in enumerate((sw1_s, sw2_s)):
                            for k in range(KD):
                                mm = pe.matmul(PS[:, 2 * (h % 2) + w, :], ws[:, k, h * P:(h + 1) * P],
                                               feat_b[:, k, bass.ds(n * CH, CH)], start=(k == 0), stop=(k == KD - 1))
                            mm.then_inc(hid_ready, 1)
                    if h:
                        pe.wait_ge(hid_done, hs * n + h)
                        if h == 1:
                            pe.wait_ge(acc_taken, TPC * n)
                        for u in range(TPC):
                            mm = pe.matmul(PS[:, 4 + u, 0:D], hidT[:, (h - 1) % 4, u * P:(u + 1) * P], sw3_s[:, h - 1, :],
                                           start=(h == 1), stop=(h == hs))
                        mm.then_inc(down_done, 1)

            pe.wait_ge(shared_w_in, 48)
            pe.wait_ge(counts_taken, 1)
            for n in range(NCH // 2):
                shared_chunk(n)

            pe.wait_ge(acc_taken, TPC * NCH // 2)
            pe.wait_ge(expert_ready, 1)
            for q in range(4):
                pe.wait_ge(routed_w_in[q], 48)

            def turn_slot(i, p):
                j = 2 * i + p
                pe.wait_ge(slot_in[p], 16 * (i + 1))
                if not (isinstance(j, int) and j < 2):
                    pe.wait_ge(slot_T, j - 1)
                for k in range(KD):
                    mm = pe.transpose(PS[:, p, k * P:(k + 1) * P], xs_in[:, p, k * P:(k + 1) * P], idf[:])
                mm.then_inc(slot_turned, 1)

            def hidden_slot(i, p, e):
                j = 2 * i + p
                pe.wait_ge(slot_T, j + 1)
                if not (isinstance(j, int) and j < 2):
                    pe.wait_ge(slot_h, j - 1)
                for k in range(KD):
                    w = w12_s[:, bass.ds(e, 1), k, :].rearrange("p o n -> p (o n)")
                    mm = pe.matmul(PS[:, 2 + p, :], xs_T[:, p, k * P:(k + 1) * P], w, start=(k == 0), stop=(k == KD - 1))
                mm.then_inc(slot_hid, 1)

            def turn_hidden(i, p):
                j = 2 * i + p
                pe.wait_ge(slot_h, j + 1)
                if not (isinstance(j, int) and j < 2):
                    pe.wait_ge(slot_hT, j - 1)
                for k in range(KD):
                    mm = pe.transpose(PS[:, 4 + p, k * P:(k + 1) * P], xs_h[:, p, k * P:(k + 1) * P], idf[:])
                mm.then_inc(slot_hturned, 1)

            def out_slot(i, p, e):
                j = 2 * i + p
                pe.wait_ge(slot_hT, j + 1)
                if not (isinstance(j, int) and j < 2):
                    pe.wait_ge(slot_y, j - 1)
                for k in range(KD):
                    w = w3_s[:, bass.ds(e, 1), k, :].rearrange("p o n -> p (o n)")
                    mm = pe.matmul(PS[:, 6 + p, 0:D], xs_hT[:, p, k * P:(k + 1) * P], w, start=(k == 0), stop=(k == KD - 1))
                mm.then_inc(slot_out, 1)

            def expert(j):
                return pe.value_load(expert_of[0:1, bass.ds(j, 1)], min_val=0, max_val=NE - 1)

            turn_slot(0, 0)
            turn_slot(0, 1)
            hidden_slot(0, 0, expert(0))
            turn_slot(1, 0)
            hidden_slot(0, 1, expert(1))
            turn_hidden(0, 0)

            def step(i, p):
                j = 2 * i + p
                turn_slot(i + p, 1 - p)
                hidden_slot(i, p, expert(j))
                out_slot(i - 1, p, expert(j - 2))
                turn_hidden(i - 1 + p, 1 - p)

            step(1, 0)
            step(1, 1)
            with pe.Fori(2, (TILES - 1) // 2) as i:
                for p in range(2):
                    step(i, p)
            i = (TILES - 1) // 2
            hidden_slot(i, 0, expert(2 * i))
            out_slot(i - 1, 0, expert(2 * i - 2))
            turn_hidden(i - 1, 1)
            out_slot(i - 1, 1, expert(2 * i - 1))
            turn_hidden(i, 0)
            out_slot(i, 0, expert(2 * i))
            pe.wait_ge(slot_y, TILES)

            with pe.Fori(NCH // 2, NCH) as n:
                shared_chunk(n)


        @block.vector
        def _(v):
            v.memset(ntop[:], 0.0).then_inc(set_up, 1)
            v.memset(tops[:], LOWEST).then_inc(set_up, 1)
            v.memset(eps_s[:], EPS).then_inc(set_up, 1)
            v.memset(k_st[STACK:STACK + 3], 1.0).then_inc(set_up, 1)
            v.memset(v_st[:], 0.0).then_inc(set_up, 1)
            v.wait_ge(set_up, 5)
            v.memset(v_st[:, :, :, :, HD:HD + 1], 1.0).then_inc(set_up, 1)
            v.memset(ones_s[:], 1.0).then_inc(ones_rows, 1)
            v.memset(xk_all[STACK:P], 1.0).then_inc(ones_rows, 1)
            v.memset(xv_all[:], 0.0).then_inc(ones_rows, 1)

            v.wait_ge(gate_sig, 1)
            v.tensor_tensor(gate_rows[:, 0, :], gate_rows[:, 0, :], gate_rows[:, 1, :], ALU.mult).then_inc(gate_prod, 1)

            v.wait_ge(small_in, SMALL)
            v.tensor_copy(mask_b, mask_u[:]).then_inc(ctx_step, 1)
            v.wait_ge(ctx_ready, 1)
            for m in range(KD):
                v.tensor_scalar(xk_whole[:, m, :], PS[:, 6, m * B * SKV:(m + 1) * B * SKV], bk_s[:, m:m + 1], None,
                                ALU.add).then_inc(ctx_step, 1)
            v.wait_ge(ctx_step, 3)
            v.tensor_tensor(xk_whole, xk_whole, mask_b[:, None, :].to_broadcast([P, KD, B * SKV]), ALU.mult).then_inc(ctx_step, 1)
            xk_part = [xk_parts[:, r, :].rearrange("p (m t) -> p m t", m=KD) for r in range(3)]
            v.wait_ge(ctx_step, 4)
            v.tensor_copy(xk_part[0], xk_whole).then_inc(ctx_step, 1)
            v.wait_ge(ctx_step, 5)
            v.tensor_tensor(xk_rest, xk_whole, xk_part[0], ALU.subtract).then_inc(ctx_step, 1)
            v.wait_ge(ctx_step, 6)
            v.tensor_copy(xk_part[1], xk_rest).then_inc(ctx_step, 1)
            v.wait_ge(ctx_step, 7)
            v.tensor_tensor(xk_part[2], xk_rest, xk_part[1], ALU.subtract).then_inc(ctx_step, 1)
            v.wait_ge(ctx_ready, 2)
            v.wait_ge(ones_rows, 3)
            for b in range(B):
                v.tensor_tensor(xv_all[0:SKV, NG * b:NG * (b + 1), :], PS[0:SKV, 7, b * D:(b + 1) * D].rearrange("p (g r) -> p g r", g=NG),
                                bv_b[0:SKV].rearrange("p (g r) -> p g r", g=NG), ALU.add).then_inc(ctx_step, 1)
            for r in range(3):
                v.tensor_scalar(fill_row[:, r, :], mask_b[0:1], -1.0, FILL_PARTS[r], ALU.add, ALU.mult).then_inc(ctx_step, 1)

            def take_whole(it, make):
                r = it % ITEMS
                v.wait_ge(projected, it + 1)
                if it >= ITEMS:
                    v.wait_ge(part1_ready, it - ITEMS + 1)
                    v.wait_ge(rest_ready, it - ITEMS + 1)
                make(whole[:, r, :]).then_inc(whole_ready, 1)

            def take_rest(it):
                r = it % ITEMS
                v.wait_ge(part1_ready, it + 1)
                if it >= ITEMS:
                    v.wait_ge(part3_ready, it - ITEMS + 1)
                v.tensor_tensor(rest[:, r, :], whole[:, r, :], parts[:, r, 0, :], ALU.subtract).then_inc(rest_ready, 1)

            def gated(m, c):
                return lambda dst: v.tensor_tensor(dst, PS[:, m, :], gate[:, m, c * CH:(c + 1) * CH], ALU.mult)

            def copied(m):
                return lambda dst: v.tensor_copy(dst, PS[:, m, :])

            def biased(m):
                return lambda dst: v.tensor_scalar(dst, PS[:, 6 + m, :], bq_s[:, m:m + 1], None, ALU.add)

            def split(first, makes):
                take_whole(first, makes[0])
                for k, make in enumerate(makes[1:]):
                    take_whole(first + k + 1, make)
                    take_rest(first + k)
                take_rest(first + len(makes) - 1)

            v.wait_ge(gate_out, 4)
            for n in range(NCH):
                split(4 * n, [gated(0, n % CPB), gated(1, n % CPB), copied(2), copied(3)])

            def attention(A, s):
                ring_units = A.nu + 1

                def take_unit(n, k):
                    i, kc, h0, nh, w = A.units[k]
                    v.wait_ge(s.unit_ready, ring_units * n + k + 1)
                    v.tensor_reduce(tops[:, h0:h0 + nh, i, kc], PS[:, k % 2, 0:nh * w].rearrange("p (a w) -> p a w", a=nh),
                                    AX.X, ALU.max).then_inc(s.unit_taken, 1)

                def fold_tops(n):
                    v.wait_ge(s.unit_taken, ring_units * n + A.nu)
                    v.wait_ge(s.unit_ready, ring_units * n)
                    v.tensor_reduce(ntop[:, 0:GH * QT], tops[:].rearrange("p h i c -> p (h i) c"), AX.X, ALU.max,
                                    negate=True).then_inc(s.tops_ready, 1)

                def split_tops(n):
                    v.wait_ge(s.unit_ready, ring_units * (n + 1))
                    v.wait_ge(s.top_rows_in, 48 * n)
                    src = PS[0:GH * QT, A.nu % 2, 0:P]
                    v.tensor_copy(ntop_p[0:GH * QT, 0, :], src).then_inc(s.top_split, 1)
                    v.wait_ge(s.top_split, 3 * n + 1)
                    v.tensor_tensor(ntop_r[0:GH * QT], src, ntop_p[0:GH * QT, 0, :], ALU.subtract).then_inc(s.unit_taken, 1)
                    v.wait_ge(s.unit_taken, ring_units * (n + 1))
                    v.tensor_copy(ntop_p[0:GH * QT, 1, :], ntop_r[0:GH * QT]).then_inc(s.top_split, 1)
                    v.wait_ge(s.top_split, 3 * n + 2)
                    v.tensor_tensor(ntop_p[0:GH * QT, 2, :], ntop_r[0:GH * QT], ntop_p[0:GH * QT, 1, :], ALU.subtract).then_inc(s.top_split, 1)

                def take_output(n, c):
                    v.wait_ge(s.values_done, A.slots + A.ns * n + A.last[c] + 1)
                    v.wait_ge(s.o_ready, CPB * n + (c + 1))
                    v.transpose(o_blk[:, c, :], PS[:, 6 + c, :]).then_inc(s.o_taken, 1)
                    v.wait_ge(s.o_taken, CPB * (n + 1) + c + 1)
                    v.reciprocal(o_rec[:, c, :], o_blk[:, c, HD:CH:32]).then_inc(s.rec_ready, 1)

                def give_output(n, c):
                    v.wait_ge(s.o_scaled, CPB * n + c + 1)
                    v.wait_ge(s.o_stored[c], 16 * (n + 1))
                    v.transpose(o_nrm[:, c, :], o_blk[:, c, :]).then_inc(s.o_ready, 1)

                def pair(n):
                    first, last = (isinstance(n, int) and n == e for e in (0, NN - 1))
                    for st in range(A.ns):
                        if not last:
                            for quarter in range(4):
                                for k in A.units_of(st, quarter):
                                    take_unit(n + 1, k)
                            if st == A.unit_steps - 1:
                                fold_tops(n + 1)
                        for back, c in A.output_at(st, A.take_lag):
                            if not (first and back):
                                take_output(n - back, c)
                        for back, c in A.output_at(st, A.take_lag + 1):
                            if not (first and back):
                                give_output(n - back, c)
                        if st == A.top_step and not last:
                            split_tops(n + 1)

                v.sem_inc(s.o_taken, CPB)
                v.sem_inc(s.o_ready, CPB)
                if A.causal:
                    for k in range(A.nu):
                        take_unit(0, k)
                    fold_tops(0)
                    split_tops(0)
                pair(0)
                with v.Fori(0, LOOPS) as i:
                    for q in range(RING):
                        pair(RING * i + (q + 1))
                pair(NN - 1)
                if not A.causal:
                    give_output(NN - 1, 0)
                take_output(NN - 1, 1)
                give_output(NN - 1, 1)

            def moments(g, n):
                for u in range(TPC):
                    v.wait_ge(g.added, TPC * n + u + 1)
                    v.bn_stats(stats[:, u, :], rows[:, TPC * n + u, :]).then_inc(g.stat_step, 1)
                for u in range(TPC):
                    v.wait_ge(g.stat_step, 2 * TPC * n + u + 1)
                    v.bn_aggr(mean_var[:, u, :], stats[:, u, :]).then_inc(g.stat_step, 1)
                v.wait_ge(g.stat_step, 2 * TPC * (n + 1))
                v.sem_inc(g.var_ready, 1)

            def add_block(g, n):
                for u in range(TPC):
                    t = TPC * n + u
                    v.wait_ge(g.out_ready, t + 1)
                    v.tensor_tensor(rows[:, t, :], PS[:, u, 0:D], rows[:, t, :], ALU.add).then_inc(g.added, 1)
                moments(g, n)

            def normalise(g, n):
                v.wait_ge(g.std_ready, n + 1)
                v.reciprocal(rstd[:], std[:]).then_inc(g.rstd_ready, 1)
                v.wait_ge(g.rstd_ready, n + 1)
                for u in range(TPC):
                    t = TPC * n + u
                    v.tensor_scalar(rows[:, t, :], rows[:, t, :], mean_var[:, u, 0:1], rstd[:, u:u + 1],
                                    ALU.subtract, ALU.mult).then_inc(g.normed, 1)

            v.wait_ge(set_up, 6)
            v.wait_ge(zeroed, 32)
            attention(SELF, ss)

            v.wait_ge(rows_in, 16)
            for n in range(NCH + 1):
                if n < NCH:
                    add_block(n1, n)
                if n:
                    split(N_ITEMS + KD * (n - 1), [biased(m) for m in range(KD)])
                if n < NCH:
                    normalise(n1, n)

            v.sem_inc(cs.unit_taken, XBANKS)
            for b in range(B):
                with v.Fori(0, NG) as g:
                    for i in range(QT):
                        v.wait_ge(cs.unit_ready, QT * g + (QT * NG * b + i + 1))
                        v.sem_inc(vector_turn, 1)
                        cols = ntop[:, bass.ds(g * (GH * QT), GH * QT)].rearrange("p (h i) -> p h i", h=GH)[:, :, i]
                        v.tensor_reduce(cols, PS[:, i % XBANKS, 0:GH * SKV].rearrange("p (h w) -> p h w", h=GH),
                                        AX.X, ALU.max, negate=True).then_inc(cs.unit_taken, 1)
                v.wait_ge(cs.unit_taken, XBANKS + QT * NG * (b + 1))
                v.sem_inc(cs.tops_ready, 1)
                v.wait_ge(xtops_turned, b + 1)
                v.wait_ge(cs.top_rows_in, 48 * b)
                src = PS[:, 4 + b, 0:P]
                v.tensor_copy(ntop_p[:, 0, :], src).then_inc(cs.top_split, 1)
                v.wait_ge(cs.top_split, 3 * b + 1)
                v.tensor_tensor(ntop_r, src, ntop_p[:, 0, :], ALU.subtract).then_inc(xtop_rest, 1)
                v.wait_ge(xtop_rest, b + 1)
                v.tensor_copy(ntop_p[:, 1, :], ntop_r).then_inc(cs.top_split, 1)
                v.wait_ge(cs.top_split, 3 * b + 2)
                v.tensor_tensor(ntop_p[:, 2, :], ntop_r, ntop_p[:, 1, :], ALU.subtract).then_inc(cs.top_split, 1)
            attention(CROSS, cs)

            for n in range(NCH):
                v.wait_ge(bias_added, n + 1)
                add_block(n2, n)
                normalise(n2, n)

            steps = 0

            def routed():
                v.wait_ge(route_step, steps)

            def by_token(a):
                return a.rearrange("p e t -> p t e")

            v.memset(experts[:, 3, :], 1.0).then_inc(route_step, 1)
            v.memset(scan_keep, 1.0).then_inc(route_step, 1)
            v.wait_ge(route_step, 2)
            v.memset(scan_keep[:, :, 0:1], 0.0).then_inc(route_step, 1)
            v.wait_ge(iota_ready, 2)
            v.tensor_scalar(rev_e, iota_e[:], -1.0, float(NE), ALU.mult, ALU.add).then_inc(route_step, 1)
            v.wait_ge(scores_done, 1)
            v.tensor_tensor(select, scores, ebias_b[:, None, :].to_broadcast([P, NT, NE]), ALU.add).then_inc(route_step, 1)
            steps += 5
            for k in range(TOPK):
                routed()
                v.tensor_reduce(best[:, k, 0, :], select, AX.X, ALU.max).then_inc(route_step, 1)
                steps += 1
                routed()
                v.tensor_tensor(by_token(work), select, best[:, k, 0, :, None].to_broadcast([P, NT, NE]),
                                ALU.is_equal).then_inc(route_step, 1)
                steps += 1
                routed()
                v.tensor_tensor(by_token(work), by_token(work), rev_e[:, None, :].to_broadcast([P, NT, NE]),
                                ALU.mult).then_inc(route_step, 1)
                steps += 1
                routed()
                v.tensor_reduce(best[:, k, 1, :], by_token(work), AX.X, ALU.max).then_inc(route_step, 1)
                steps += 1
                routed()
                v.tensor_tensor(by_token(onehot[:, k]), rev_e[:, None, :].to_broadcast([P, NT, NE]),
                                best[:, k, 1, :, None].to_broadcast([P, NT, NE]), ALU.is_equal).then_inc(route_step, 1)
                steps += 1
                if k == 0:
                    routed()
                    v.scalar_tensor_tensor(select, by_token(onehot[:, k]), LOWEST, select, ALU.mult, ALU.add).then_inc(route_step, 1)
                    steps += 1
            routed()
            v.tensor_tensor(picked, onehot[:, 0], onehot[:, 1], ALU.add).then_inc(counted, 1)
            for k in range(TOPK):
                v.tensor_tensor(by_token(work), by_token(onehot[:, k]), scores, ALU.mult).then_inc(route_step, 1)
                steps += 1
                routed()
                v.tensor_reduce(gates[:, k, :], by_token(work), AX.X, ALU.add).then_inc(route_step, 1)
                steps += 1
                routed()

            v.wait_ge(counts_ready, 1)
            before_n = PS[:, 7, 0:NE * NT].rearrange("p (e t) -> p e t", e=NE)
            in_tile = PS[:, 7, NE * NT:2 * NE * NT].rearrange("p (e t) -> p e t", e=NE)
            v.tensor_tensor_scan(work.rearrange("p e t -> p (e t)"), scan_keep.rearrange("p e t -> p (e t)"),
                                 PS[:, 7, NE * NT:2 * NE * NT], 0.0, ALU.mult, ALU.add).then_inc(route_step, 1)
            steps += 1
            routed()
            v.tensor_scalar(tiles_i[:], work[:, :, NT - 1], float(P - 1), None, ALU.add).then_inc(route_step, 1)
            steps += 1
            routed()
            v.tensor_single_scalar(tiles_i[:], tiles_i[:], P.bit_length() - 1, ALU.arith_shift_right).then_inc(route_step, 1)
            steps += 1
            routed()
            v.tensor_copy(experts[:, 0, :], tiles_i[:]).then_inc(route_step, 1)
            steps += 1
            routed()
            v.tensor_tensor_scan(experts[:, 1, :], experts[:, 3, :], experts[:, 0, :], 0.0, ALU.mult, ALU.add).then_inc(route_step, 1)
            steps += 1
            routed()
            v.tensor_tensor(experts[:, 2, :], experts[:, 1, :], experts[:, 0, :], ALU.subtract).then_inc(route_step, 1)
            v.tensor_tensor(work, work, in_tile, ALU.subtract).then_inc(route_step, 1)
            steps += 2
            routed()
            v.tensor_tensor(work, work, before_n, ALU.add).then_inc(route_step, 1)
            steps += 1
            routed()
            v.sem_inc(counts_taken, 1)
            v.scalar_tensor_tensor(work, experts[:, 2, :, None].to_broadcast([P, NE, NT]), float(P), work,
                                   ALU.mult, ALU.add).then_inc(route_step, 1)
            steps += 1
            for k in range(TOPK):
                routed()
                v.tensor_tensor(picked, onehot[:, k], work, ALU.mult).then_inc(route_step, 1)
                steps += 1
                routed()
                v.tensor_reduce(slots_f[:, k, :], by_token(picked), AX.X, ALU.add).then_inc(route_step, 1)
                steps += 1
            routed()
            v.tensor_copy(slots_u[:], slots_f).then_inc(slots_ready, 1)
            ended = xs_out[0:1].rearrange("p r n -> p (r n)")[:, 0:48 * NE].rearrange("p (j e) -> p j e", e=NE)
            v.tensor_tensor(ended, iota_t[:, :, None].to_broadcast([1, 48, NE]),
                            experts[0:1, 1, None, :].to_broadcast([1, 48, NE]), ALU.is_ge).then_inc(route_step, 1)
            steps += 1
            routed()
            v.tensor_reduce(tile_work, ended, AX.X, ALU.add).then_inc(route_step, 1)
            steps += 1
            routed()
            v.tensor_scalar(expert_of[:], tile_work, float(NE - 1), None, ALU.min).then_inc(expert_ready, 1)

            def shared_chunk(n, between=lambda h: None):
                hs = FH // P
                for h in range(hs):
                    v.wait_ge(hid_ready, 2 * hs * n + 2 * h + 2)
                    v.wait_ge(sil_done, hs * n + h + 1)
                    v.wait_ge(down_done, hs * n + max(0, h - 3))
                    v.tensor_tensor(hidT[:, h % 4, :], sil[:, h % 2, :], PS[:, 2 * (h % 2) + 1, :], ALU.mult).then_inc(hid_done, 1)
                    between(h)
                v.wait_ge(down_done, hs * (n + 1))
                v.sem_inc(vector_turn, 1)
                for u in range(TPC):
                    dst = shared[:, bass.ds(TPC * n + u, 1), :].rearrange("p o d -> p (o d)")
                    v.tensor_copy(dst, PS[:, 4 + u, 0:D]).then_inc(acc_taken, 1)

            for n in range(NCH // 2):
                shared_chunk(n)

            def multiply(i, p):
                j = 2 * i + p
                v.wait_ge(slot_sil, j + 1)
                if not (isinstance(j, int) and j < 2):
                    v.wait_ge(slot_hturned, j - 1)
                v.tensor_tensor(xs_h[:, p, :], xs_sil[:, p, :], PS[:, 2 + p, RH:2 * RH], ALU.mult).then_inc(slot_h, 1)

            def take_hidden(i, p):
                v.wait_ge(slot_hturned, 2 * i + p + 1)
                v.tensor_copy(xs_hT[:, p, :], PS[:, 4 + p, 0:KD * P]).then_inc(slot_hT, 1)

            def take_slot(i, p):
                v.wait_ge(slot_out, 2 * i + p + 1)
                v.wait_ge(slot_stored[p], 16 * i)
                v.tensor_copy(xs_y[:, p, :], PS[:, 6 + p, 0:D]).then_inc(slot_y, 1)

            multiply(0, 0)
            multiply(0, 1)
            take_hidden(0, 0)

            def step(i, p):
                multiply(i, p)
                take_slot(i - 1, p)
                take_hidden(i - 1 + p, 1 - p)

            step(1, 0)
            step(1, 1)
            with v.Fori(2, (TILES - 1) // 2) as i:
                for p in range(2):
                    step(i, p)
            i = (TILES - 1) // 2
            multiply(i, 0)
            take_slot(i - 1, 0)
            take_hidden(i - 1, 1)
            take_slot(i - 1, 1)
            take_hidden(i, 0)
            take_slot(i, 0)

            def finish(n, part):
                tiles = range(TPC * n, TPC * (n + 1))
                if part == 0:
                    v.wait_ge(acc_taken, TPC * (n + 1))
                    chunk = rows[:, TPC * n:TPC * (n + 1), :]
                    v.tensor_tensor(chunk, chunk, shared[:, TPC * n:TPC * (n + 1), :], ALU.add).then_inc(final_step, 1)
                    v.wait_ge(gathered_in[n], 16 * TOPK * TPC)
                if part < TOPK:
                    v.wait_ge(final_step, (TPC + 1) * n + 1 + TPC * part)
                    for t in tiles:
                        v.scalar_tensor_tensor(rows[:, t, :], gathered[:, t, part, :], gates[:, part, t:t + 1], rows[:, t, :],
                                               ALU.mult, ALU.add).then_inc(n3.added if part else final_step, 1)
                elif part == TOPK:
                    moments(n3, n)
                else:
                    normalise(n3, n)

            for n in range(NCH // 2, NCH):
                shared_chunk(n, lambda h: finish(*FINISH[n, h]) if (n, h) in FINISH else None)
            for part in range(TOPK + 2):
                finish(NCH - 1, part)


_HEADS = D // HD


def _columns():
    return np.array([GH * HD * g + HD * h + d for g in range(NG) for d in range(HD) for h in range(GH)])


def _gate_rows(values):
    raw = np.zeros((P, D), values.dtype)
    pick = np.zeros((P, D), np.float32)
    row = 0
    for c, cycle in enumerate(TALA_CYCLES):
        for r in range(cycle):
            for h in range(c, _HEADS, len(TALA_CYCLES)):
                raw[row, HD * h:HD * (h + 1)] = values[h, r]
                pick[row, HD * h:HD * (h + 1)] = 1
            row += 1
    cols = _columns()
    return raw[:, cols], pick[:, cols]


def _phase_rows():
    rows = np.zeros((P, S), np.float32)
    row = 0
    for cycle in TALA_CYCLES:
        for r in range(cycle):
            rows[row, r::cycle] = 1
            row += 1
    return rows


def _operands(inputs):
    g = {k: np.asarray(v) for k, v in inputs.items()}
    cols = _columns()
    w_qkv = g["L0_attn_w_qkv"]
    raw, pick = _gate_rows(g["L0_attn_bandha_gate"])
    key, query = np.arange(P)[None, :], np.arange(P)[:, None]
    causal = np.where(key <= query, 0, bf16_bits(LATER_KEY)).astype(np.uint16)
    ops = {
        "x": g["x"], "xT": g["x"].reshape(TOK, D).T, "ctxT": g["ctx_1024"].reshape(B * SKV, D).T,
        "mask": g["mask_BxS2_bf1"].view(np.uint8),
        "w_qkv": np.concatenate([w_qkv[:, 0:D][:, cols], w_qkv[:, D:2 * D][:, cols], w_qkv[:, 2 * D:]], axis=1),
        "gate_raw": raw, "gate_pick": pick, "phase": _phase_rows(), "w_out": g["L0_attn_w_out"],
        "w_q": g["L0_xattn_Wq"].T[:, cols], "b_q": g["L0_xattn_bq"][cols].reshape(KD, P).T,
        "w_k": g["L0_xattn_Wk"].T[:, cols], "b_k": g["L0_xattn_bk"][cols].reshape(KD, P).T,
        "w_v": g["L0_xattn_Wv"].T, "b_v": g["L0_xattn_bv"], "w_o": g["L0_xattn_Wo"].T, "b_o": g["L0_xattn_bo"],
        "router_w": g["L0_ffn_router_w"], "expert_bias": g["L0_ffn_expert_bias"],
        "sw1": g["L0_ffn_shared_w1"][0], "sw2": g["L0_ffn_shared_w2"][0], "sw3": g["L0_ffn_shared_w3"][0],
        "rw1": g["L0_ffn_routed_w1"], "rw2": g["L0_ffn_routed_w2"], "rw3": g["L0_ffn_routed_w3"],
        "ident_f": np.eye(P, dtype=np.float32), "ident_b": np.eye(P, dtype=np.uint16) * np.uint16(bf16_bits(1.0)),
        "causal": np.broadcast_to(causal[:, None, :], (P, GH, P)),
        "before": (np.arange(P)[:, None] < np.arange(P)[None, :]).astype(np.float32),
        "ones": np.full(GH * S, bf16_bits(1.0), np.uint16),
    }
    return {k: np.ascontiguousarray(v) for k, v in ops.items()}


def kernel(**inputs):
    import concourse.bacc as bacc
    from concourse import mybir as mb
    from concourse.bass_utils import run_bass_kernel_spmd

    nc = bacc.Bacc("TRN2", target_bir_lowering=False, num_devices=1)
    arrays, args = {}, []
    for name, a in _operands(inputs).items():
        arrays[f"in_{name}_dram"] = a
        args.append(nc.dram_tensor(f"in_{name}_dram", a.shape, mb.dt.from_np(a.dtype), kind="ExternalInput").ap())
    args.append(nc.dram_tensor("out_dram", (B, S, D), mb.dt.float32, kind="ExternalOutput").ap())
    decoder_layer(nc, *args)
    result = run_bass_kernel_spmd(nc, [arrays], core_ids=[0])
    return result.results[0]["out_dram"]
```

```python
from contextlib import ExitStack

import numpy as np

import concourse.bass as bass
from concourse import mybir

ALU = mybir.AluOpType
ACT = mybir.ActivationFunctionType
AX = mybir.AxisListType
F32 = mybir.dt.float32
BF16 = mybir.dt.bfloat16
I32 = mybir.dt.int32
U32 = mybir.dt.uint32
U16 = mybir.dt.uint16
U8 = mybir.dt.uint8

P = 128
B, S, D = 2, 1024, 256
TOK = B * S
HD = 16
SKV = 77
KD = D // P
CH = 512
NCH = TOK // CH
CPB = S // CH
GH = 4
NG = D // HD // GH
NN = B * NG
QT = S // P
TPC = CH // P
NT = TOK // P
FH = 1024
NE, RH, TOPK = 16, 256, 2
TILES = (TOPK * TOK + NE * (P - 1)) // P
assert (TILES + 1) % NN == 0
EPS = 1e-5
SCALE = float(HD) ** -0.5
MASK_FILL = 1e8
LOWEST = -3e38
LATER_KEY = -1e30
RING = 3
UNIT_STEP = 400
ITEMS = 3
QUERY_PARTS = (0, 0, 0, 1, 1, 2)
KEY_PARTS = (0, 1, 2, 0, 1, 0)
STACK = len(QUERY_PARTS) * HD
SMALL = 16 * 13
TALA_CYCLES = (5, 6, 7, 8)


def row_groups(parts):
    runs, r = [], 0
    while r < len(parts):
        n = 1
        step = 0 if r + 1 < len(parts) and parts[r + 1] == parts[r] else 1
        while r + n < len(parts) and parts[r + n] == parts[r] + step * n:
            n += 1
        runs.append((r, r + n, parts[r], 1 if step == 0 else n, n if step == 0 else 1))
        r += n
    return runs


def bf16_bits(x):
    bits = int(np.float32(x).view(np.uint32))
    return (bits + 0x7FFF + ((bits >> 16) & 1)) >> 16


def bf16_round(x):
    return float(np.uint32(bf16_bits(x) << 16).view(np.float32))


def bf16_parts(x):
    out = []
    for _ in range(3):
        out.append(bf16_round(x))
        x -= out[-1]
    assert x == 0
    return out


FILL_PARTS = bf16_parts(MASK_FILL / SCALE)


class Attention:

    def __init__(self, causal):
        self.causal = causal
        self.keys = P if causal else SKV
        if causal:
            self.units = []
            for i in range(QT):
                for kc in range(i // TPC + 1):
                    w = min(CH, (i + 1) * P - CH * kc)
                    per = CH // w
                    self.units += [(i, kc, h0, per, w) for h0 in range(0, GH, per)]
            order = ((0, 3, 1, 2), (0, 7, 6, 5, 4, 1, 2, 3))
            self.steps = [(c, j, max(0, j - TPC * c) * P) for c in range(CPB) for j in order[c]]
            self.unit_steps, self.top_step, self.next_step = 8, 8, 9
            self.extra = 0
            self.slots, self.lag, self.take_lag = 4, 2, 3
        else:
            self.units = []
            self.steps = [(c, 0, 0) for c in range(CPB)]
            self.unit_steps, self.top_step, self.next_step = 0, -1, len(self.steps)
            self.slots, self.lag, self.take_lag = 2, 1, 1
            self.extra = 3
        self.nu, self.ns = len(self.units), len(self.steps)
        self.last = [max(s for s, e in enumerate(self.steps) if e[0] == c) for c in range(CPB)]
        self.diagonal = [s for s, (c, j, _) in enumerate(self.steps) if causal and j >= TPC * c]
        self.top_row = STACK + self.extra
        self.max_rows, self.exp_rows = STACK + self.extra, STACK + self.extra + 3

    def units_of(self, s, quarter, first):
        order = list(range(self.unit_steps))
        if not first:
            order = list(range(self.next_step, self.ns)) + order
        if s not in order:
            return range(0)
        cost = [CH - self.steps[e][2] + UNIT_STEP for e in order]
        e = order.index(s)
        at = sum(cost[:e]) * 4 + cost[e] * quarter
        return range(self.nu * at // (4 * sum(cost)), self.nu * (at + cost[e]) // (4 * sum(cost)))

    def output_at(self, s, lag):
        return [(back, c) for back in (1, 0) for c in range(CPB) if self.last[c] + lag == s + self.ns * back]


FINISH = {(NCH - 2, 4 + part): (0, part) for part in range(TOPK + 2)}
FINISH.update({(NCH - 1, 4 * n + part): (1 + n, part) for n in range(2) for part in range(TOPK + 2)})

SELF, CROSS = Attention(True), Attention(False)


def decoder_layer(nc, x, xT, ctxT, mask, w_qkv, gate_raw, gate_pick, phase, w_out, w_q, b_q, w_k, b_k, w_v, b_v,
                  w_o, b_o, router_w, expert_bias, sw1, sw2, sw3, rw1, rw2, rw3,
                  ident_f, ident_b, causal, before, ones, out):
    q_parts_d = nc.dram_tensor("q_parts_d", [3, NN, GH * HD, S], BF16, kind="Internal").ap()
    k_parts_d = nc.dram_tensor("k_parts_d", [3, NN, GH * HD, S], BF16, kind="Internal").ap()
    xq_parts_d = nc.dram_tensor("xq_parts_d", [3, NN, GH * HD, S], BF16, kind="Internal").ap()
    xk_parts_d = nc.dram_tensor("xk_parts_d", [3, NN, GH * HD, SKV], BF16, kind="Internal").ap()
    o_self_d = nc.dram_tensor("o_self_d", [NN, P, S], F32, kind="Internal").ap()
    o_cross_d = nc.dram_tensor("o_cross_d", [NN, P, S], F32, kind="Internal").ap()
    slots_x_d = nc.dram_tensor("slots_x_d", [(TILES + 1) * P, D], F32, kind="Internal").ap()
    slots_y_d = nc.dram_tensor("slots_y_d", [TILES * P, D], F32, kind="Internal").ap()

    ctx = ExitStack()
    with ctx:
        def sb(name, shape, dt=F32):
            return ctx.enter_context(nc.sbuf_tensor(name, shape, dt))

        def sem(name):
            return ctx.enter_context(nc.semaphore(name))

        def sems(name, n):
            return [sem(f"{name}{i}") for i in range(n)]

        PS = ctx.enter_context(nc.psum_tensor("PS", [P, 8, CH], F32))

        feat_a = sb("feat_a", [P, KD, TOK])
        feat_b = sb("feat_b", [P, KD, TOK])
        rows = sb("rows", [P, NT, D])
        region_r = sb("region_r", [P, 24576])
        region_s = sb("region_s", [P, 6144])
        region_m = sb("region_m", [P, 6144])
        region_w = sb("region_w", [P, 2560])
        used = {}

        def carve(region, key, shape, dt=F32, parts=P):
            words = int(np.prod(shape)) * (2 if dt == BF16 else 4) // 4
            at = used.get(key, 0)
            used[key] = at + words
            assert at + words <= region.shape[1], (key, at + words)
            flat = region[0:parts, at:at + words]
            if dt != F32:
                flat = flat.bitcast(dt)
            names = "abcde"[:len(shape)]
            if len(shape) == 1:
                return flat
            return flat.rearrange(f"p ({' '.join(names)}) -> p {' '.join(names)}",
                                  **{n: s for n, s in zip(names[1:], shape[1:])})

        rows_flat = rows[:].rearrange("p t d -> p (t d)")
        wqkv_s = carve(rows_flat, "rows", [KD, 3 * D])
        gate_rows = carve(rows_flat, "rows", [2, D])
        phase_s = carve(rows_flat, "rows", [S])
        mask_b = carve(rows_flat, "rows", [B * SKV])
        xk_rest = carve(rows_flat, "rows", [KD, B * SKV])
        bv_b = carve(rows_flat, "rows", [D])
        v_st = carve(region_r, "r", [RING, QT, GH, 32])
        xk_parts = carve(region_r, "r", [3, KD * B * SKV], BF16)
        bo_b = carve(region_r, "r", [D])
        ntop_p = carve(region_r, "r", [3, P], BF16)
        used["rx"] = used["r"]
        q_st = carve(region_r, "r", [RING, GH, S], BF16)
        k_st = carve(region_r, "r", [RING, GH, S], BF16)
        probs = carve(region_r, "r", [SELF.slots, GH, CH])
        stacks_at, probs_at = used["rx"], used["r"] - SELF.slots * GH * CH
        xq_all = carve(region_r, "rx", [NN, GH * S], BF16)
        xprobs = carve(region_r, "rx", [CROSS.slots, GH, CH])
        gate = carve(region_s, "s", [KD, S])
        o_blk = carve(region_s, "s", [CPB, CH])
        o_nrm = carve(region_s, "s", [CPB, CH])
        o_rec = carve(region_s, "s", [CPB, CH // 32])
        xk_all = carve(region_s, "s", [NN, GH * SKV], BF16)
        xv_all = carve(region_s, "s", [NN, GH * HD])
        fill_row = carve(region_s, "s", [3, B * SKV], BF16, parts=1)
        v_all = feat_b[:].rearrange("p k t -> p (k t)").rearrange("p (n t r) -> p n t r", n=NN, t=QT)
        whole = carve(region_m, "m", [ITEMS, CH])
        rest = carve(region_m, "m", [ITEMS, CH])
        parts = carve(region_m, "m", [ITEMS, 3, CH], BF16)
        ctxT_s = carve(region_m, "m", [KD, B * SKV])
        xk_whole = carve(region_m, "m", [KD, B * SKV])
        ntop_r = carve(region_m, "m", [P])
        wo_s = carve(region_w, "w", [KD, D])
        wq_s = carve(region_w, "w", [KD, D])
        wk_s = carve(region_w, "w", [KD, D])
        wv_s = carve(region_w, "w", [KD, D])
        wxo_s = carve(region_w, "w", [KD, D])
        w12_s = region_r[:, 0:NE * KD * 2 * RH].rearrange("p (e k n) -> p e k n", e=NE, k=KD)
        w3_s = region_r[:, NE * KD * 2 * RH:].rearrange("p (e k n) -> p e k n", e=NE, k=KD)
        gathered = region_r[:, 0:NT * TOPK * D].rearrange("p (t k d) -> p t k d", t=NT, k=TOPK)
        sw1_s = region_s[:, 0:KD * FH].rearrange("p (k n) -> p k n", k=KD)
        sw2_s = region_s[:, KD * FH:2 * KD * FH].rearrange("p (k n) -> p k n", k=KD)
        sw3_s = region_s[:, 2 * KD * FH:].rearrange("p (k n) -> p k n", n=D)
        shared = feat_a[:].rearrange("p k t -> p (k t)").rearrange("p (t d) -> p t d", d=D)
        hidT = carve(region_w, "w2", [4, CH])
        sil = carve(region_m, "m2", [2, CH])
        scores = carve(region_m, "m2", [NT, NE])
        select = carve(region_m, "m2", [NT, NE])
        best = carve(region_m, "m2", [TOPK, 2, NT])
        onehot = carve(region_m, "m2", [TOPK, NE, NT])
        picked = carve(region_m, "m2", [NE, NT])
        work = carve(region_m, "m2", [NE, NT])
        scan_keep = carve(region_m, "m2", [NE, NT])
        rev_e = carve(region_m, "m2", [NE])
        experts = carve(region_m, "m2", [4, NE])
        slots_f = carve(region_m, "m2", [TOPK, NT])
        tile_work = carve(region_m, "m2", [48], parts=1)
        xs_in = carve(region_m, "m2", [2, D])
        xs_T = carve(region_m, "m2", [2, KD * P])
        xs_sil = carve(region_m, "m2", [2, RH])
        xs_h = carve(region_m, "m2", [2, RH])
        xs_out = carve(region_m, "m2", [4, KD * P])
        xs_hT, xs_y = xs_out[:, 0:2, :], xs_out[:, 2:4, :]

        idf = sb("idf", [P, P])
        idb = sb("idb", [P, P], BF16)
        causal_s = sb("causal_s", [P, GH, P], BF16)
        before_s = sb("before_s", [P, P])
        ones_s = sb("ones_s", [P, P])
        tops = sb("tops", [P, GH, QT, 2])
        ntop = sb("ntop", [P, P])
        stats = sb("stats", [P, TPC, 6])
        mean_var = sb("mean_var", [P, 2, TPC, 2])
        std = sb("std", [P, 2, TPC])
        rstd = sb("rstd", [P, 2, TPC])
        bq_s = sb("bq_s", [P, KD])
        bk_s = sb("bk_s", [P, KD])
        router_s = sb("router_s", [P, KD, NE])
        ebias_b = sb("ebias_b", [P, NE])
        mask_u = sb("mask_u", [P, B * SKV], U8)
        eps_s = sb("eps_s", [P, 1])
        gates = sb("gates", [P, TOPK, NT])
        slots_u = sb("slots_u", [P, TOPK, NT], U32)
        tiles_i = sb("tiles_i", [P, NE], I32)
        expert_of = sb("expert_of", [1, 48], I32)
        iota_e = sb("iota_e", [P, NE])
        iota_t = sb("iota_t", [1, 48])

        gate_in, wqkv_in, small_in, ident_in, cross_w_in, rows_in = map(sem, (
            "gate_in", "wqkv_in", "small_in", "ident_in", "cross_w_in", "rows_in"))
        xT_in, oT_in, oxT_in = sems("xT_in", NCH), sems("oT_in", NCH), sems("oxT_in", NCH)
        xk_stored, xk_in, ones_rows, zeroed = map(sem, ("xk_stored", "xk_in", "ones_rows", "zeroed"))
        shared_w_in, routed_w_in = sem("shared_w_in"), sems("routed_w_in", 4)
        gate_sig, gate_prod, gate_ready, gate_out = map(sem, ("gate_sig", "gate_prod", "gate_ready", "gate_out"))
        ctx_ready, ctx_step, v_ready, v_taken = map(sem, ("ctx_ready", "ctx_step", "v_ready", "v_taken"))
        projected, whole_ready, part1_ready, rest_ready, part2_ready, part3_ready = map(sem, (
            "projected", "whole_ready", "part1_ready", "rest_ready", "part2_ready", "part3_ready"))
        parts_stored = sems("parts_stored", ITEMS)
        set_up = sem("set_up")
        iota_ready = sem("iota_ready")

        class Signals:

            def __init__(self, a, causal):
                if causal:
                    self.stacks_in = sems(f"{a}_stacks_in", RING)
                    self.masked = sem(f"{a}_masked")
                self.staged = sem(f"{a}_staged")
                self.unit_ready = sem(f"{a}_unit_ready")
                self.unit_taken = sem(f"{a}_unit_taken")
                self.tops_ready = sem(f"{a}_tops_ready")
                self.top_split = sem(f"{a}_top_split")
                self.top_rows_in = sem(f"{a}_top_rows_in")
                self.scores_ready = sem(f"{a}_scores_ready")
                self.exp_done = sem(f"{a}_exp_done")
                self.values_done = sem(f"{a}_values_done")
                self.o_taken = sem(f"{a}_o_taken")
                self.rec_ready = sem(f"{a}_rec_ready")
                self.o_scaled = sem(f"{a}_o_scaled")
                self.o_ready = sem(f"{a}_o_ready")
                self.o_stored = sems(f"{a}_o_stored", CPB)

        class BlockSignals:

            def __init__(self, a):
                self.out_ready = sem(f"{a}_out_ready")
                self.added = sem(f"{a}_added")
                self.stat_step = sem(f"{a}_stat_step")
                self.var_ready = sem(f"{a}_var_ready")
                self.std_ready = sem(f"{a}_std_ready")
                self.rstd_ready = sem(f"{a}_rstd_ready")
                self.normed = sem(f"{a}_normed")
                self.turned = sem(f"{a}_turned")
                self.turned_taken = sem(f"{a}_turned_taken")

        ss, cs = Signals("self", True), Signals("cross", False)
        n1, n2, n3 = BlockSignals("norm1"), BlockSignals("norm2"), BlockSignals("norm3")
        bias_added, pads_zero = sem("bias_added"), sem("pads_zero")
        xq_in = sems("xq_in", B)
        xtops_turned, xtop_rest, xpairs_ready = sem("xtops_turned"), sem("xtop_rest"), sem("xpairs_ready")
        pool_turn, sync_turn, vector_turn = sem("pool_turn"), sem("sync_turn"), sem("vector_turn")
        logits_ready, scores_done, route_step, counted, slots_ready, expert_ready = map(sem, (
            "logits_ready", "scores_done", "route_step", "counted", "slots_ready", "expert_ready"))
        counts_ready, counts_taken = sem("counts_ready"), sem("counts_taken")
        scattered, gathered_in = sem("scattered"), sems("gathered_in", NCH)
        hid_ready, sil_done, hid_done, acc_taken, down_done = map(sem, (
            "hid_ready", "sil_done", "hid_done", "acc_taken", "down_done"))
        slot_in, slot_turned, slot_T, slot_hid, slot_sil, slot_h, slot_hturned, slot_hT, slot_out, slot_y = (
            sems("slot_in", 2), sem("slot_turned"), sem("slot_T"), sem("slot_hid"), sem("slot_sil"), sem("slot_h"),
            sem("slot_hturned"), sem("slot_hT"), sem("slot_out"), sem("slot_y"))
        slot_stored = sems("slot_stored", 2)
        final_step, out_stored = sem("final_step"), sem("out_stored")

        block = ctx.enter_context(nc.Block())
        LOOPS = (NN - 2) // RING
        N_ITEMS = 4 * NCH
        AHEAD = 2
        ROUNDS = (TILES - 5) // 6
        assert 6 * ROUNDS + 5 == TILES
        EARLY_UNITS = [range(3 * e, 3 * e + 3) for e in range(6)]
        XB = 2

        @block.sync
        def _(sync):
            sync.dma_start(gate_rows[:, 0, :], gate_raw).then_inc(gate_in, 16)
            sync.dma_start(gate_rows[:, 1, :], gate_pick).then_inc(gate_in, 16)
            sync.dma_start(phase_s, phase).then_inc(gate_in, 16)
            sync.dma_start(wqkv_s, w_qkv.rearrange("(k p) n -> p k n", p=P)).then_inc(wqkv_in, 16)
            xT_v = xT.rearrange("(k p) t -> p k t", p=P)
            for n in range(NCH):
                sync.dma_start(feat_a[:, :, n * CH:(n + 1) * CH], xT_v[:, :, n * CH:(n + 1) * CH]).then_inc(xT_in[n], 16)
            for dst, src in ((idf[:], ident_f), (idb[:].bitcast(U16), ident_b), (causal_s[:].bitcast(U16), causal), (before_s[:], before)):
                sync.dma_start(dst, src).then_inc(ident_in, 16)

            sync.wait_ge(pads_zero, 1)
            sync.dma_start(k_st[STACK:STACK + 3].rearrange("p r h t -> p r (h t)").bitcast(U16),
                           ones.rearrange("(o n t) -> o n t", o=1, n=1).to_broadcast([3, RING, GH * S])).then_inc(ident_in, 16)

            def store_parts(it, n, m, dst_d, tile):
                sync.wait_ge(part3_ready, it + 1)
                b, c = divmod(n, CPB)
                g0 = NG * b + 2 * tile
                dst = dst_d[:, g0:g0 + 2, :, c * CH:(c + 1) * CH].rearrange("s g r t -> (g r) s t")
                sync.dma_start(dst, parts[:, it % ITEMS, :, :]).then_inc(parts_stored[it % ITEMS], 16)

            def wait_stored(items):
                for r in range(ITEMS):
                    sync.wait_ge(parts_stored[r], 16 * len(range(r, items, ITEMS)))

            def load_stacks(s, n, p):
                for st, order, src_d in ((q_st, QUERY_PARTS, q_parts_d), (k_st, KEY_PARTS, k_parts_d)):
                    for r0, r1, s0, count, copies in row_groups(order):
                        src = src_d[s0:s0 + count, bass.ds(n, 1)].rearrange("s o (d h) t -> s (o d) (h t)", d=HD)
                        if copies > 1:
                            src = src.to_broadcast([copies, HD, GH * S])
                        dst = st[r0 * HD:r1 * HD, p, :, :].rearrange("r h t -> r (h t)")
                        sync.dma_start(dst, src).then_inc(s.stacks_in[p], 16)

            def store_output(A, s, dst_d, n, c):
                sync.wait_ge(s.o_ready, CPB * (n + 1) + (c + 1))
                sync.sem_inc(sync_turn, 1)
                dst = dst_d[bass.ds(n, 1), :, c * CH:(c + 1) * CH].rearrange("o r t -> (o r) t")
                sync.dma_start(dst, o_nrm[:, c, :]).then_inc(s.o_stored[c], 16)

            def store_top_rows(A, s, n, p):
                sync.wait_ge(s.top_split, 3 * n + 3)
                for k in range(3):
                    dst = q_st[A.top_row + k:A.top_row + k + 1, p, :, :].rearrange("o h (i t) -> o (h i) t", t=P)
                    sync.dma_start(dst, ntop_p[0:GH * QT, k:k + 1, :]).then_inc(s.top_rows_in, 16)

            def load_output(in_sems, src_d, n):
                b, c = divmod(n, CPB)
                for k in range(KD):
                    g0 = NG * b + 2 * k
                    src = src_d[g0:g0 + 2, :, c * CH:(c + 1) * CH].rearrange("g (h r) t -> (g h) r t", r=32)[:, 0:HD, :]
                    sync.dma_start(feat_a[:, k, n * CH:(n + 1) * CH], src).then_inc(in_sems[n], 16)

            def zero_slots(n):
                share = (TILES + 1) // NN
                dst = slots_x_d.rearrange("(n p j) d -> n p (j d)", n=NN, p=P)[bass.ds(n, 1)].rearrange("o p m -> p (o m)")
                src = ntop[:, None, P // 2:P].to_broadcast([P, share * D // (P // 2), P // 2])
                sync.dma_start(dst.rearrange("p (m z) -> p m z", z=P // 2), src).then_inc(zeroed, 16)

            def stack_context():
                sync.wait_ge(ctx_step, 13)
                for m in range(KD):
                    for b in range(B):
                        g0 = NG * b + 2 * m
                        src = xk_parts[:, :, (B * m + b) * SKV:(B * m + b + 1) * SKV]
                        sync.dma_start(xk_parts_d[:, g0:g0 + 2, :, :].rearrange("s g r t -> (g r) s t"), src).then_inc(xk_stored, 16)
                sync.wait_ge(xk_stored, 16 * KD * B)
                sync.wait_ge(ones_rows, 2)
                for r, part in enumerate(KEY_PARTS):
                    src = xk_parts_d[part].rearrange("n (d h) t -> d n (h t)", d=HD)
                    sync.dma_start(xk_all[r * HD:(r + 1) * HD, :, :], src).then_inc(xk_in, 16)
                sync.dma_start(xk_all[CROSS.top_row:CROSS.exp_rows].rearrange("p n t -> p (n t)").bitcast(U16),
                               ones[0:NN * GH * SKV].rearrange("(o t) -> o t", o=1).to_broadcast([3, NN * GH * SKV])).then_inc(xk_in, 16)
                for r in range(3):
                    for b in range(B):
                        src = fill_row[:, r, b * SKV:(b + 1) * SKV][:, None, :].to_broadcast([1, NG * GH, SKV])
                        dst = xk_all[STACK + r:STACK + r + 1, NG * b:NG * (b + 1), :].rearrange("o g (h t) -> o (g h) t", h=GH)
                        sync.dma_start(dst, src).then_inc(xk_in, 16)

            def attention(A, s, dst_d, in_sems):
                def pair(n, p, last):
                    store_output(A, s, dst_d, n, 0)
                    if A.causal and not last:
                        store_top_rows(A, s, n + 1, (p + 1) % RING)
                    if A.causal:
                        zero_slots(n)
                    store_output(A, s, dst_d, n, 1)

                for c in range(CPB):
                    sync.sem_inc(s.o_stored[c], 16)
                if A.causal:
                    store_top_rows(A, s, 0, 0)
                    stack_context()
                if A.causal:
                    with sync.Fori(0, LOOPS) as i:
                        for p in range(RING):
                            n = RING * i + p
                            sync.wait_ge(s.values_done, A.slots + A.ns * n)
                            load_stacks(s, n + 2, (p + 2) % RING)
                            pair(n, p, False)
                else:
                    for n in range(NG + 1):
                        pair(n, n % RING, False)
                for c in range(CPB):
                    sync.wait_ge(s.o_stored[c], 16 * (NG + 1))
                    load_output(in_sems, dst_d, c)
                if not A.causal:
                    for n in range(NG + 1, NN - 2):
                        pair(n, n % RING, False)
                pair(NN - 2, (NN - 2) % RING, False)
                pair(NN - 1, (NN - 1) % RING, True)
                for c in range(CPB):
                    sync.wait_ge(s.o_stored[c], 16 * (NN + 1))
                    load_output(in_sems, dst_d, CPB + c)

            for n in range(NCH):
                for m in range(4):
                    store_parts(4 * n + m, n, m, (q_parts_d, k_parts_d)[m // KD], m % KD)
                if n == CPB - 1:
                    wait_stored(4 * CPB)
                    sync.wait_ge(set_up, 5)
                    load_stacks(ss, 0, 0)
            load_stacks(ss, 1, 1)
            wait_stored(N_ITEMS)
            sync.wait_ge(v_ready, 2 * NCH)
            attention(SELF, ss, o_self_d, oT_in)

            sync.wait_ge(pads_zero, 3)
            sync.dma_start(xq_all[STACK:STACK + 3].bitcast(U16), ones.rearrange("(o n t) -> o n t", o=1, n=1)
                           .to_broadcast([3, NN, GH * S])).then_inc(xq_in[0], 16)
            for n in range(NCH):
                for m in range(KD):
                    store_parts(N_ITEMS + KD * n + m, n, m, xq_parts_d, m)
                if n % CPB == CPB - 1:
                    wait_stored(N_ITEMS + KD * (n + 1))
                    b = n // CPB
                    for r, part in enumerate(QUERY_PARTS):
                        src = xq_parts_d[part, NG * b:NG * (b + 1)].rearrange("g (d h) t -> d g (h t)", d=HD)
                        sync.dma_start(xq_all[r * HD:(r + 1) * HD, NG * b:NG * (b + 1), :], src).then_inc(xq_in[b], 16)
            for b in range(B):
                sync.wait_ge(cs.top_split, 3 * (b + 1))
                for k in range(3):
                    dst = xq_all[CROSS.top_row + k:CROSS.top_row + k + 1, NG * b:NG * (b + 1), :]
                    dst = dst.rearrange("o g (r t) -> o (g r) t", t=P)
                    sync.dma_start(dst, ntop_p[:, k:k + 1, :]).then_inc(cs.top_rows_in, 16)
                sync.wait_ge(cs.top_rows_in, 48 * (b + 1))
                sync.sem_inc(xpairs_ready, NG)
            sync.wait_ge(n1.out_ready, NT)
            attention(CROSS, cs, o_cross_d, oxT_in)

            sync.wait_ge(cs.values_done, CROSS.slots + CROSS.ns * NN)
            sync.wait_ge(bias_added, NT // TPC)
            for dst, src in ((sw1_s, sw1), (sw2_s, sw2)):
                sync.dma_start(dst, src.rearrange("(k p) n -> p k n", p=P)).then_inc(shared_w_in, 16)
            sync.dma_start(sw3_s, sw3.rearrange("(k p) n -> p k n", p=P)).then_inc(shared_w_in, 16)
            for q in range(4):
                e0, e1 = NE // 4 * q, NE // 4 * (q + 1)
                for w, src in enumerate((rw1, rw2)):
                    dst = w12_s[:, e0:e1, :, w * RH:(w + 1) * RH].rearrange("p e k n -> p (e k) n")
                    sync.dma_start(dst, src[e0:e1].rearrange("e (k p) n -> p (e k) n", p=P)).then_inc(routed_w_in[q], 16)
                dst = w3_s[:, e0:e1, :, :].rearrange("p e k n -> p (e k) n")
                sync.dma_start(dst, rw3[e0:e1].rearrange("e (k p) n -> p (e k) n", p=P)).then_inc(routed_w_in[q], 16)

            def load_slot(j, p):
                src = slots_x_d[bass.ds(j * P, P), :]
                sync.dma_start(xs_in[:, p, :], src).then_inc(slot_in[p], 16)

            def store_slot(j, p):
                sync.wait_ge(slot_y, j + 1)
                sync.sem_inc(sync_turn, 1)
                sync.dma_start(slots_y_d[bass.ds(j * P, P), :], xs_y[:, p, :]).then_inc(slot_stored[p], 16)

            sync.wait_ge(scattered, 16 * TOPK * NT)
            sync.wait_ge(zeroed, 16 * NN)
            load_slot(0, 0)
            load_slot(1, 1)
            for j in range(3):
                sync.wait_ge(slot_turned, j + 1)
                load_slot(j + 2, j % 2)
            with sync.Fori(1, (TILES - 1) // 2 - 1) as i:
                for p in range(2):
                    j = 2 * i + p
                    sync.wait_ge(slot_turned, j + 2)
                    sync.sem_inc(sync_turn, 1)
                    load_slot(j + 3, 1 - p)
                    store_slot(j - 2, p)
            for j in range(TILES - 5, TILES):
                store_slot(j, j % 2)

            out_v = out.rearrange("b (t p) d -> p (b t) d", p=P)
            for n in range(NCH):
                sync.wait_ge(n3.normed, TPC * (n + 1))
                sync.dma_start(out_v[:, TPC * n:TPC * (n + 1), :], rows[:, TPC * n:TPC * (n + 1), :]).then_inc(out_stored, 16)
            sync.wait_ge(out_stored, 16 * NCH)
            for r in range(2):
                sync.wait_ge(slot_stored[r], 16 * len(range(r, TILES, 2)))

        @block.gpsimd
        def _(pool):
            pool.iota(iota_e[:], [[1, NE]], base=0, channel_multiplier=0,
                      allow_small_or_imprecise_dtypes=True).then_inc(iota_ready, 1)
            pool.wait_ge(iota_ready, 1)
            pool.iota(iota_t[:], [[1, 48]], base=0, channel_multiplier=0,
                      allow_small_or_imprecise_dtypes=True).then_inc(iota_ready, 1)
            pool.wait_ge(iota_ready, 2)
            pool.memset(region_r[STACK:P, stacks_at:probs_at], 0.0).then_inc(pads_zero, 1)
            pool.wait_ge(pads_zero, 1)
            zero = pool.to_reg(0.0)

            def part3(it):
                r = it % ITEMS
                pool.wait_ge(part2_ready, it + 1)
                pool.tensor_tensor(parts[:, r, 2, :], rest[:, r, :], parts[:, r, 1, :], ALU.subtract).then_inc(part3_ready, 1)

            for it in range(N_ITEMS):
                part3(it)

            def stage(A, s, n, p):
                if A.causal:
                    src = v_all[:, bass.ds(n, 1), :, :].rearrange("p o t (h d) -> p (o t) h d", d=HD)
                    pool.tensor_copy(v_st[:, p, :, :, 0:HD], src).then_inc(s.staged, 1)
                else:
                    src = xv_all[:, bass.ds(n, 1), :].rearrange("p o (h d) -> p (o h) d", d=HD)
                    pool.tensor_copy(v_st[:, p, 0, :, 0:HD], src).then_inc(s.staged, 1)

            def scale_output(s, n, c):
                pool.wait_ge(s.rec_ready, CPB * n + c + 1)
                blocks = o_blk[:, c, :].rearrange("p (q r) -> p q r", r=32)[:, :, 0:HD]
                rec = o_rec[:, c, :, None].to_broadcast([P, CH // 32, HD])
                pool.tensor_tensor(blocks, blocks, rec, ALU.mult).then_inc(s.o_scaled, 1)

            def self_attention(A, s):
                def pair(n, p):
                    for st, (_, _, q0) in enumerate(A.steps):
                        if st in A.diagonal:
                            pool.wait_ge(s.exp_done, 2 * (A.ns * n + st + 1))
                            pool.sem_inc(pool_turn, 1)
                            blk = probs[:, st % A.slots, :, q0:q0 + P]
                            pool.affine_select(out=blk, in_=blk, pattern=[[0, GH], [1, P]], compare_op=ALU.is_ge,
                                               fill=zero, base=0, channel_multiplier=-1).then_inc(s.masked, 1)
                        for back, c in A.output_at(st, A.take_lag):
                            if not (isinstance(n, int) and n < back):
                                scale_output(s, n - back, c)
                        if st == A.take_lag and not (isinstance(n, int) and n == NN - 1):
                            stage(A, s, n + 1, (p + 1) % RING)

                stage(A, s, 0, 0)
                pair(0, 0)
                with pool.Fori(0, LOOPS) as i:
                    for q in range(RING):
                        pair(RING * i + (q + 1), (q + 1) % RING)
                pair(NN - 1, (NN - 1) % RING)
                scale_output(s, NN - 1, 1)

            def cross_attention(A, s):
                def pair(n):
                    scale_output(s, n, 0)
                    scale_output(s, n, 1)

                stage(A, s, 0, 0)
                stage(A, s, 1, 1)
                with pool.Fori(0, LOOPS) as i:
                    for p in range(RING):
                        n = RING * i + p
                        pool.wait_ge(s.values_done, A.slots + A.ns * n)
                        stage(A, s, n + 2, (p + 2) % RING)
                        pair(n)
                pair(NN - 2)
                pair(NN - 1)

            pool.wait_ge(v_taken, 2 * NCH)
            pool.wait_ge(set_up, 5)
            self_attention(SELF, ss)
            pool.wait_ge(ss.values_done, SELF.slots + SELF.ns * NN)
            pool.wait_ge(ss.o_scaled, CPB * NN)
            pool.memset(region_r[STACK:P, probs_at:stacks_at + NN * GH * S // 2], 0.0).then_inc(pads_zero, 1)
            pool.wait_ge(pads_zero, 2)
            pool.memset(xprobs[P // 2:P], 0.0).then_inc(pads_zero, 1)
            pool.wait_ge(pads_zero, 3)
            for it in range(N_ITEMS, N_ITEMS + KD * NCH):
                part3(it)
            for n in range(NCH):
                pool.wait_ge(n1.turned_taken, KD * (n + 1))
                pool.wait_ge(small_in, SMALL)
                tiles = rows[:, TPC * n:TPC * (n + 1), :]
                pool.tensor_tensor(tiles, tiles, bo_b[:, None, :].to_broadcast([P, TPC, D]), ALU.add).then_inc(bias_added, 1)
            pool.wait_ge(xk_in, 16 * (len(KEY_PARTS) + 1 + 3 * B))
            cross_attention(CROSS, cs)

            pool.wait_ge(slots_ready, 1)
            pool.wait_ge(zeroed, 16 * NN)
            for t in range(NT):
                for k in range(TOPK):
                    pool.indirect_dma_start(out=slots_x_d, out_offset=bass.IndirectOffsetOnAxis(ap=slots_u[:, k, t:t + 1], axis=0),
                                            in_=rows[:, t, :], in_offset=None).then_inc(scattered, 16)
            for r in range(2):
                pool.wait_ge(slot_stored[r], 16 * len(range(r, TILES, 2)))
            pool.wait_ge(slot_out, TILES)
            for t in range(NT):
                for k in range(TOPK):
                    pool.indirect_dma_start(out=gathered[:, t, k, :], out_offset=None, in_=slots_y_d,
                                            in_offset=bass.IndirectOffsetOnAxis(ap=slots_u[:, k, t:t + 1], axis=0)
                                            ).then_inc(gathered_in[t // TPC], 16)

        @block.scalar
        def _(act):
            act.wait_ge(gate_in, 48)
            act.activation(gate_rows[:, 0, :], gate_rows[:, 0, :], ACT.Sigmoid).then_inc(gate_sig, 1)
            small = [(router_s[:], router_w.rearrange("(k p) n -> p k n", p=P)),
                     (ctxT_s, ctxT.rearrange("(k p) t -> p k t", p=P)),
                     (wk_s, w_k.rearrange("(k p) n -> p k n", p=P)), (wv_s, w_v.rearrange("(k p) n -> p k n", p=P)),
                     (bq_s[:], b_q), (bk_s[:], b_k),
                     (mask_u[:], mask.rearrange("b t -> (b t)").rearrange("(o t) -> o t", o=1).to_broadcast([P, B * SKV])),
                     (bv_b[0:SKV], b_v.rearrange("(o t) -> o t", o=1).to_broadcast([SKV, D])),
                     (bo_b, b_o.rearrange("(o t) -> o t", o=1).to_broadcast([P, D])),
                     (ebias_b[:], expert_bias.rearrange("(o t) -> o t", o=1).to_broadcast([P, NE])),
                     (wo_s, w_out.rearrange("(k p) n -> p k n", p=P)), (wq_s, w_q.rearrange("(k p) n -> p k n", p=P)),
                     (wxo_s, w_o.rearrange("(k p) n -> p k n", p=P))]
            for dst, src in small:
                act.dma_start(dst, src).then_inc(small_in, 16)
            assert 16 * len(small) == SMALL
            for k in range(4):
                act.wait_ge(gate_ready, k + 1)
                act.activation(gate[:, k // 2, (k % 2) * CH:(k % 2 + 1) * CH], PS[:, k, :], ACT.Copy).then_inc(gate_out, 1)

            def part1(it):
                act.wait_ge(whole_ready, it + 1)
                if it >= ITEMS:
                    act.wait_ge(parts_stored[it % ITEMS], 16 * (it // ITEMS))
                act.activation(parts[:, it % ITEMS, 0, :], whole[:, it % ITEMS, :], ACT.Copy).then_inc(part1_ready, 1)

            def part2(it):
                act.wait_ge(rest_ready, it + 1)
                act.activation(parts[:, it % ITEMS, 1, :], rest[:, it % ITEMS, :], ACT.Copy).then_inc(part2_ready, 1)

            for n in range(NCH):
                b, c = divmod(n, CPB)
                part1(4 * n)
                for it in range(4 * n + 1, 4 * n + 4):
                    part1(it)
                    part2(it - 1)
                part2(4 * n + 3)
                for v in range(2):
                    act.wait_ge(v_ready, 2 * n + v + 1)
                    for u in range(2):
                        ins = act.activation(v_all[:, NG * b:NG * (b + 1), TPC * c + 2 * v + u, :],
                                             PS[:, 4 + v, u * D:(u + 1) * D].rearrange("p (g r) -> p g r", g=NG), ACT.Copy)
                    ins.then_inc(v_taken, 1)
            act.wait_ge(v_ready, 2 * NCH)
            act.wait_ge(ctx_step, 13)
            act.dma_start(rows[:], x.rearrange("b (t p) d -> p (b t) d", p=P)).then_inc(rows_in, 16)

            def attention(A, s, probs):
                def exponentials(n):
                    for st, (c, j, q0) in enumerate(A.steps):
                        act.wait_ge(s.values_done, A.ns * n + (st + 1))
                        for hp in range(2):
                            act.wait_ge(s.scores_ready, 2 * (A.ns * n + st) + hp + 1)
                            act.activation(probs[0:A.keys, st % A.slots, 2 * hp:2 * hp + 2, q0:CH],
                                           PS[0:A.keys, 2 + 2 * hp:4 + 2 * hp, q0:CH], ACT.Exp, scale=SCALE).then_inc(s.exp_done, 1)

                with act.Fori(0, LOOPS) as i:
                    for p in range(RING):
                        exponentials(RING * i + p)
                exponentials(NN - 2)
                exponentials(NN - 1)

            def norm(g, n):
                act.wait_ge(g.var_ready, n + 1)
                act.wait_ge(g.rstd_ready, max(0, n - 1))
                act.activation(std[:, n % 2], mean_var[:, n % 2, :, 1], ACT.Sqrt, bias=eps_s[:]).then_inc(g.std_ready, 1)

            def take_turned(g, n):
                for k in range(KD):
                    act.wait_ge(g.turned, KD * n + k + 1)
                    act.activation(feat_b[:, k, n * CH:(n + 1) * CH], PS[:, 4 + k, :], ACT.Copy).then_inc(g.turned_taken, 1)

            attention(SELF, ss, probs)
            for n in range(AHEAD):
                norm(n1, n)
            for n in range(NCH):
                if n == 0:
                    take_turned(n1, 0)
                    take_turned(n1, 1)
                elif n == AHEAD:
                    norm(n1, 2)
                    take_turned(n1, 2)
                    norm(n1, 3)
                    take_turned(n1, 3)
                it = N_ITEMS + KD * n
                part1(it)
                part1(it + 1)
                part2(it)
                part2(it + 1)
            attention(CROSS, cs, xprobs)
            for n in range(AHEAD):
                norm(n2, n)
            for n in range(NCH):
                take_turned(n2, n)
                if n + AHEAD < NCH:
                    norm(n2, n + AHEAD)

            act.wait_ge(logits_ready, 1)
            act.activation(scores, PS[:, 7, 0:NT * NE].rearrange("p (t e) -> p t e", e=NE), ACT.Sigmoid).then_inc(scores_done, 1)

            def shared_chunk(n):
                for h in range(FH // P):
                    act.wait_ge(hid_ready, 2 * (FH // P) * n + 2 * h + 1)
                    act.wait_ge(hid_done, (FH // P) * n + max(0, h - 1))
                    act.activation(sil[:, h % 2, :], PS[:, 2 * (h % 2), :], ACT.Silu).then_inc(sil_done, 1)
                    chunk, part = FINISH.get((n, h), (0, 0))
                    if part == TOPK + 1:
                        norm(n3, chunk)

            for n in range(NCH // 2):
                shared_chunk(n)

            def slot_turn(j, p):
                act.wait_ge(slot_turned, j + 1)
                act.activation(xs_T[:, p, :], PS[:, p, 0:KD * P], ACT.Copy).then_inc(slot_T, 1)

            def slot_silu(j, p):
                act.wait_ge(slot_hid, j + 1)
                if not (isinstance(j, int) and j < 2):
                    act.wait_ge(slot_h, j - 1)
                act.activation(xs_sil[:, p, :], PS[:, 2 + p, 0:RH], ACT.Silu).then_inc(slot_sil, 1)

            act.wait_ge(acc_taken, 4 * NCH // 2)
            slot_turn(0, 0)
            for j in range(2):
                slot_turn(j + 1, (j + 1) % 2)
                slot_silu(j, j)
            with act.Fori(1, (TILES - 1) // 2) as i:
                for p in range(2):
                    slot_turn(2 * i + p + 1, 1 - p)
                    slot_silu(2 * i + p, p)
            slot_silu(TILES - 1, 0)
            for n in range(NCH // 2, NCH):
                shared_chunk(n)
            norm(n3, NCH - 1)

        @block.tensor
        def _(pe):
            pe.wait_ge(gate_prod, 1)
            for k in range(4):
                pe.matmul(PS[:, k, :], gate_rows[:, 0, (k // 2) * P:(k // 2 + 1) * P],
                          phase_s[:, (k % 2) * CH:(k % 2 + 1) * CH], start=True, stop=True).then_inc(gate_ready, 1)
            def project_context():
                pe.wait_ge(small_in, SMALL)
                for m in range(KD):
                    for k in range(KD):
                        mm = pe.matmul(PS[:, 6, m * B * SKV:(m + 1) * B * SKV], wk_s[:, k, m * P:(m + 1) * P], ctxT_s[:, k, :],
                                       start=(k == 0), stop=(k == KD - 1))
                mm.then_inc(ctx_ready, 1)
                for b in range(B):
                    for k in range(KD):
                        mm = pe.matmul(PS[0:SKV, 7, b * D:(b + 1) * D], ctxT_s[:, k, b * SKV:(b + 1) * SKV], wv_s[:, k, :],
                                       start=(k == 0), stop=(k == KD - 1))
                mm.then_inc(ctx_ready, 1)

            loads = sum(len(row_groups(o)) for o in (QUERY_PARTS, KEY_PARTS))

            def max_unit(A, s, n, p, k, bank0=0):
                i, kc, h0, nh, w = A.units[k]
                pe.wait_ge(s.unit_taken, (A.nu + 1) * n + max(0, k - 1))
                bank = PS[:, bank0 + k % 2, :]
                for a in range(nh):
                    mm = pe.matmul(bank[:, a * w:(a + 1) * w], q_st[0:A.max_rows, p, h0 + a, i * P:(i + 1) * P],
                                   k_st[0:A.max_rows, p, h0 + a, kc * CH:kc * CH + w],
                                   start=(a == 0), stop=False, skip_group_check=True)
                if kc == i // TPC:
                    out_ = bank[:, 0:nh * w].rearrange("p (a w) -> p a w", a=nh)[:, :, w - P:w]
                    mm = pe.matmul(out_, idb[:], causal_s[:, 0:nh, :], start=False, stop=True, skip_group_check=True)
                mm.then_inc(s.unit_ready, 1)

            def first_units(ks):
                if not ks:
                    pe.wait_ge(ss.stacks_in[0], 16 * loads)
                    pe.wait_ge(ctx_step, 10)
                    pe.wait_ge(ident_in, 80)
                    pe.wait_ge(set_up, 5)
                for k in ks:
                    max_unit(SELF, ss, 0, 0, k, 6)

            def out_tile(g, t, w, bank):
                for k in range(KD):
                    mm = pe.matmul(PS[:, bank, 0:D], feat_a[:, k, t * P:(t + 1) * P], w[:, k, :],
                                   start=(k == 0), stop=(k == KD - 1))
                mm.then_inc(g.out_ready, 1)

            def out_projection(g, n, w, in_sems):
                pe.wait_ge(in_sems[n], 16 * KD)
                for t in range(TPC * n, TPC * (n + 1)):
                    if t >= TPC:
                        pe.wait_ge(g.added, t - TPC + 1)
                    out_tile(g, t, w, t % TPC)

            def attention(A, s, weights):
                def stack_slot(turn, p):
                    pe.wait_ge(s.stacks_in[p], 16 * loads * (turn + 1))

                def turn_tops(n):
                    pe.wait_ge(s.tops_ready, n + 1)
                    pe.transpose(PS[:, A.nu % 2, 0:P], ntop[:], idf[:]).then_inc(s.unit_ready, 1)

                def scores(n, p, st, hp):
                    c, j, q0 = A.steps[st]
                    if not (isinstance(n, int) and n == 0 and st == 0):
                        pe.wait_ge(s.exp_done, 2 * (A.ns * n + st) + hp - 1)
                    for h in (2 * hp, 2 * hp + 1):
                        if A.causal:
                            keys = k_st[:, p, h, j * P:(j + 1) * P]
                            queries = q_st[:, p, h, c * CH + q0:(c + 1) * CH]
                        else:
                            keys = xk_all[:, bass.ds(n, 1), h * SKV:(h + 1) * SKV].rearrange("p o t -> p (o t)")
                            queries = xq_all[:, bass.ds(n, 1), h * S + c * CH:h * S + (c + 1) * CH]
                            queries = queries.rearrange("p o t -> p (o t)")
                        mm = pe.matmul(PS[0:A.keys, 2 + h, q0:CH], keys, queries, start=True, stop=True)
                    mm.then_inc(s.scores_ready, 1)

                def values(n, p, st, hp):
                    c, j, q0 = A.steps[st]
                    if hp == 0:
                        pe.wait_ge(s.exp_done, 2 * (A.ns * n + st + 1))
                        if st in A.diagonal:
                            pe.wait_ge(s.masked, len(A.diagonal) * n + A.diagonal.index(st) + 1)
                        if j == 0:
                            pe.wait_ge(s.staged, n + 1)
                            pe.wait_ge(s.o_taken, CPB * n + (c + 1))
                    for h in (2 * hp, 2 * hp + 1):
                        mm = pe.matmul(PS[32 * h:32 * h + 32, 6 + c, q0:CH], v_st[:, p, j, h, :],
                                       weights[:, st % A.slots, h, q0:CH], start=(j == 0), stop=(st == A.last[c]),
                                       skip_group_check=True)
                    if hp == 1:
                        mm.then_inc(s.values_done, 1)

                def step(n, q, st, ahead):
                    def units(quarter):
                        if ahead:
                            for k in A.units_of(st, quarter, isinstance(n, int) and n == 0):
                                max_unit(A, s, n + ahead, (q + 1 + ahead) % RING, k)

                    for hp in range(2):
                        scores(n, (q + 1) % RING, st, hp)
                        units(hp)
                    for hp in range(2):
                        if st >= A.lag:
                            values(n, (q + 1) % RING, st - A.lag, hp)
                        elif not (isinstance(n, int) and n == 0):
                            values(n - 1, q % RING, A.ns + st - A.lag, hp)
                        units(2 + hp)
                    if st == A.top_step and ahead:
                        turn_tops(n + 1)
                    if A.causal and isinstance(n, int) and n == NN - 1 and st < AHEAD * TPC:
                        if st == 0:
                            pe.wait_ge(s.unit_taken, (A.nu + 1) * NN)
                            pe.wait_ge(small_in, SMALL)
                        if st % TPC == 0:
                            pe.wait_ge(oT_in[st // TPC], 16 * KD)
                        if st >= 2:
                            pe.wait_ge(n1.added, st - 1)
                        out_tile(n1, st, wo_s, st % 2)

                def pair_turn(n, i, q):
                    first, last = (isinstance(n, int) and n == e for e in (0, NN - 1))
                    if A.causal and not last:
                        stack_slot(i + (q + 2) // RING, (q + 2) % RING)
                    if not first:
                        for st in range(A.next_step, A.ns):
                            step(n - 1, q - 1, st, 0 if last else 2)
                    if A.causal:
                        pe.wait_ge(s.top_rows_in, 48 * (n + 1))
                    else:
                        pe.wait_ge(xpairs_ready, n + 1)
                    for st in range(A.next_step):
                        step(n, q, st, 0 if last else 1)

                pe.sem_inc(s.values_done, A.slots)
                if A.causal:
                    turn_tops(0)
                pair_turn(0, 0, -1)
                with pe.Fori(0, LOOPS) as i:
                    for q in range(RING):
                        pair_turn(RING * i + (q + 1), i, q)
                pair_turn(NN - 1, LOOPS, 0)
                for st in range(A.next_step, A.ns):
                    step(NN - 1, 0, st, 0)
                for st in range(A.ns - A.lag, A.ns):
                    for hp in range(2):
                        values(NN - 1, (NN - 1) % RING, st, hp)

            def turn(g, n):
                for k in range(KD):
                    if n:
                        pe.wait_ge(g.turned_taken, KD * (n - 1) + k + 1)
                    for u in range(TPC):
                        t = TPC * n + u
                        pe.wait_ge(g.normed, t + 1)
                        mm = pe.transpose(PS[:, 4 + k, u * P:(u + 1) * P], rows[:, t, k * P:(k + 1) * P], idf[:])
                    mm.then_inc(g.turned, 1)

            pe.wait_ge(wqkv_in, 16)
            pe.wait_ge(gate_out, 4)
            for n in range(NCH):
                last = n == NCH - 1
                if n == CPB:
                    project_context()
                if last:
                    first_units(range(0))
                pe.wait_ge(xT_in[n], 16)
                for m in range(4):
                    if n:
                        pe.wait_ge(whole_ready, 4 * (n - 1) + m + 1)
                    for k in range(KD):
                        mm = pe.matmul(PS[:, m, :], wqkv_s[:, k, m * P:(m + 1) * P], feat_a[:, k, n * CH:(n + 1) * CH],
                                       start=(k == 0), stop=(k == KD - 1))
                    mm.then_inc(projected, 1)
                    if last:
                        first_units(EARLY_UNITS[m])
                if n:
                    pe.wait_ge(v_taken, 2 * n)
                for v in range(2):
                    for u in range(2):
                        t0 = n * CH + (2 * v + u) * P
                        for k in range(KD):
                            mm = pe.matmul(PS[:, 4 + v, u * D:(u + 1) * D], feat_a[:, k, t0:t0 + P], wqkv_s[:, k, 2 * D:3 * D],
                                           start=(k == 0), stop=(k == KD - 1))
                    mm.then_inc(v_ready, 1)
                    if last:
                        first_units(EARLY_UNITS[4 + v])
            first_units(range(EARLY_UNITS[-1].stop, SELF.nu))

            pe.wait_ge(whole_ready, N_ITEMS)
            pe.wait_ge(v_taken, 2 * NCH)
            attention(SELF, ss, probs)

            pe.wait_ge(ss.o_taken, CPB * (NN + 1))
            pe.wait_ge(n1.added, AHEAD * TPC)
            for n in range(NCH):
                if n == AHEAD:
                    for late in range(AHEAD, NCH):
                        out_projection(n1, late, wo_s, oT_in)
                if n == 0:
                    turn(n1, 0)
                    turn(n1, 1)
                elif n > 1:
                    turn(n1, n)
                pe.wait_ge(n1.turned_taken, KD * (n + 1))
                for m in range(KD):
                    if n:
                        pe.wait_ge(whole_ready, N_ITEMS + KD * (n - 1) + m + 1)
                    for k in range(KD):
                        mm = pe.matmul(PS[:, 6 + m, :], wq_s[:, k, m * P:(m + 1) * P], feat_b[:, k, n * CH:(n + 1) * CH],
                                       start=(k == 0), stop=(k == KD - 1))
                    mm.then_inc(projected, 1)

            pe.wait_ge(n1.added, NT)
            pe.wait_ge(whole_ready, N_ITEMS + KD * NCH)
            pe.wait_ge(xk_in, 16 * (len(KEY_PARTS) + 1 + 3 * B))
            rows_ = CROSS.max_rows
            for b in range(B):
                pe.wait_ge(xq_in[b], 16 * (len(QUERY_PARTS) + (0 if b else 1)))
                for g in range(NG):
                    for u in range(QT // XB):
                        pe.wait_ge(cs.unit_taken, QT // XB * g + (QT // XB * NG * b + u + 1))
                        for i in range(XB * u, XB * (u + 1)):
                            for h in range(GH):
                                queries = xq_all[0:rows_, bass.ds(g + NG * b, 1), h * S + i * P:h * S + (i + 1) * P]
                                keys = xk_all[0:rows_, bass.ds(g + NG * b, 1), h * SKV:(h + 1) * SKV]
                                mm = pe.matmul(PS[:, i % (2 * XB), h * SKV:(h + 1) * SKV],
                                               queries.rearrange("p o t -> p (o t)"), keys.rearrange("p o t -> p (o t)"),
                                               start=True, stop=True)
                        mm.then_inc(cs.unit_ready, 1)
                pe.wait_ge(cs.tops_ready, b + 1)
                pe.transpose(PS[:, 6 + b, 0:P], ntop[:], idf[:]).then_inc(xtops_turned, 1)
            attention(CROSS, cs, xprobs)

            for n in range(AHEAD):
                out_projection(n2, n, wxo_s, oxT_in)
            pe.wait_ge(cs.o_taken, CPB * (NN + 1))
            for n in range(NCH):
                turn(n2, n)
                if n + AHEAD < NCH:
                    out_projection(n2, n + AHEAD, wxo_s, oxT_in)
                pe.wait_ge(n2.turned_taken, KD * (n + 1))
                for t in range(TPC * n, TPC * (n + 1)):
                    for k in range(KD):
                        mm = pe.matmul(PS[:, 7, t * NE:(t + 1) * NE], feat_b[:, k, t * P:(t + 1) * P], router_s[:, k, :],
                                       start=(k == 0), stop=(k == KD - 1))
            mm.then_inc(logits_ready, 1)
            pe.wait_ge(n2.added, NT)

            def count_tokens():
                pe.wait_ge(scores_done, 1)
                pe.wait_ge(counted, 1)
                flat = picked.rearrange("p e t -> p (e t)")
                pe.matmul(PS[:, 7, 0:NE * NT], before_s[:], flat, start=True, stop=True)
                pe.matmul(PS[:, 7, NE * NT:2 * NE * NT], ones_s[:], flat, start=True, stop=True).then_inc(counts_ready, 1)

            def shared_chunk(n):
                hs = FH // P
                for h in range(hs + 1):
                    if h == 1 and isinstance(n, int) and n == 0:
                        count_tokens()
                    if h < hs:
                        pe.wait_ge(hid_done, hs * n + max(0, h - 1))
                        for w, ws in enumerate((sw1_s, sw2_s)):
                            for k in range(KD):
                                mm = pe.matmul(PS[:, 2 * (h % 2) + w, :], ws[:, k, h * P:(h + 1) * P],
                                               feat_b[:, k, bass.ds(n * CH, CH)], start=(k == 0), stop=(k == KD - 1))
                            mm.then_inc(hid_ready, 1)
                    if h == 1 and isinstance(n, int) and n == 0:
                        pe.wait_ge(counts_taken, 1)
                    if h:
                        pe.wait_ge(hid_done, hs * n + h)
                        if h == 1:
                            pe.wait_ge(acc_taken, TPC * n)
                        for u in range(TPC):
                            mm = pe.matmul(PS[:, 4 + u, 0:D], hidT[:, (h - 1) % 4, u * P:(u + 1) * P], sw3_s[:, h - 1, :],
                                           start=(h == 1), stop=(h == hs))
                        mm.then_inc(down_done, 1)

            pe.wait_ge(shared_w_in, 48)
            for n in range(NCH // 2):
                shared_chunk(n)

            pe.wait_ge(acc_taken, TPC * NCH // 2)
            pe.wait_ge(expert_ready, 1)
            for q in range(4):
                pe.wait_ge(routed_w_in[q], 48)

            def turn_slot(i, p):
                j = 2 * i + p
                pe.wait_ge(slot_in[p], 16 * (i + 1))
                if not (isinstance(j, int) and j < 2):
                    pe.wait_ge(slot_T, j - 1)
                for k in range(KD):
                    mm = pe.transpose(PS[:, p, k * P:(k + 1) * P], xs_in[:, p, k * P:(k + 1) * P], idf[:])
                mm.then_inc(slot_turned, 1)

            def hidden_slot(i, p, e):
                j = 2 * i + p
                pe.wait_ge(slot_T, j + 1)
                if not (isinstance(j, int) and j < 2):
                    pe.wait_ge(slot_h, j - 1)
                for k in range(KD):
                    w = w12_s[:, bass.ds(e, 1), k, :].rearrange("p o n -> p (o n)")
                    mm = pe.matmul(PS[:, 2 + p, :], xs_T[:, p, k * P:(k + 1) * P], w, start=(k == 0), stop=(k == KD - 1))
                mm.then_inc(slot_hid, 1)

            def turn_hidden(i, p):
                j = 2 * i + p
                pe.wait_ge(slot_h, j + 1)
                if not (isinstance(j, int) and j < 2):
                    pe.wait_ge(slot_hT, j - 1)
                for k in range(KD):
                    mm = pe.transpose(PS[:, 4 + p, k * P:(k + 1) * P], xs_h[:, p, k * P:(k + 1) * P], idf[:])
                mm.then_inc(slot_hturned, 1)

            def out_slot(i, p, e):
                j = 2 * i + p
                pe.wait_ge(slot_hT, j + 1)
                if not (isinstance(j, int) and j < 2):
                    pe.wait_ge(slot_y, j - 1)
                for k in range(KD):
                    w = w3_s[:, bass.ds(e, 1), k, :].rearrange("p o n -> p (o n)")
                    mm = pe.matmul(PS[:, 6 + p, 0:D], xs_hT[:, p, k * P:(k + 1) * P], w, start=(k == 0), stop=(k == KD - 1))
                mm.then_inc(slot_out, 1)

            def expert(j):
                return pe.value_load(expert_of[0:1, bass.ds(j, 1)], min_val=0, max_val=NE - 1)

            turn_slot(0, 0)
            turn_slot(0, 1)
            hidden_slot(0, 0, expert(0))
            turn_slot(1, 0)
            hidden_slot(0, 1, expert(1))
            turn_hidden(0, 0)

            def step(i, p):
                j = 2 * i + p
                turn_slot(i + p, 1 - p)
                hidden_slot(i, p, expert(j))
                out_slot(i - 1, p, expert(j - 2))
                turn_hidden(i - 1 + p, 1 - p)

            step(1, 0)
            step(1, 1)
            with pe.Fori(0, ROUNDS) as r:
                for i in range(2, 5):
                    for p in range(2):
                        step(3 * r + i, p)
            i = (TILES - 1) // 2
            hidden_slot(i, 0, expert(2 * i))
            out_slot(i - 1, 0, expert(2 * i - 2))
            turn_hidden(i - 1, 1)
            out_slot(i - 1, 1, expert(2 * i - 1))
            turn_hidden(i, 0)
            out_slot(i, 0, expert(2 * i))
            pe.wait_ge(slot_y, TILES)

            with pe.Fori(NCH // 2, NCH) as n:
                shared_chunk(n)


        @block.vector
        def _(v):
            v.memset(ntop[:], 0.0).then_inc(set_up, 1)
            v.memset(tops[:], LOWEST).then_inc(set_up, 1)
            v.memset(eps_s[:], EPS).then_inc(set_up, 1)
            v.wait_ge(gate_sig, 1)
            v.tensor_tensor(gate_rows[:, 0, :], gate_rows[:, 0, :], gate_rows[:, 1, :], ALU.mult).then_inc(gate_prod, 1)
            v.memset(v_st[:], 0.0).then_inc(set_up, 1)
            v.wait_ge(set_up, 4)
            v.memset(v_st[:, :, :, :, HD:HD + 1], 1.0).then_inc(set_up, 1)
            v.memset(ones_s[:], 1.0).then_inc(ones_rows, 1)
            v.memset(xk_all[STACK:P], 0.0).then_inc(ones_rows, 1)
            v.memset(xv_all[:], 0.0).then_inc(ones_rows, 1)

            def split_context():
                v.wait_ge(small_in, SMALL)
                v.tensor_copy(mask_b, mask_u[:]).then_inc(ctx_step, 1)
                v.wait_ge(ctx_ready, 1)
                for m in range(KD):
                    v.tensor_scalar(xk_whole[:, m, :], PS[:, 6, m * B * SKV:(m + 1) * B * SKV], bk_s[:, m:m + 1], None,
                                    ALU.add).then_inc(ctx_step, 1)
                v.wait_ge(ctx_step, 3)
                v.tensor_tensor(xk_whole, xk_whole, mask_b[:, None, :].to_broadcast([P, KD, B * SKV]), ALU.mult).then_inc(ctx_step, 1)
                xk_part = [xk_parts[:, r, :].rearrange("p (m t) -> p m t", m=KD) for r in range(3)]
                v.wait_ge(ctx_step, 4)
                v.tensor_copy(xk_part[0], xk_whole).then_inc(ctx_step, 1)
                v.wait_ge(ctx_step, 5)
                v.tensor_tensor(xk_rest, xk_whole, xk_part[0], ALU.subtract).then_inc(ctx_step, 1)
                v.wait_ge(ctx_step, 6)
                v.tensor_copy(xk_part[1], xk_rest).then_inc(ctx_step, 1)
                v.wait_ge(ctx_step, 7)
                v.tensor_tensor(xk_part[2], xk_rest, xk_part[1], ALU.subtract).then_inc(ctx_step, 1)
                v.wait_ge(ctx_ready, 2)
                v.wait_ge(ones_rows, 3)
                for b in range(B):
                    v.tensor_tensor(xv_all[0:SKV, NG * b:NG * (b + 1), :], PS[0:SKV, 7, b * D:(b + 1) * D].rearrange("p (g r) -> p g r", g=NG),
                                    bv_b[0:SKV].rearrange("p (g r) -> p g r", g=NG), ALU.add).then_inc(ctx_step, 1)
                for r in range(3):
                    v.tensor_scalar(fill_row[:, r, :], mask_b[0:1], -1.0, FILL_PARTS[r], ALU.add, ALU.mult).then_inc(ctx_step, 1)

            def take_whole(it, make):
                r = it % ITEMS
                v.wait_ge(projected, it + 1)
                if it >= ITEMS:
                    v.wait_ge(part1_ready, it - ITEMS + 1)
                    v.wait_ge(rest_ready, it - ITEMS + 1)
                make(whole[:, r, :]).then_inc(whole_ready, 1)

            def take_rest(it):
                r = it % ITEMS
                v.wait_ge(part1_ready, it + 1)
                if it >= ITEMS:
                    v.wait_ge(part3_ready, it - ITEMS + 1)
                v.tensor_tensor(rest[:, r, :], whole[:, r, :], parts[:, r, 0, :], ALU.subtract).then_inc(rest_ready, 1)

            def gated(m, c):
                return lambda dst: v.tensor_tensor(dst, PS[:, m, :], gate[:, m, c * CH:(c + 1) * CH], ALU.mult)

            def copied(m):
                return lambda dst: v.tensor_copy(dst, PS[:, m, :])

            def biased(m):
                return lambda dst: v.tensor_scalar(dst, PS[:, 6 + m, :], bq_s[:, m:m + 1], None, ALU.add)

            def split(first, makes, between=lambda k: None):
                take_whole(first, makes[0])
                between(0)
                for k, make in enumerate(makes[1:]):
                    take_whole(first + k + 1, make)
                    take_rest(first + k)
                    between(k + 1)
                take_rest(first + len(makes) - 1)

            def take_unit(A, s, n, k, bank0=0):
                i, kc, h0, nh, w = A.units[k]
                v.wait_ge(s.unit_ready, (A.nu + 1) * n + k + 1)
                v.tensor_reduce(tops[:, h0:h0 + nh, i, kc], PS[:, bank0 + k % 2, 0:nh * w].rearrange("p (a w) -> p a w", a=nh),
                                AX.X, ALU.max).then_inc(s.unit_taken, 1)

            def first_units(ks):
                for k in ks:
                    take_unit(SELF, ss, 0, k, 6)

            v.wait_ge(gate_out, 4)
            for n in range(NCH):
                if n == CPB:
                    split_context()
                if n == NCH - 1:
                    v.wait_ge(set_up, 5)
                split(4 * n, [gated(0, n % CPB), gated(1, n % CPB), copied(2), copied(3)],
                      lambda k: first_units(EARLY_UNITS[k]) if n == NCH - 1 else None)
            for k in range(4, 6):
                first_units(EARLY_UNITS[k])
            first_units(range(EARLY_UNITS[-1].stop, SELF.nu))

            def moments(g, n):
                for u in range(TPC):
                    v.wait_ge(g.added, TPC * n + u + 1)
                    v.bn_stats(stats[:, u, :], rows[:, TPC * n + u, :]).then_inc(g.stat_step, 1)
                for u in range(TPC):
                    v.wait_ge(g.stat_step, 2 * TPC * n + u + 1)
                    v.bn_aggr(mean_var[:, n % 2, u, :], stats[:, u, :]).then_inc(g.stat_step, 1)
                v.wait_ge(g.stat_step, 2 * TPC * (n + 1))
                v.sem_inc(g.var_ready, 1)

            def add_tile(g, t, bank):
                v.wait_ge(g.out_ready, t + 1)
                v.tensor_tensor(rows[:, t, :], PS[:, bank, 0:D], rows[:, t, :], ALU.add).then_inc(g.added, 1)

            def add_block(g, n):
                for t in range(TPC * n, TPC * (n + 1)):
                    add_tile(g, t, t % TPC)
                moments(g, n)

            def attention(A, s):
                ring_units = A.nu + 1

                def fold_tops(n):
                    v.wait_ge(s.unit_taken, ring_units * n + A.nu)
                    v.wait_ge(s.unit_ready, ring_units * n)
                    v.tensor_reduce(ntop[:, 0:GH * QT], tops[:].rearrange("p h i c -> p (h i) c"), AX.X, ALU.max,
                                    negate=True).then_inc(s.tops_ready, 1)

                def split_tops(n):
                    v.wait_ge(s.unit_ready, ring_units * (n + 1))
                    v.wait_ge(s.top_rows_in, 48 * n)
                    src = PS[0:GH * QT, A.nu % 2, 0:P]
                    v.tensor_copy(ntop_p[0:GH * QT, 0, :], src).then_inc(s.top_split, 1)
                    v.wait_ge(s.top_split, 3 * n + 1)
                    v.tensor_tensor(ntop_r[0:GH * QT], src, ntop_p[0:GH * QT, 0, :], ALU.subtract).then_inc(s.unit_taken, 1)
                    v.wait_ge(s.unit_taken, ring_units * (n + 1))
                    v.tensor_copy(ntop_p[0:GH * QT, 1, :], ntop_r[0:GH * QT]).then_inc(s.top_split, 1)
                    v.wait_ge(s.top_split, 3 * n + 2)
                    v.tensor_tensor(ntop_p[0:GH * QT, 2, :], ntop_r[0:GH * QT], ntop_p[0:GH * QT, 1, :], ALU.subtract).then_inc(s.top_split, 1)

                def take_output(n, c):
                    v.wait_ge(s.values_done, A.slots + A.ns * n + A.last[c] + 1)
                    v.wait_ge(s.o_ready, CPB * n + (c + 1))
                    v.transpose(o_blk[:, c, :], PS[:, 6 + c, :]).then_inc(s.o_taken, 1)
                    v.wait_ge(s.o_taken, CPB * (n + 1) + c + 1)
                    v.reciprocal(o_rec[:, c, :], o_blk[:, c, HD:CH:32]).then_inc(s.rec_ready, 1)

                def give_output(n, c):
                    v.wait_ge(s.o_scaled, CPB * n + c + 1)
                    v.wait_ge(s.o_stored[c], 16 * (n + 1))
                    v.transpose(o_nrm[:, c, :], o_blk[:, c, :]).then_inc(s.o_ready, 1)

                def step(n, st, ahead):
                    first = isinstance(n, int) and n == 0
                    if ahead:
                        for quarter in range(4):
                            for k in A.units_of(st, quarter, first):
                                take_unit(A, s, n + ahead, k)
                        if st == A.unit_steps - 1:
                            fold_tops(n + 1)
                    for back, c in A.output_at(st, A.take_lag):
                        if not (first and back):
                            take_output(n - back, c)
                    for back, c in A.output_at(st, A.take_lag + 1):
                        if not (first and back):
                            give_output(n - back, c)
                    if st == A.top_step and ahead:
                        split_tops(n + 1)
                    if A.causal and isinstance(n, int) and n == NN - 1 and st < AHEAD * TPC:
                        if st == 0:
                            v.wait_ge(rows_in, 16)
                        add_tile(n1, st, st % 2)
                        if st % TPC == TPC - 1:
                            moments(n1, st // TPC)

                def pair_turn(n):
                    first, last = (isinstance(n, int) and n == e for e in (0, NN - 1))
                    if not first:
                        for st in range(A.next_step, A.ns):
                            step(n - 1, st, 0 if last else 2)
                    for st in range(A.next_step):
                        step(n, st, 0 if last else 1)

                v.sem_inc(s.o_taken, CPB)
                v.sem_inc(s.o_ready, CPB)
                if A.causal:
                    fold_tops(0)
                    split_tops(0)
                pair_turn(0)
                with v.Fori(0, LOOPS) as i:
                    for q in range(RING):
                        pair_turn(RING * i + (q + 1))
                pair_turn(NN - 1)
                for st in range(A.next_step, A.ns):
                    step(NN - 1, st, 0)
                if not A.causal:
                    give_output(NN - 1, 0)
                take_output(NN - 1, 1)
                give_output(NN - 1, 1)

            def normalise(g, n):
                v.wait_ge(g.std_ready, n + 1)
                v.reciprocal(rstd[:, n % 2], std[:, n % 2]).then_inc(g.rstd_ready, 1)
                v.wait_ge(g.rstd_ready, n + 1)
                for u in range(TPC):
                    t = TPC * n + u
                    v.tensor_scalar(rows[:, t, :], rows[:, t, :], mean_var[:, n % 2, u, 0:1], rstd[:, n % 2, u:u + 1],
                                    ALU.subtract, ALU.mult).then_inc(g.normed, 1)

            attention(SELF, ss)

            for n in range(AHEAD):
                normalise(n1, n)
            for n in range(NCH):
                if n == AHEAD:
                    for late in range(AHEAD, NCH):
                        add_block(n1, late)
                        normalise(n1, late)
                split(N_ITEMS + KD * n, [biased(m) for m in range(KD)])

            v.sem_inc(cs.unit_taken, 2)
            v.wait_ge(zeroed, 16 * NN)
            for b in range(B):
                for g in range(NG):
                    for u in range(QT // XB):
                        v.wait_ge(cs.unit_ready, QT // XB * g + (QT // XB * NG * b + u + 1))
                        v.sem_inc(vector_turn, 1)
                        at = XB * (u % 2)
                        cols = ntop[:, bass.ds(g * (GH * QT), GH * QT)].rearrange("p (h i) -> p i h", h=GH)
                        v.tensor_reduce(cols[:, XB * u:XB * (u + 1), :],
                                        PS[:, at:at + XB, 0:GH * SKV].rearrange("p u (h w) -> p u h w", h=GH),
                                        AX.X, ALU.max, negate=True).then_inc(cs.unit_taken, 1)
                v.wait_ge(cs.unit_taken, 2 + QT // XB * NG * (b + 1))
                v.sem_inc(cs.tops_ready, 1)
                v.wait_ge(xtops_turned, b + 1)
                v.wait_ge(cs.top_rows_in, 48 * b)
                src = PS[:, 6 + b, 0:P]
                v.tensor_copy(ntop_p[:, 0, :], src).then_inc(cs.top_split, 1)
                v.wait_ge(cs.top_split, 3 * b + 1)
                v.tensor_tensor(ntop_r, src, ntop_p[:, 0, :], ALU.subtract).then_inc(xtop_rest, 1)
                v.wait_ge(xtop_rest, b + 1)
                v.tensor_copy(ntop_p[:, 1, :], ntop_r).then_inc(cs.top_split, 1)
                v.wait_ge(cs.top_split, 3 * b + 2)
                v.tensor_tensor(ntop_p[:, 2, :], ntop_r, ntop_p[:, 1, :], ALU.subtract).then_inc(cs.top_split, 1)
            attention(CROSS, cs)

            for n in range(NCH):
                v.wait_ge(bias_added, n + 1)
                add_block(n2, n)
                normalise(n2, n)

            steps = 0

            def routed():
                v.wait_ge(route_step, steps)

            def by_token(a):
                return a.rearrange("p e t -> p t e")

            v.memset(experts[:, 3, :], 1.0).then_inc(route_step, 1)
            v.memset(scan_keep, 1.0).then_inc(route_step, 1)
            v.wait_ge(route_step, 2)
            v.memset(scan_keep[:, :, 0:1], 0.0).then_inc(route_step, 1)
            v.wait_ge(iota_ready, 2)
            v.tensor_scalar(rev_e, iota_e[:], -1.0, float(NE), ALU.mult, ALU.add).then_inc(route_step, 1)
            v.wait_ge(scores_done, 1)
            v.tensor_tensor(select, scores, ebias_b[:, None, :].to_broadcast([P, NT, NE]), ALU.add).then_inc(route_step, 1)
            steps += 5
            for k in range(TOPK):
                routed()
                v.tensor_reduce(best[:, k, 0, :], select, AX.X, ALU.max).then_inc(route_step, 1)
                steps += 1
                routed()
                v.tensor_tensor(by_token(work), select, best[:, k, 0, :, None].to_broadcast([P, NT, NE]),
                                ALU.is_equal).then_inc(route_step, 1)
                steps += 1
                routed()
                v.tensor_tensor(by_token(work), by_token(work), rev_e[:, None, :].to_broadcast([P, NT, NE]),
                                ALU.mult).then_inc(route_step, 1)
                steps += 1
                routed()
                v.tensor_reduce(best[:, k, 1, :], by_token(work), AX.X, ALU.max).then_inc(route_step, 1)
                steps += 1
                routed()
                v.tensor_tensor(by_token(onehot[:, k]), rev_e[:, None, :].to_broadcast([P, NT, NE]),
                                best[:, k, 1, :, None].to_broadcast([P, NT, NE]), ALU.is_equal).then_inc(route_step, 1)
                steps += 1
                if k == 0:
                    routed()
                    v.scalar_tensor_tensor(select, by_token(onehot[:, k]), LOWEST, select, ALU.mult, ALU.add).then_inc(route_step, 1)
                    steps += 1
            routed()
            v.tensor_tensor(picked, onehot[:, 0], onehot[:, 1], ALU.add).then_inc(counted, 1)

            v.wait_ge(counts_ready, 1)
            before_n = PS[:, 7, 0:NE * NT].rearrange("p (e t) -> p e t", e=NE)
            in_tile = PS[:, 7, NE * NT:2 * NE * NT].rearrange("p (e t) -> p e t", e=NE)
            v.tensor_tensor_scan(work.rearrange("p e t -> p (e t)"), scan_keep.rearrange("p e t -> p (e t)"),
                                 PS[:, 7, NE * NT:2 * NE * NT], 0.0, ALU.mult, ALU.add).then_inc(route_step, 1)
            steps += 1
            routed()
            v.tensor_scalar(tiles_i[:], work[:, :, NT - 1], float(P - 1), None, ALU.add).then_inc(route_step, 1)
            steps += 1
            routed()
            v.tensor_single_scalar(tiles_i[:], tiles_i[:], P.bit_length() - 1, ALU.arith_shift_right).then_inc(route_step, 1)
            steps += 1
            routed()
            v.tensor_copy(experts[:, 0, :], tiles_i[:]).then_inc(route_step, 1)
            steps += 1
            routed()
            v.tensor_tensor_scan(experts[:, 1, :], experts[:, 3, :], experts[:, 0, :], 0.0, ALU.mult, ALU.add).then_inc(route_step, 1)
            steps += 1
            routed()
            v.tensor_tensor(experts[:, 2, :], experts[:, 1, :], experts[:, 0, :], ALU.subtract).then_inc(route_step, 1)
            v.tensor_tensor(work, work, in_tile, ALU.subtract).then_inc(route_step, 1)
            steps += 2
            routed()
            v.tensor_tensor(work, work, before_n, ALU.add).then_inc(route_step, 1)
            steps += 1
            routed()
            v.sem_inc(counts_taken, 1)
            v.scalar_tensor_tensor(work, experts[:, 2, :, None].to_broadcast([P, NE, NT]), float(P), work,
                                   ALU.mult, ALU.add).then_inc(route_step, 1)
            steps += 1
            for k in range(TOPK):
                routed()
                v.tensor_tensor(picked, onehot[:, k], work, ALU.mult).then_inc(route_step, 1)
                steps += 1
                routed()
                v.tensor_reduce(slots_f[:, k, :], by_token(picked), AX.X, ALU.add).then_inc(route_step, 1)
                steps += 1
            routed()
            v.tensor_copy(slots_u[:], slots_f).then_inc(slots_ready, 1)

            def shared_chunk(n, between=lambda h: None):
                hs = FH // P
                for h in range(hs):
                    v.wait_ge(hid_ready, 2 * hs * n + 2 * h + 2)
                    v.wait_ge(sil_done, hs * n + h + 1)
                    v.wait_ge(down_done, hs * n + max(0, h - 3))
                    v.tensor_tensor(hidT[:, h % 4, :], sil[:, h % 2, :], PS[:, 2 * (h % 2) + 1, :], ALU.mult).then_inc(hid_done, 1)
                    between(h)
                v.wait_ge(down_done, hs * (n + 1))
                if isinstance(n, int) and n == NCH - 1:
                    return
                v.sem_inc(vector_turn, 1)
                for u in range(TPC):
                    dst = shared[:, bass.ds(TPC * n + u, 1), :].rearrange("p o d -> p (o d)")
                    v.tensor_copy(dst, PS[:, 4 + u, 0:D]).then_inc(acc_taken, 1)

            def late_routing(h):
                nonlocal steps
                if h == 2:
                    ended = xs_out[0:1].rearrange("p r n -> p (r n)")[:, 0:48 * NE].rearrange("p (j e) -> p j e", e=NE)
                    v.tensor_tensor(ended, iota_t[:, :, None].to_broadcast([1, 48, NE]),
                                    experts[0:1, 1, None, :].to_broadcast([1, 48, NE]), ALU.is_ge).then_inc(route_step, 1)
                    steps += 1
                    routed()
                    v.tensor_reduce(tile_work, ended, AX.X, ALU.add).then_inc(route_step, 1)
                    steps += 1
                    routed()
                    v.tensor_scalar(expert_of[:], tile_work, float(NE - 1), None, ALU.min).then_inc(expert_ready, 1)
                if h == 4:
                    for k in range(TOPK):
                        routed()
                        v.tensor_tensor(by_token(work), by_token(onehot[:, k]), scores, ALU.mult).then_inc(route_step, 1)
                        steps += 1
                        routed()
                        v.tensor_reduce(gates[:, k, :], by_token(work), AX.X, ALU.add).then_inc(route_step, 1)
                        steps += 1

            for n in range(NCH // 2):
                shared_chunk(n, late_routing if n == 0 else lambda h: None)
            routed()

            def multiply(i, p):
                j = 2 * i + p
                v.wait_ge(slot_sil, j + 1)
                if not (isinstance(j, int) and j < 2):
                    v.wait_ge(slot_hturned, j - 1)
                v.tensor_tensor(xs_h[:, p, :], xs_sil[:, p, :], PS[:, 2 + p, RH:2 * RH], ALU.mult).then_inc(slot_h, 1)

            def take_hidden(i, p):
                v.wait_ge(slot_hturned, 2 * i + p + 1)
                v.tensor_copy(xs_hT[:, p, :], PS[:, 4 + p, 0:KD * P]).then_inc(slot_hT, 1)

            def take_slot(i, p):
                v.wait_ge(slot_out, 2 * i + p + 1)
                v.wait_ge(slot_stored[p], 16 * i)
                v.tensor_copy(xs_y[:, p, :], PS[:, 6 + p, 0:D]).then_inc(slot_y, 1)

            multiply(0, 0)
            multiply(0, 1)
            take_hidden(0, 0)

            def step(i, p):
                multiply(i, p)
                take_slot(i - 1, p)
                take_hidden(i - 1 + p, 1 - p)

            step(1, 0)
            step(1, 1)
            with v.Fori(2, (TILES - 1) // 2) as i:
                for p in range(2):
                    step(i, p)
            i = (TILES - 1) // 2
            multiply(i, 0)
            take_slot(i - 1, 0)
            take_hidden(i - 1, 1)
            take_slot(i - 1, 1)
            take_hidden(i, 0)
            take_slot(i, 0)

            def add_experts(n, k, done):
                v.wait_ge(gathered_in[n], 16 * TOPK * TPC)
                for t in range(TPC * n, TPC * (n + 1)):
                    v.scalar_tensor_tensor(rows[:, t, :], gathered[:, t, k, :], gates[:, k, t:t + 1], rows[:, t, :],
                                           ALU.mult, ALU.add).then_inc(done, 1)

            def finish(n, part):
                if part == 0:
                    v.wait_ge(acc_taken, TPC * (n + 1))
                    chunk = rows[:, TPC * n:TPC * (n + 1), :]
                    v.tensor_tensor(chunk, chunk, shared[:, TPC * n:TPC * (n + 1), :], ALU.add).then_inc(final_step, 1)
                if part < TOPK:
                    v.wait_ge(final_step, (TPC + 1) * n + 1 + TPC * part)
                    add_experts(n, part, n3.added if part else final_step)
                elif part == TOPK:
                    moments(n3, n)
                else:
                    normalise(n3, n)

            def between(n, h):
                if (n, h) in FINISH:
                    finish(*FINISH[n, h])
                k = h - (FH // P - TOPK)
                if n == NCH - 1 and k >= 0:
                    v.wait_ge(final_step, (TPC + 1) * n + TPC * k)
                    add_experts(n, k, final_step)

            for n in range(NCH // 2, NCH):
                shared_chunk(n, lambda h: between(n, h))
            n = NCH - 1
            v.wait_ge(final_step, (TPC + 1) * n + TPC * TOPK)
            for u in range(TPC):
                row = rows[:, TPC * n + u, :]
                v.tensor_tensor(row, PS[:, 4 + u, 0:D], row, ALU.add).then_inc(n3.added, 1)
            moments(n3, n)
            normalise(n3, n)


_HEADS = D // HD


def _columns():
    return np.array([GH * HD * g + HD * h + d for g in range(NG) for d in range(HD) for h in range(GH)])


def _gate_rows(values):
    raw = np.zeros((P, D), values.dtype)
    pick = np.zeros((P, D), np.float32)
    row = 0
    for c, cycle in enumerate(TALA_CYCLES):
        for r in range(cycle):
            for h in range(c, _HEADS, len(TALA_CYCLES)):
                raw[row, HD * h:HD * (h + 1)] = values[h, r]
                pick[row, HD * h:HD * (h + 1)] = 1
            row += 1
    cols = _columns()
    return raw[:, cols], pick[:, cols]


def _phase_rows():
    rows = np.zeros((P, S), np.float32)
    row = 0
    for cycle in TALA_CYCLES:
        for r in range(cycle):
            rows[row, r::cycle] = 1
            row += 1
    return rows


def _operands(inputs):
    g = {k: np.asarray(v) for k, v in inputs.items()}
    cols = _columns()
    w_qkv = g["L0_attn_w_qkv"]
    raw, pick = _gate_rows(g["L0_attn_bandha_gate"])
    key, query = np.arange(P)[None, :], np.arange(P)[:, None]
    causal = np.where(key <= query, 0, bf16_bits(LATER_KEY)).astype(np.uint16)
    ops = {
        "x": g["x"], "xT": g["x"].reshape(TOK, D).T, "ctxT": g["ctx_1024"].reshape(B * SKV, D).T,
        "mask": g["mask_BxS2_bf1"].view(np.uint8),
        "w_qkv": np.concatenate([w_qkv[:, 0:D][:, cols], w_qkv[:, D:2 * D][:, cols], w_qkv[:, 2 * D:]], axis=1),
        "gate_raw": raw, "gate_pick": pick, "phase": _phase_rows(), "w_out": g["L0_attn_w_out"],
        "w_q": g["L0_xattn_Wq"].T[:, cols], "b_q": g["L0_xattn_bq"][cols].reshape(KD, P).T,
        "w_k": g["L0_xattn_Wk"].T[:, cols], "b_k": g["L0_xattn_bk"][cols].reshape(KD, P).T,
        "w_v": g["L0_xattn_Wv"].T, "b_v": g["L0_xattn_bv"], "w_o": g["L0_xattn_Wo"].T, "b_o": g["L0_xattn_bo"],
        "router_w": g["L0_ffn_router_w"], "expert_bias": g["L0_ffn_expert_bias"],
        "sw1": g["L0_ffn_shared_w1"][0], "sw2": g["L0_ffn_shared_w2"][0], "sw3": g["L0_ffn_shared_w3"][0],
        "rw1": g["L0_ffn_routed_w1"], "rw2": g["L0_ffn_routed_w2"], "rw3": g["L0_ffn_routed_w3"],
        "ident_f": np.eye(P, dtype=np.float32), "ident_b": np.eye(P, dtype=np.uint16) * np.uint16(bf16_bits(1.0)),
        "causal": np.broadcast_to(causal[:, None, :], (P, GH, P)),
        "before": (np.arange(P)[:, None] < np.arange(P)[None, :]).astype(np.float32),
        "ones": np.full(GH * S, bf16_bits(1.0), np.uint16),
    }
    return {k: np.ascontiguousarray(v) for k, v in ops.items()}


def kernel(**inputs):
    import concourse.bacc as bacc
    from concourse import mybir as mb
    from concourse.bass_utils import run_bass_kernel_spmd

    nc = bacc.Bacc("TRN2", target_bir_lowering=False, num_devices=1)
    arrays, args = {}, []
    for name, a in _operands(inputs).items():
        arrays[f"in_{name}_dram"] = a
        args.append(nc.dram_tensor(f"in_{name}_dram", a.shape, mb.dt.from_np(a.dtype), kind="ExternalInput").ap())
    args.append(nc.dram_tensor("out_dram", (B, S, D), mb.dt.float32, kind="ExternalOutput").ap())
    decoder_layer(nc, *args)
    result = run_bass_kernel_spmd(nc, [arrays], core_ids=[0])
    return result.results[0]["out_dram"]
```
